# Optimizing a Trainium2 kernel written in Bass

```python
import numpy as np
import jax
import jax.numpy as jnp

def _softmax(x, axis=-1):
    return jax.nn.softmax(x, axis=axis)

def _gelu(x):
    return jax.nn.gelu(x, approximate=True)

def _silu(x):
    return jax.nn.silu(x)

def _sigmoid(x):
    return jax.nn.sigmoid(x)

def _layernorm(x, axis=-1, eps=1e-05):
    m = jnp.mean(x, axis=axis, keepdims=True)
    v = jnp.var(x, axis=axis, keepdims=True)
    return (x - m) / jnp.sqrt(v + eps)

def _scatter_add(tgt, idx, src, axis=0):
    return tgt.at[idx].add(src)

def _segment_sum(src, seg, n):
    return jax.ops.segment_sum(src, seg, n)
kernel_name = 'mk_decoder_postln_d1_seqx_r4_24ba00'

def setup_inputs(seed: int=0):
    np.random.seed(seed)
    _w = jnp.asarray

    def _rec_inputs():
        import jax
        import jax.numpy as jnp
        _rk = jax.random.key(seed)
        x = -0.0002928 + 1 * jax.random.normal(jax.random.fold_in(_rk, 1), (8, 256, 256), jnp.float32)
        _lenS = 256 - jax.random.randint(jax.random.fold_in(_rk, 7), (8,), 0, max(1, 256 // 4) + 1, jnp.int32)
        _lenS2 = 256 - jax.random.randint(jax.random.fold_in(_rk, 8), (8,), 0, max(1, 256 // 4) + 1, jnp.int32)
        _ctx_1024P = jax.random.normal(jax.random.fold_in(_rk, 11), (8, 16, 256), jnp.float32)
        _ctx_1024c = jax.random.dirichlet(jax.random.fold_in(_rk, 511), 0.3 * jnp.ones((16,), jnp.float32), (8, 256))
        _ctx_1024t = jnp.einsum('bsk,bkd->bsd', _ctx_1024c, _ctx_1024P)
        _ctx_1024t = _ctx_1024t * jax.lax.rsqrt(jnp.mean(jnp.square(_ctx_1024t)) + 1e-12) * 0.953939
        ctx_1024 = -1.39393e-06 + 0.999914 * (_ctx_1024t + 0.3 * jax.random.normal(jax.random.fold_in(_rk, 611), (8, 256, 256), jnp.float32))
        return (x, ctx_1024)
    x, ctx_1024 = _rec_inputs()

    def _L0_attn_setup():
        import jax, jax.numpy as jnp
        import numpy as np
        N_EMBD = 256
        N_HEAD = 16
        HEAD_DIM = N_EMBD // N_HEAD
        KV_RANK = 64
        Q_RANK = 128
        ROPE_DIM = 32
        B, T = (2, 512)
        EPS = 1e-06

        def _rope_tables(T, dim):
            inv_freq = 1.0 / 10000.0 ** (np.arange(0, dim, 2, dtype=np.float32) / dim)
            t = np.arange(T, dtype=np.float32)
            freqs = np.outer(t, inv_freq)
            emb = np.concatenate([freqs, freqs], -1)
            return (jnp.asarray(np.cos(emb)), jnp.asarray(np.sin(emb)))

        def _apply_rope(x, cos, sin):
            d2 = x.shape[-1] // 2
            x1, x2 = (x[..., :d2], x[..., d2:])
            rot = jnp.concatenate([-x2, x1], axis=-1)
            return x * cos[None, None, :, :] + rot * sin[None, None, :, :]
        key = jax.random.key(seed)
        ks = jax.random.split(key, 10)

        def w(k, fan_in, fan_out):
            return jax.random.normal(k, (fan_in, fan_out), dtype=jnp.float32) * fan_in ** (-0.5)
        return {'x': jax.random.normal(ks[0], (B, T, N_EMBD), dtype=jnp.float32), 'W_kv': w(ks[1], N_EMBD, KV_RANK), 'g_kv': jnp.ones((KV_RANK,), dtype=jnp.float32), 'W_kdec': w(ks[2], KV_RANK, N_HEAD * HEAD_DIM), 'W_vdec': w(ks[3], KV_RANK, N_HEAD * HEAD_DIM), 'W_q': w(ks[4], N_EMBD, Q_RANK), 'W_qdec': w(ks[5], Q_RANK, N_HEAD * HEAD_DIM), 'W_krope': w(ks[6], N_EMBD, N_HEAD * ROPE_DIM), 'W_qrope': w(ks[7], Q_RANK, N_HEAD * ROPE_DIM), 'W_o': w(ks[8], N_HEAD * HEAD_DIM, N_EMBD)}
    _L0_attn_all = _L0_attn_setup()
    _L0_attn_in = {k: v for k, v in _L0_attn_all.items() if k in ('W_kv', 'g_kv', 'W_kdec', 'W_vdec', 'W_q', 'W_qdec', 'W_krope', 'W_qrope', 'W_o')}
    del _L0_attn_all

    def _L0_xattn_setup():
        import jax, jax.numpy as jnp
        import numpy as np
        D_MODEL = 256
        NUM_HEADS = 16
        D_K = D_MODEL // NUM_HEADS
        SCALE = D_K ** (-0.5)
        key = jax.random.key(seed)
        kq, kk, kv, kw, kb = jax.random.split(key, 5)
        B, S = (2, 512)
        q = jax.random.normal(kq, (B, S, D_MODEL), dtype=jnp.float32)
        k = jax.random.normal(kk, (B, S, D_MODEL), dtype=jnp.float32)
        v = jax.random.normal(kv, (B, S, D_MODEL), dtype=jnp.float32)
        W = jax.random.normal(kw, (D_MODEL, D_MODEL), dtype=jnp.float32) * D_MODEL ** (-0.5)
        b = jax.random.normal(kb, (D_MODEL,), dtype=jnp.float32) * 0.01
        return {'q': q, 'k': k, 'v': v, 'W': W, 'b': b}
    _L0_xattn_all = _L0_xattn_setup()
    _L0_xattn_in = {k: v for k, v in _L0_xattn_all.items() if k in ('W', 'b')}
    del _L0_xattn_all

    def _L0_ffn_setup():
        import jax, jax.numpy as jnp
        import numpy as np
        D_MODEL = 256
        D_FF = 1024
        NUM_EXPERTS = 8
        TOP_K = 2
        key = jax.random.key(seed)
        ks = jax.random.split(key, 8)
        s_in = 1.0 / np.sqrt(D_MODEL)
        s_ff = 1.0 / np.sqrt(D_FF)
        x = jax.random.normal(ks[0], (2, 512, D_MODEL), dtype=jnp.float32)
        Wg = jax.random.uniform(ks[1], (D_MODEL, NUM_EXPERTS), minval=-s_in, maxval=s_in, dtype=jnp.float32)
        bg = jax.random.uniform(ks[2], (NUM_EXPERTS,), minval=-s_in, maxval=s_in, dtype=jnp.float32)
        W1 = jax.random.uniform(ks[3], (NUM_EXPERTS, D_MODEL, D_FF), minval=-s_in, maxval=s_in, dtype=jnp.float32)
        b1 = jax.random.uniform(ks[4], (NUM_EXPERTS, D_FF), minval=-s_in, maxval=s_in, dtype=jnp.float32)
        W2 = jax.random.uniform(ks[5], (NUM_EXPERTS, D_FF, D_MODEL), minval=-s_ff, maxval=s_ff, dtype=jnp.float32)
        b2 = jax.random.uniform(ks[6], (NUM_EXPERTS, D_MODEL), minval=-s_ff, maxval=s_ff, dtype=jnp.float32)
        return {'x': x, 'Wg': Wg, 'bg': bg, 'W1': W1, 'b1': b1, 'W2': W2, 'b2': b2}
    _L0_ffn_all = _L0_ffn_setup()
    _L0_ffn_in = {k: v for k, v in _L0_ffn_all.items() if k in ('Wg', 'bg', 'W1', 'b1', 'W2', 'b2')}
    del _L0_ffn_all
    return {'x': x, 'ctx_1024': ctx_1024, 'L0_attn_W_kv': _L0_attn_in['W_kv'], 'L0_attn_g_kv': _L0_attn_in['g_kv'], 'L0_attn_W_kdec': _L0_attn_in['W_kdec'], 'L0_attn_W_vdec': _L0_attn_in['W_vdec'], 'L0_attn_W_q': _L0_attn_in['W_q'], 'L0_attn_W_qdec': _L0_attn_in['W_qdec'], 'L0_attn_W_krope': _L0_attn_in['W_krope'], 'L0_attn_W_qrope': _L0_attn_in['W_qrope'], 'L0_attn_W_o': _L0_attn_in['W_o'], 'L0_xattn_W': _L0_xattn_in['W'], 'L0_xattn_b': _L0_xattn_in['b'], 'L0_ffn_Wg': _L0_ffn_in['Wg'], 'L0_ffn_bg': _L0_ffn_in['bg'], 'L0_ffn_W1': _L0_ffn_in['W1'], 'L0_ffn_b1': _L0_ffn_in['b1'], 'L0_ffn_W2': _L0_ffn_in['W2'], 'L0_ffn_b2': _L0_ffn_in['b2']}

def reference(x, ctx_1024, L0_attn_W_kv, L0_attn_g_kv, L0_attn_W_kdec, L0_attn_W_vdec, L0_attn_W_q, L0_attn_W_qdec, L0_attn_W_krope, L0_attn_W_qrope, L0_attn_W_o, L0_xattn_W, L0_xattn_b, L0_ffn_Wg, L0_ffn_bg, L0_ffn_W1, L0_ffn_b1, L0_ffn_W2, L0_ffn_b2):
    import jax
    import jax.numpy as jnp

    def _L0_attn_ref(x, W_kv, g_kv, W_kdec, W_vdec, W_q, W_qdec, W_krope, W_qrope, W_o):
        import jax, jax.numpy as jnp
        import numpy as np
        N_EMBD = 256
        N_HEAD = 16
        HEAD_DIM = N_EMBD // N_HEAD
        KV_RANK = 64
        Q_RANK = 128
        ROPE_DIM = 32
        B, T = (2, 512)
        EPS = 1e-06

        def _rope_tables(T, dim):
            inv_freq = 1.0 / 10000.0 ** (np.arange(0, dim, 2, dtype=np.float32) / dim)
            t = np.arange(T, dtype=np.float32)
            freqs = np.outer(t, inv_freq)
            emb = np.concatenate([freqs, freqs], -1)
            return (jnp.asarray(np.cos(emb)), jnp.asarray(np.sin(emb)))

        def _apply_rope(x, cos, sin):
            d2 = x.shape[-1] // 2
            x1, x2 = (x[..., :d2], x[..., d2:])
            rot = jnp.concatenate([-x2, x1], axis=-1)
            return x * cos[None, None, :, :] + rot * sin[None, None, :, :]
        Bx, Tx, C = x.shape
        kv_c = x @ W_kv
        kv_c = kv_c * jax.lax.rsqrt(jnp.mean(kv_c * kv_c, axis=-1, keepdims=True) + EPS) * g_kv
        q_c = x @ W_q

        def heads(y, d):
            return y.reshape(Bx, Tx, N_HEAD, d).transpose(0, 2, 1, 3)
        k_content = heads(kv_c @ W_kdec, HEAD_DIM)
        v = heads(kv_c @ W_vdec, HEAD_DIM)
        q_content = heads(q_c @ W_qdec, HEAD_DIM)
        k_rope = heads(x @ W_krope, ROPE_DIM)
        q_rope = heads(q_c @ W_qrope, ROPE_DIM)
        cos, sin = _rope_tables(Tx, ROPE_DIM)
        q_rope = _apply_rope(q_rope, cos, sin)
        k_rope = _apply_rope(k_rope, cos, sin)
        q = jnp.concatenate([q_content, q_rope], axis=-1)
        k = jnp.concatenate([k_content, k_rope], axis=-1)
        scale = 1.0 / jnp.sqrt(jnp.float32(q.shape[-1]))
        scores = jnp.einsum('bhqd,bhkd->bhqk', q, k) * scale
        causal = jnp.tril(jnp.ones((Tx, Tx), dtype=bool))
        scores = jnp.where(causal[None, None], scores, jnp.float32(-jnp.inf))
        attn = jax.nn.softmax(scores, axis=-1)
        out = jnp.einsum('bhqk,bhkd->bhqd', attn, v)
        out = out.transpose(0, 2, 1, 3).reshape(Bx, Tx, N_HEAD * HEAD_DIM)
        return out @ W_o

    def _L0_xattn_ref(q, k, v, W, b):
        import jax, jax.numpy as jnp
        import numpy as np
        D_MODEL = 256
        NUM_HEADS = 16
        D_K = D_MODEL // NUM_HEADS
        SCALE = D_K ** (-0.5)
        B, S, _ = q.shape

        def split(x):
            return x.reshape(B, S, NUM_HEADS, D_K).transpose(0, 2, 1, 3)
        qh, kh, vh = (split(q), split(k), split(v))
        scores = jnp.einsum('bhid,bhjd->bhij', qh, kh) * SCALE
        weights = jax.nn.softmax(scores, axis=-1)
        attn = jnp.einsum('bhij,bhjd->bhid', weights, vh)
        out = attn.transpose(0, 2, 1, 3).reshape(B, S, D_MODEL)
        return out @ W.T + b

    def _L0_ffn_ref(x, Wg, bg, W1, b1, W2, b2):
        import jax, jax.numpy as jnp
        import numpy as np
        D_MODEL = 256
        D_FF = 1024
        NUM_EXPERTS = 8
        TOP_K = 2
        gate_logits = jnp.einsum('bsd,de->bse', x, Wg) + bg
        gate_probs = jax.nn.softmax(gate_logits, axis=-1)
        topk_probs, topk_idx = jax.lax.top_k(gate_probs, TOP_K)
        topk_probs = topk_probs / jnp.sum(topk_probs, axis=-1, keepdims=True)
        onehot = jax.nn.one_hot(topk_idx, NUM_EXPERTS, dtype=x.dtype)
        weights = jnp.einsum('bske,bsk->bse', onehot, topk_probs)
        h = jnp.einsum('bsd,edf->bsef', x, W1) + b1
        h = jax.nn.gelu(h, approximate=False)
        y = jnp.einsum('bsef,efd->bsed', h, W2) + b2
        return jnp.einsum('bsed,bse->bsd', y, weights)
    x = _layernorm(x + _L0_attn_ref(x, L0_attn_W_kv, L0_attn_g_kv, L0_attn_W_kdec, L0_attn_W_vdec, L0_attn_W_q, L0_attn_W_qdec, L0_attn_W_krope, L0_attn_W_qrope, L0_attn_W_o), axis=-1)
    x = _layernorm(x + _L0_xattn_ref(x, ctx_1024, ctx_1024, L0_xattn_W, L0_xattn_b), axis=-1)
    x = _layernorm(x + _L0_ffn_ref(x, L0_ffn_Wg, L0_ffn_bg, L0_ffn_W1, L0_ffn_b1, L0_ffn_W2, L0_ffn_b2), axis=-1)
    return x

_drawn_inputs = setup_inputs


def setup_inputs(seed=0):
    import zlib

    import numpy as np

    out = dict(_drawn_inputs(seed))
    spreads = {'L0_attn_g_kv': (1.0, 0.2)}
    factors = {'L0_xattn_b': 4.66, 'L0_ffn_b1': 6.152, 'L0_ffn_b2': 4.353}
    for name, (base, spread) in spreads.items():
        noise = np.random.default_rng([zlib.crc32(name.encode()), seed]).standard_normal(out[name].shape)
        drawn = base * np.exp(spread * noise) if base else spread * noise
        out[name] = jnp.asarray(drawn.astype(out[name].dtype))
    for name, factor in factors.items():
        out[name] = (out[name] * factor).astype(out[name].dtype)
    return out
```

```python
import concourse.bass as bass
from concourse import mybir
from contextlib import ExitStack

F32 = mybir.dt.float32
F16 = mybir.dt.float16
BF16 = mybir.dt.bfloat16
I32 = mybir.dt.int32
ACT = mybir.ActivationFunctionType
ALU = mybir.AluOpType
AX = mybir.AxisListType

P = 128
B, T, D = 8, 256, 256
TT = T // P
DC = D // P
H = 16
HD = D // H
RD = 32
QK = 64
KVR, QR = 64, 128
E, F = 8, 1024
EW = 2 * D * F // P
PIECE = F
PIECES = EW // PIECE
EARLY = 6
PER_ROW = EARLY * PIECES // 8
FC = F // P
NT = B * TT
TOK = B * T
N_TILES = (2 * TOK + E * (P - 1)) // P
ROWS = TOK + P
W_SCALE = 64.0
RMS_EPS, LN_EPS = 1e-6, 1e-5
SELF_SCALE = float(HD + RD) ** -0.5
CROSS_SCALE = float(HD) ** -0.5

C_COS = 0
C_SIN = C_COS + T
C_ID = C_SIN + T
C_MASK = C_ID + P
C_MASKT = C_MASK + P
C_UP = C_MASKT + P
C_REV = C_UP + P
C_CNT = C_REV + E
C_LT = C_CNT + NT
C_TILE = C_LT + E * E
C_LANE = C_TILE + N_TILES
C_TOK1 = C_LANE + P
C_DUMMY = C_TOK1 + NT
C_ALL = C_DUMMY + 1


def decoder_layer(nc, x, ctx_in, w_kv, g_kv, w_q, wq_heads, wk_content, wk_rope, wv, wo_heads, wx_heads,
                  xb, wg, bg, w_exp, b1t, b2, table, out, x2_rows, acc_rows):
    stack = ExitStack()
    with stack:
        def sb(name, shape, dt=F32):
            return stack.enter_context(nc.sbuf_tensor(name, shape, dt))

        def sem(name):
            return stack.enter_context(nc.semaphore(name))

        tab = sb("tab", [P, C_ALL])
        ident = tab[:, C_ID:C_ID + P]
        ident_b = sb("ident_b", [P, P], BF16)
        mask_b = sb("mask_b", [P, P], BF16)
        maskt_b = sb("maskt_b", [P, P], BF16)
        up_b = sb("up_b", [P, P], BF16)
        ones_b = sb("ones_b", [P, P], BF16)
        w_kv_sb = sb("w_kv_sb", [P, DC, KVR])
        w_q_sb = sb("w_q_sb", [P, DC, QR])
        wq_sb = sb("wq_sb", [P, H * QK])
        wkc_sb = sb("wkc_sb", [P, H * QK])
        wkr_sb = sb("wkr_sb", [P, DC, H * QK])
        wv_sb = sb("wv_sb", [KVR, D])
        wo_sb = sb("wo_sb", [P, 4, D])
        wx_sb = sb("wx_sb", [P, 4, D])
        wg_sb = sb("wg_sb", [P, DC, E])
        g_sb = sb("g_sb", [KVR, 1])
        xb_sb = sb("xb_sb", [P, D])
        bg_sb = sb("bg_sb", [P, E])
        b1_sb = sb("b1_sb", [P, E * FC])
        whi = sb("whi", [P, E * EW], F16)
        wlo = sb("wlo", [P, E * EW], F16)
        hi_tail = whi[:, EARLY * EW:E * EW].bitcast(F32)
        lo_tail = wlo[:, EARLY * EW:E * EW].bitcast(F32)
        wstage0 = sb("wstage0", [P, PIECE])

        x_sb = sb("x_sb", [P, TT, D])
        c_sb = sb("c_sb", [P, TT, H, 32])
        xT = sb("xT", [P, DC, T])
        qcT = sb("qcT", [P, T])
        kvn = sb("kvn", [P, TT, KVR])
        kvcT = sb("kvcT", [KVR, T])
        v_sb = lo_tail[:, 2048:3072].rearrange("p (t h d) -> p t h d", t=TT, h=H)
        sq = sb("sq", [P, KVR])
        ss = sb("ss", [P, TT])
        rs = sb("rs", [P, TT])
        swap = [sb(f"swap{i}", [P, 2, T]) for i in range(2)]
        qk = hi_tail.rearrange("p (g a t) -> p g a t", g=H // 2, a=2)
        qk_b = lo_tail[:, 0:2048].bitcast(BF16).rearrange("p (g a t) -> p g a t", g=H // 2, a=2)
        xc = qk[:, 0:4, :, :]
        xc_b = qk_b[:, 0:4, :, :]
        mx = sb("mx", [P, H, 3])
        mx2 = sb("mx2", [P, H])
        negm = sb("negm", [P, TT, P], BF16)
        mT = sb("mT", [P, T], BF16)
        probs = sb("probs", [P, 4, 2 * T])
        osum = [sb(f"osum{i}", [P, T]) for i in range(2)]
        oT = sb("oT", [P, 4, T])
        stats = sb("stats", [P, TT, 6])
        mv = sb("mv", [P, TT, 2])
        rstd = sb("rstd", [P, TT])
        spare = sb("spare", [P, 1])
        minus_half = sb("minus_half", [P, 4])
        x1 = sb("x1", [P, TT, D])
        x1p = lo_tail[:, 3072:4096].rearrange("p (t h d) -> p t h d", t=TT, h=H)
        x2 = sb("x2", [P, TT, D])
        x2T = xT
        logits = sb("logits", [P, NT, E])

        rt = [wo_sb[:, :, :].rearrange("p g d -> p (g d)")[:, i * NT * E:(i + 1) * NT * E].rearrange(
            "p (t e) -> p t e", e=E) for i in range(8)]
        wx_flat = wx_sb[:, :, :].rearrange("p g d -> p (g d)")
        oh_lane = [wx_flat[:, i * P:(i + 1) * P] for i in range(2)]
        oh_tile = [wx_flat[:, 256 + i * 2 * N_TILES:256 + (i + 1) * 2 * N_TILES] for i in range(2)]
        over_rank = probs[:, :, :].rearrange("p a n -> p (a n)").rearrange("p (m k) -> p m k", k=NT)
        ttmp = wx_flat[:, 512:512 + N_TILES * E].rearrange("p (i e) -> p i e", e=E)
        ltmp = wx_flat[:, 840:840 + E * NT]
        rs1 = [sb(f"rs1_{i}", [P, NT]) for i in range(8)]
        m_b = sb("m_b", [P, NT, E], BF16)
        ex = [sb(f"ex{i}", [P, E]) for i in range(4)]
        slot_w = sb("slot_w", [P, N_TILES])
        slot_t = [sb(f"slot_t{i}", [P, N_TILES]) for i in range(3)]
        slot_row = sb("slot_row", [P, N_TILES], I32)
        tile_e = sb("tile_e", [P, N_TILES], I32)
        wstage = [wstage0[:, :], c_sb[:, :, :, :].rearrange("p t h d -> p (t h d)")]

        b2_sb = wkr_sb[:, :, :].rearrange("p c n -> p (c n)")
        xg = [x_sb[:, i, :] for i in range(2)]
        idx_g = [sb(f"idx_g{i}", [P, 1], I32) for i in range(2)]
        idx_s = [sb(f"idx_s{i}", [P, 1], I32) for i in range(2)]
        xparts = xT[:, :, :].rearrange("p c t -> p (c t)").bitcast(F16).rearrange("p (u k c t) -> p u k c t", u=2, k=2, c=DC)
        xh = [xparts[:, i, 0, :, :] for i in range(2)]
        xl = [xparts[:, i, 1, :, :] for i in range(2)]
        act = probs[:, :, :].rearrange("p a n -> p (a n)").rearrange("p (u f t) -> p u f t", u=2, f=FC)
        ah = wq_sb[:, :].bitcast(F16).rearrange("p (u f t) -> p u f t", u=2, f=FC)
        al = wkc_sb[:, :].bitcast(F16).rearrange("p (u f t) -> p u f t", u=2, f=FC)
        yb = [x1[:, i, :] for i in range(2)]
        fin = whi[:, 0:NT * D * 2].bitcast(F32).rearrange("p (t d) -> p t d", d=D)
        fst = sb("fst", [P, NT, 6])
        fmv = sb("fmv", [P, NT, 2])
        frs = sb("frs", [P, NT])

        bank = [stack.enter_context(nc.psum_tensor(f"bank{i}", [P, 512], F32)) for i in range(8)]
        ps_s, ps_t, ps_o, ps_m = bank[0:2], bank[2:4], bank[4:6], bank[6:8]

        c_ld = sem("consts_loaded")
        c_ms = sem("pads_set")
        c_bf = sem("bf16_consts")
        x_ld, ctx_ld = sem("x_loaded"), sem("ctx_loaded")
        w_ld = [sem(f"wstage_loaded{i}") for i in range(2)]
        w_hi, w_lo = sem("w_high_done"), sem("w_low_done")
        pe_xT, v_xT = sem("pe_x_transposed"), sem("xT_ready")
        pe_qkv, a_qc = sem("pe_latents"), sem("qc_ready")
        a_ss, v_kvn = sem("kv_squares"), sem("kv_normed")
        pe_kvT, v_kvT = sem("pe_kv_transposed"), sem("kvcT_ready")
        pe_v, a_v = sem("pe_values"), sem("values_ready")
        pe_qk, v_sw = sem("pe_qk"), sem("qk_swapped")
        p_sin, v_qk, a_qkb = sem("qk_sin_done"), sem("qk_ready"), sem("qk_bf16_ready")
        pe_s, v_mx = sem("pe_scores"), sem("max_done")
        v_nm, pe_mT, v_mT = sem("neg_max_ready"), sem("pe_max_transposed"), sem("maxT_ready")
        pe_t, a_p = sem("pe_scoresT"), sem("probs_ready")
        pe_pv, v_o = sem("pe_pv"), sem("out_normed")
        pe_wo, v_x1, a_x1p = sem("pe_wo"), sem("x1_ready"), sem("x1_padded")
        pe_xc, v_xc, a_xcb = sem("pe_cross_transposed"), sem("cross_ready"), sem("cross_bf16_ready")
        pe_wx, v_x2 = sem("pe_wx"), sem("x2_ready")
        x2_st = sem("x2_stored")
        b2_ld = sem("b2_loaded")
        pe_x2T, a_x2T = sem("pe_x2_transposed"), sem("x2T_ready")
        pe_lg, v_lg = sem("pe_logits"), sem("logits_ready")
        v_var, p_rs = sem("variance_ready"), sem("inverse_root_ready")
        v_ch = sem("vector_chain")
        v_rl, a_re, v_m = sem("shifted_logits"), sem("gate_exp"), sem("choices_ready")
        pe_rank, v_oh, pe_slot = sem("pe_ranks"), sem("onehots_ready"), sem("pe_slots")
        v_te, v_rows = sem("tile_experts_ready"), sem("slot_rows_ready")
        p_ix0, p_ix, p_ixs = sem("first_gather_index_ready"), sem("gather_index_ready"), sem("scatter_index_ready")
        g_ld = [sem(f"slots_gathered{i}") for i in range(2)]
        pe_ft, a_xh, v_xl = sem("pe_slots_transposed"), sem("slots_high"), sem("slots_low")
        pe_h, a_g = sem("pe_hidden"), sem("hidden_act")
        v_ah, v_al = sem("hidden_high"), sem("hidden_low")
        pe_y, v_yt, v_y = sem("pe_expert_out"), sem("expert_biased"), sem("expert_weighted")
        sc_st = sem("scatter_added")
        f_ld, v_f, f_st = sem("sums_loaded"), sem("final_ready"), sem("out_stored")

        loads = [(tab[:, :], table[:, :]),
                 (w_kv_sb[:, :, :], w_kv.rearrange("(c p) n -> p c n", p=P)),
                 (w_q_sb[:, :, :], w_q.rearrange("(c p) n -> p c n", p=P)),
                 (wq_sb[:, :], wq_heads[:, :]), (wkc_sb[0:KVR, :], wk_content[:, :]),
                 (wkr_sb[:, :, :], wk_rope.rearrange("(c p) n -> p c n", p=P)),
                 (wv_sb[:, :], wv[:, :]), (wo_sb[:, :, :], wo_heads.rearrange("(g p) n -> p g n", p=P)),
                 (wx_sb[:, :, :], wx_heads.rearrange("(g p) n -> p g n", p=P)),
                 (wg_sb[:, :, :], wg.rearrange("(c p) n -> p c n", p=P)),
                 (g_sb[:, :], g_kv.rearrange("(r a) -> r a", a=1)),
                 (xb_sb[:, :], xb.partition_broadcast(P)), (bg_sb[:, :], bg.partition_broadcast(P)),
                 (b1_sb[:, :], b1t[:, :])]
        N_LOADS = len(loads)
        LATE = (E - EARLY) * PIECES

        x_rows = x.rearrange("b (t p) d -> p (b t) d", p=P)
        c_rows = ctx_in.rearrange("b (t p) (h d) -> p (b t) h d", p=P, d=HD)
        w_pieces = w_exp.rearrange("n p f -> p n f")
        x2_st_rows = x2_rows[0:TOK, :].rearrange("(t p) d -> p t d", p=P)
        acc_st_rows = acc_rows[0:TOK, :].rearrange("(t p) d -> p t d", p=P)
        out_rows = out.rearrange("b (t p) d -> p (b t) d", p=P)

        block = stack.enter_context(nc.Block())

        @block.sync
        def _(sp):
            for dst, src in loads:
                sp.dma_start(dst, src).then_inc(c_ld, 16)
            sp.wait_ge(c_ms, 1)
            sp.dma_start(x2_rows[TOK:ROWS, :], oT[:, 0, :]).then_inc(x2_st, 16)
            sp.dma_start(acc_rows[TOK:ROWS, :], oT[:, 0, :]).then_inc(x2_st, 16)
            sp.wait_ge(x2_st, 32)
            with sp.Fori(0, B) as b:
                sp.wait_ge(v_x1, b + 1)
                sp.dma_start(x_sb[:, :, :], x_rows[:, bass.ds(b * TT, TT), :]).then_inc(x_ld, 16)
                sp.wait_ge(v_x2, b + 1)
                for t in range(TT):
                    sp.dma_start(c_sb[:, t, :, 0:HD], c_rows[:, bass.ds(b * TT + t, 1), :, :]).then_inc(ctx_ld, 16)
                for j in range(PER_ROW):
                    sp.wait_ge(w_lo, b * PER_ROW + j + 1)
                    sp.dma_start(wstage[0].unsqueeze(1), w_pieces[:, bass.ds(b * PER_ROW + j, 1), :]).then_inc(w_ld[0], 16)
                sp.wait_ge(v_x2, b + 2)
                sp.dma_start(x2_st_rows[:, bass.ds(b * TT, TT), :], x2[:, :, :]).then_inc(x2_st, 16)
                sp.dma_start(acc_st_rows[:, bass.ds(b * TT, TT), :], x2[:, :, :]).then_inc(x2_st, 16)
            sp.wait_ge(x2_st, 32 * (B + 1))
            sp.dma_start(b2_sb, b2.rearrange("e d -> (e d)").partition_broadcast(P)).then_inc(b2_ld, 16)
            for j in range(LATE):
                sp.wait_ge(w_lo, EARLY * PIECES + 1 + max(j - 1, 0))
                sp.dma_start(wstage[j % 2].unsqueeze(1), w_pieces[:, EARLY * PIECES + j:EARLY * PIECES + j + 1, :]).then_inc(w_ld[j % 2], 16)
            sp.wait_ge(sc_st, 16 * N_TILES)
            for k in range(4):
                sp.dma_start(fin[:, 4 * k:4 * k + 4, :], acc_st_rows[:, 4 * k:4 * k + 4, :]).then_inc(f_ld, 16)
                sp.wait_ge(f_ld, 16 * (k + 1))
            for k in range(4):
                sp.wait_ge(v_f, k + 1)
                sp.dma_start(out_rows[:, 4 * k:4 * k + 4, :], fin[:, 4 * k:4 * k + 4, :]).then_inc(f_st, 16)
            sp.wait_ge(f_st, 64)

        @block.gpsimd
        def _(pool):
            nc.gpsimd.memset(minus_half[:, :], -0.5)
            nc.gpsimd.memset(oT[:, 0, :], 0.0)
            nc.gpsimd.memset(x1p[:, :, :, :], 0.0)
            nc.gpsimd.memset(v_sb[:, :, :, :], 1.0)
            nc.gpsimd.memset(c_sb[:, :, :, :], 1.0).then_inc(c_ms, 1)
            pool.wait_ge(c_ld, 16 * N_LOADS)

            def inverse_root(value, count):
                pool.wait_ge(v_var, count)
                nc.gpsimd.tensor_tensor(value, value, minus_half[:, 0:value.shape[1]], ALU.pow).then_inc(p_rs, 1)

            with pool.Fori(0, B) as b:
                inverse_root(rs[:, :], b * 3 + 1)
                for hp in range(H // 2):
                    pool.wait_ge(v_sw, b * (H // 2) + hp + 1)
                    nc.gpsimd.tensor_tensor(
                        swap[hp % 2][:, :, :], swap[hp % 2][:, :, :],
                        tab[:, C_SIN:C_SIN + T].unsqueeze(1).broadcast_to([P, 2, T]), ALU.mult).then_inc(p_sin, 1)
                inverse_root(rstd[:, :], b * 3 + 2)
                inverse_root(rstd[:, :], b * 3 + 3)
            pool.wait_ge(v_rows, 1)

            def gather(n, u, gate):
                if gate is not None:
                    pool.wait_ge(pe_ft, gate)
                first = gate is None
                nc.gpsimd.tensor_copy(idx_g[u][:, :], slot_row[:, bass.ds(n, 1)]).then_inc(p_ix0 if first else p_ix, 1)
                pool.wait_ge(x2_st, 32 * (B + 1))
                pool.wait_ge(p_ix0 if first else p_ix, n + 1 if first else gate)
                nc.gpsimd.indirect_dma_start(
                    out=xg[u], out_offset=None, in_=x2_rows[:, :],
                    in_offset=bass.IndirectOffsetOnAxis(ap=idx_g[u][:, 0:1], axis=0)).then_inc(g_ld[u], 16)

            def scatter(n, u, after):
                if after is not None:
                    pool.wait_ge(sc_st, after)
                nc.gpsimd.tensor_copy(idx_s[u][:, :], slot_row[:, bass.ds(n, 1)]).then_inc(p_ixs, 1)
                pool.wait_ge(x2_st, 32 * (B + 1))
                pool.wait_ge(p_ixs, n + 1)
                pool.wait_ge(v_y, n + 1)
                nc.gpsimd.indirect_dma_start(
                    out=acc_rows[:, :], out_offset=bass.IndirectOffsetOnAxis(ap=idx_s[u][:, 0:1], axis=0),
                    in_=yb[u], in_offset=None, compute_op=ALU.add).then_inc(sc_st, 16)

            gather(0, 0, None)
            gather(1, 1, None)
            gather(2, 0, 1)
            scatter(0, 0, None)
            with pool.Fori(0, (N_TILES - 3) // 2) as j:
                for u in range(2):
                    gather(j * 2 + 3 + u, (1 + u) % 2, j * 2 + 2 + u)
                    scatter(j * 2 + 1 + u, (1 + u) % 2, (j * 2 + 1 + u) * 16)
            for n in range(N_TILES - 2, N_TILES):
                scatter(n, n % 2, 16 * n)
            pool.wait_ge(sc_st, 16 * N_TILES)
            for k in range(4):
                inverse_root(frs[:, 4 * k:4 * k + 4], B * 3 + k + 1)

        @block.scalar
        def _(act_e):
            act_e.wait_ge(c_ld, 16 * N_LOADS)
            act_e.wait_ge(c_ms, 1)

            def split_high(stage, loaded, p):
                act_e.wait_ge(w_ld[stage], loaded)
                nc.scalar.activation(whi[:, bass.ds(p * PIECE, PIECE)], wstage[stage], ACT.Copy, scale=W_SCALE).then_inc(w_hi, 1)

            with act_e.Fori(0, B) as b:
                act_e.wait_ge(pe_qkv, b + 1)
                nc.scalar.activation(qcT[:, :], ps_m[1][:, 0:T], ACT.Copy).then_inc(a_qc, 1)
                for t in range(TT):
                    if t:
                        act_e.wait_ge(a_ss, b * TT + t)
                    nc.scalar.activation(sq[:, :], ps_m[0][:, t * KVR:(t + 1) * KVR], ACT.Square,
                                         accum_out=ss[:, t:t + 1]).then_inc(a_ss, 1)
                act_e.wait_ge(pe_v, b + 1)
                nc.scalar.activation(v_sb[:, :, :, 0:HD].rearrange("p t h d -> p (t h) d"),
                                     ps_m[1][:, :].rearrange("p (s d) -> p s d", d=HD), ACT.Copy).then_inc(a_v, 1)
                for hp in range(H // 2):
                    act_e.wait_ge(v_qk, b * (H // 2) + hp + 1)
                    nc.scalar.activation(qk_b[:, hp, :, :], qk[:, hp, :, :], ACT.Copy).then_inc(a_qkb, 1)
                for h in range(H):
                    act_e.wait_ge(pe_t, b * (2 * H) + h + 1)
                    if h % 4 == 0 and h:
                        act_e.wait_ge(pe_pv, b * 8 + h // 4)
                    nc.scalar.activation(probs[:, h % 4, 0:3 * P], ps_t[h % 2][:, 0:3 * P], ACT.Exp,
                                         scale=SELF_SCALE).then_inc(a_p, 1)
                    if h % 4 == 3 and h // 4 < PER_ROW:
                        split_high(0, b * (16 * PER_ROW) + 16 * (h // 4) + 16, b * PER_ROW + h // 4)
                act_e.wait_ge(v_x1, b + 2)
                nc.scalar.activation(x1p[:, :, :, 0:HD].rearrange("p t h d -> p (t h) d"),
                                     x1[:, :, :].rearrange("p t (h d) -> p (t h) d", d=HD), ACT.Copy).then_inc(a_x1p, 1)
                for g in range(4):
                    act_e.wait_ge(v_xc, b * 4 + g + 1)
                    nc.scalar.activation(xc_b[:, g, :, :], xc[:, g, :, :], ACT.Copy).then_inc(a_xcb, 1)
                for h in range(H):
                    act_e.wait_ge(pe_t, b * (2 * H) + H + h + 1)
                    if h % 4 == 0 and h:
                        act_e.wait_ge(pe_pv, b * 8 + 4 + h // 4)
                    nc.scalar.activation(probs[:, h % 4, :], ps_t[h % 2][:, :], ACT.Exp,
                                         scale=CROSS_SCALE).then_inc(a_p, 1)
                act_e.wait_ge(pe_x2T, b + 1)
                nc.scalar.activation(x2T[:, :, :].rearrange("p c t -> p (c t)"), ps_m[0][:, :], ACT.Copy).then_inc(a_x2T, 1)

            act_e.wait_ge(v_rl, 1)
            nc.scalar.activation(rt[1][:, :, :], rt[0][:, :, :], ACT.Exp).then_inc(a_re, 1)

            for j in range(LATE):
                split_high(j % 2, (B * PER_ROW if j % 2 == 0 else 0) * 16 + 16 * (j // 2) + 16, EARLY * PIECES + j)
            act_e.wait_ge(v_te, 1)

            def hidden(n, u, e):
                act_e.wait_ge(pe_ft, n + 1)
                nc.scalar.activation(xh[u][:, :, :].rearrange("p c t -> p (c t)"), bank[u][:, 0:D], ACT.Copy).then_inc(a_xh, 1)
                for half in range(2):
                    act_e.wait_ge(pe_h, n * 2 + half + 1)
                    for f in range(4 * half, 4 * half + 4):
                        last = nc.scalar.activation(
                            act[:, u, f, :], bank[2 + 2 * u + half][:, (f % 4) * P:(f % 4 + 1) * P], ACT.Gelu,
                            bias=b1_sb[:, bass.ds(e * FC + f, 1)], scale=1.0 / W_SCALE)
                    last.then_inc(a_g, 1)

            def expert(n):
                return act_e.value_load(tile_e[0:1, bass.ds(n, 1)], min_val=0, max_val=E - 1)

            hidden(0, 0, expert(0))
            hidden(1, 1, expert(1))
            act_e.wait_ge(v_al, 2)
            hidden(2, 0, expert(2))
            with act_e.Fori(0, (N_TILES - 3) // 2) as j:
                for u in range(2):
                    act_e.wait_ge(v_al, j * 4 + 2 * u + 4)
                    hidden(j * 2 + 3 + u, (1 + u) % 2, expert(j * 2 + 3 + u))

        @block.vector
        def _(dve):
            chain = {"n": 0, "base": 0}

            def link(ins, plain=False):
                chain["n"] += 1
                ins.then_inc(v_ch, 1)
                dve.wait_ge(v_ch, chain["base"] + chain["n"])
                if plain:
                    nc.vector.memset(spare[:, :], 0.0)

            dve.wait_ge(c_ld, 16 * N_LOADS)
            nc.vector.memset(ones_b[:, :], 1.0)
            nc.vector.tensor_copy(ident_b[:, :], ident)
            nc.vector.tensor_copy(mask_b[:, :], tab[:, C_MASK:C_MASK + P])
            nc.vector.tensor_copy(maskt_b[:, :], tab[:, C_MASKT:C_MASKT + P])
            nc.vector.tensor_copy(up_b[:, :], tab[:, C_UP:C_UP + P]).then_inc(c_bf, 1)
            nc.vector.memset(rs[:, :], 0.0).then_inc(v_x1, 1)
            nc.vector.memset(rstd[:, :], 0.0).then_inc(v_x2, 1)
            nc.vector.memset(negm[:, :, :], 0.0)
            link(nc.vector.memset(ss[:, 0:1], 0.0))
            nc.vector.memset(mx2[:, :], 0.0).then_inc(w_lo, 1)
            chain["base"], chain["n"] = 0, 1
            BASE = 1

            def split_low(stage, p):
                dve.wait_ge(w_hi, p + 1)
                at = bass.ds(p * PIECE, PIECE)
                nc.vector.scalar_tensor_tensor(wlo[:, at], wstage[stage], W_SCALE, whi[:, at],
                                               ALU.mult, ALU.subtract).then_inc(w_lo, 1)

            def layer_norm(src, dst, roots, done):
                for t in range(TT):
                    last = nc.vector.bn_stats(stats[:, t, :], src[:, t, :])
                link(last, plain=True)
                for t in range(TT):
                    last = nc.vector.bn_aggr(mv[:, t, :], stats[:, t, :])
                link(last)
                nc.vector.tensor_scalar(rstd[:, :], mv[:, :, 1], LN_EPS, None, ALU.add).then_inc(v_var, 1)
                dve.wait_ge(p_rs, roots)
                for t in range(TT):
                    last = nc.vector.tensor_scalar(dst[:, t, :], src[:, t, :], mv[:, t, 0:1], rstd[:, t:t + 1],
                                                   ALU.subtract, ALU.mult)
                last.then_inc(done, 1)

            def normalise(b, phase, g):
                dve.wait_ge(c_ld, 16 * N_LOADS)
                dve.wait_ge(pe_pv, b * 8 + 4 * phase + g + 1)
                link(nc.vector.stream_shuffle(osum[g % 2][:, :], ps_o[g % 2][:, 0:T], [16 + i % 16 for i in range(32)]))
                link(nc.vector.reciprocal(osum[g % 2][:, :], osum[g % 2][:, :]))
                nc.vector.tensor_tensor(oT[:, g, :], ps_o[g % 2][:, 0:T], osum[g % 2][:, :], ALU.mult).then_inc(v_o, 1)

            def max_transposed(b, phase):
                dve.wait_ge(pe_mT, b * 2 + phase + 1)
                nc.vector.tensor_copy(mT[:, :], ps_m[0][:, 0:T // 2].bitcast(BF16)).then_inc(v_mT, 1)

            VCH = 24
            with dve.Fori(0, B) as b:
                chain["base"], chain["n"] = b * VCH + BASE, 0
                dve.wait_ge(pe_xT, b + 1)
                nc.vector.tensor_copy(xT[:, :, :].rearrange("p c t -> p (c t)"), ps_m[0][:, :]).then_inc(v_xT, 1)
                dve.wait_ge(a_ss, b * TT + TT)
                nc.vector.tensor_scalar(rs[:, :], ss[:, :], 1.0 / KVR, RMS_EPS, ALU.mult, ALU.add).then_inc(v_var, 1)
                dve.wait_ge(p_rs, b * 3 + 1)
                for t in range(TT):
                    last = nc.vector.tensor_scalar(kvn[:, t, :], ps_m[0][:, t * KVR:(t + 1) * KVR], rs[:, t:t + 1],
                                                   None, ALU.mult)
                last.then_inc(v_kvn, 1)
                dve.wait_ge(pe_kvT, b + 1)
                nc.vector.tensor_scalar(kvcT[:, :], ps_m[0][0:KVR, 0:T], g_sb[:, 0:1], None, ALU.mult).then_inc(v_kvT, 1)
                for hp in range(H // 2):
                    dve.wait_ge(pe_qk, b * (H // 2) + hp + 1)
                    nc.vector.tensor_tensor(qk[:, hp, :, :], ps_s[hp % 2][:, :].rearrange("p (a t) -> p a t", a=2),
                                            tab[:, C_COS:C_COS + T].unsqueeze(1).broadcast_to([P, 2, T]), ALU.mult)
                    nc.vector.stream_shuffle(swap[hp % 2][:, :, :].rearrange("p a t -> p (a t)"), ps_s[hp % 2][:, :],
                                             [(i + 16) % 32 for i in range(32)]).then_inc(v_sw, 1)
                    dve.wait_ge(p_sin, b * (H // 2) + hp + 1)
                    nc.vector.tensor_tensor(qk[:, hp, :, :], qk[:, hp, :, :], swap[hp % 2][:, :, :],
                                            ALU.add).then_inc(v_qk, 1)
                for h in range(H):
                    dve.wait_ge(pe_s, b * (2 * H) + h + 1)
                    nc.vector.tensor_reduce(mx[:, h, :], ps_s[h % 2][:, 0:3 * P].rearrange("p (a k) -> p a k", a=3),
                                            axis=AX.X, op=ALU.max).then_inc(v_mx, 1)
                dve.wait_ge(v_mx, b * (2 * H) + H)
                nm = negm[:, :, :].rearrange("p t (a n) -> p t a n", a=2)[:, :, :, 0:H // 2]
                nc.vector.tensor_scalar(nm[:, 0], mx[:, :, 0].rearrange("p (n a) -> p a n", a=2), -1.0, None, ALU.mult)
                link(nc.vector.tensor_tensor(mx2[:, :], mx[:, :, 1], mx[:, :, 2], ALU.max))
                nc.vector.tensor_scalar(nm[:, 1], mx2[:, :].rearrange("p (n a) -> p a n", a=2), -1.0, None, ALU.mult).then_inc(v_nm, 1)
                max_transposed(b, 0)
                for g in range(4):
                    normalise(b, 0, g)
                    if g < PER_ROW:
                        split_low(0, b * PER_ROW + g)
                dve.wait_ge(pe_wo, b + 1)
                link(nc.vector.tensor_tensor(x1[:, :, :].rearrange("p t d -> p (t d)"), ps_m[1][:, :],
                                             x_sb[:, :, :].rearrange("p t d -> p (t d)"), ALU.add))
                layer_norm(x1, x1, b * 3 + 2, v_x1)
                for g in range(4):
                    dve.wait_ge(pe_xc, b * 4 + g + 1)
                    nc.vector.tensor_copy(xc[:, g, :, :].rearrange("p a t -> p (a t)"), ps_s[g % 2][:, :]).then_inc(v_xc, 1)
                for h in range(H):
                    dve.wait_ge(pe_s, b * (2 * H) + H + h + 1)
                    nc.vector.tensor_reduce(mx[:, h, 0:2], ps_s[h % 2][:, :].rearrange("p (a k) -> p a k", a=2),
                                            axis=AX.X, op=ALU.max).then_inc(v_mx, 1)
                dve.wait_ge(v_mx, b * (2 * H) + 2 * H)
                nm = negm[:, :, :].rearrange("p t (j n) -> p t j n", j=4)[:, :, :, 0:H // 4]
                for t in range(TT):
                    last = nc.vector.tensor_scalar(nm[:, t], mx[:, :, t].rearrange("p (n j) -> p j n", j=4), -1.0, None, ALU.mult)
                last.then_inc(v_nm, 1)
                max_transposed(b, 1)
                for g in range(4):
                    normalise(b, 1, g)
                dve.wait_ge(pe_wx, b + 1)
                dve.wait_ge(x2_st, b * 32 + 32)
                for t in range(TT):
                    last = nc.vector.tensor_tensor(x2[:, t, :], ps_m[1][:, t * D:(t + 1) * D], xb_sb[:, :], ALU.add)
                link(last)
                link(nc.vector.tensor_tensor(x2[:, :, :], x2[:, :, :], x1[:, :, :], ALU.add))
                layer_norm(x2, x2, b * 3 + 3, v_x2)
                dve.wait_ge(pe_lg, b + 1)
                nc.vector.tensor_tensor(logits[:, bass.ds(b * TT, TT), :],
                                        ps_m[1][:, 0:TT * E].rearrange("p (t e) -> p t e", e=E),
                                        bg_sb[:, :].unsqueeze(1).broadcast_to([P, TT, E]), ALU.add).then_inc(v_lg, 1)
                used = chain["n"]
            assert used == VCH, used
            chain["base"], chain["n"] = B * VCH + BASE, 0

            def over_e(a):
                return a[:, :].unsqueeze(2).broadcast_to([P, NT, E])

            def tab_e(col):
                return tab[:, col:col + E].unsqueeze(1).broadcast_to([P, NT, E])

            dve.wait_ge(v_lg, B)
            top, total, best1, best2 = rs1[0], rs1[1], rs1[2], rs1[3]
            link(nc.vector.tensor_reduce(top[:, :], logits[:, :, :], axis=AX.X, op=ALU.max))
            nc.vector.tensor_tensor(rt[0][:, :, :], logits[:, :, :], over_e(top), ALU.subtract).then_inc(v_rl, 1)
            dve.wait_ge(a_re, 1)
            link(nc.vector.tensor_reduce(total[:, :], rt[1][:, :, :], axis=AX.X, op=ALU.add))
            prob = rt[2]
            link(nc.vector.reciprocal(total[:, :], total[:, :]))
            link(nc.vector.tensor_tensor(prob[:, :, :], rt[1][:, :, :], over_e(total), ALU.mult))

            def choose(src, best, rank, onehot, tmp):
                link(nc.vector.tensor_reduce(best[:, :], src[:, :, :], axis=AX.X, op=ALU.max))
                link(nc.vector.tensor_tensor(tmp[:, :, :], src[:, :, :], over_e(best), ALU.is_equal))
                link(nc.vector.tensor_tensor(tmp[:, :, :], tmp[:, :, :], tab_e(C_REV), ALU.mult))
                link(nc.vector.tensor_reduce(rank[:, :], tmp[:, :, :], axis=AX.X, op=ALU.max))
                link(nc.vector.tensor_tensor(onehot[:, :, :], tmp[:, :, :], over_e(rank), ALU.is_equal))

            first, second = rt[4], rt[5]
            choose(prob, best1, rs1[4], first, rt[3])
            rest = rt[6]
            link(nc.vector.scalar_tensor_tensor(rest[:, :, :].rearrange("p t e -> p (t e)"),
                                                first[:, :, :].rearrange("p t e -> p (t e)"), -2.0,
                                                prob[:, :, :].rearrange("p t e -> p (t e)"), ALU.mult, ALU.add))
            choose(rest, best2, rs1[5], second, rt[3])
            nc.vector.tensor_tensor(m_b[:, :, :], first[:, :, :], second[:, :, :], ALU.add).then_inc(v_m, 1)
            link(nc.vector.tensor_tensor(rs1[6][:, :], best1[:, :], best2[:, :], ALU.add))
            weight = [rs1[7], rs1[4]]
            link(nc.vector.reciprocal(rs1[6][:, :], rs1[6][:, :]))
            link(nc.vector.tensor_tensor(weight[0][:, :], best1[:, :], rs1[6][:, :], ALU.mult))
            link(nc.vector.tensor_tensor(weight[1][:, :], best2[:, :], rs1[6][:, :], ALU.mult))

            dve.wait_ge(pe_rank, 1)
            count, tiles, start, end = ex[0], ex[1], ex[2], ex[3]
            link(nc.vector.tensor_copy(count[:, :], bank[1][:, 0:E]))
            over = ltmp.rearrange("p (e k) -> p e k", e=E)
            link(nc.vector.tensor_tensor(over, count[:, :].unsqueeze(2).broadcast_to([P, E, NT]),
                                         tab[:, C_CNT:C_CNT + NT].unsqueeze(1).broadcast_to([P, E, NT]), ALU.is_gt))
            link(nc.vector.tensor_reduce(tiles[:, :], over, axis=AX.X, op=ALU.add))
            before = ltmp[:, 0:E * E].rearrange("p (e k) -> p e k", e=E)
            link(nc.vector.tensor_tensor(before, tiles[:, :].unsqueeze(1).broadcast_to([P, E, E]),
                                         tab[:, C_LT:C_LT + E * E].rearrange("p (e k) -> p e k", e=E), ALU.mult))
            link(nc.vector.tensor_reduce(start[:, :], before, axis=AX.X, op=ALU.add))
            link(nc.vector.tensor_tensor(end[:, :], start[:, :], tiles[:, :], ALU.add))
            link(nc.vector.tensor_tensor(ttmp,
                                         tab[:, C_TILE:C_TILE + N_TILES].unsqueeze(2).broadcast_to([P, N_TILES, E]),
                                         end[:, :].unsqueeze(1).broadcast_to([P, N_TILES, E]), ALU.is_ge))
            link(nc.vector.tensor_reduce(slot_t[0][:, :], ttmp, axis=AX.X, op=ALU.add))
            nc.vector.tensor_scalar(tile_e[:, :], slot_t[0][:, :], float(E - 1), None, ALU.min).then_inc(v_te, 1)
            rank = rt[0]
            link(nc.vector.tensor_copy(rank[:, :, :].rearrange("p t e -> p (t e)"), bank[0][:, 0:NT * E]))
            rtile = rt[1]
            link(nc.vector.tensor_tensor(over_rank, rank[:, :, :].rearrange("p t e -> p (t e)").unsqueeze(2).broadcast_to([P, NT * E, NT]),
                                         tab[:, C_CNT:C_CNT + NT].unsqueeze(1).broadcast_to([P, NT * E, NT]), ALU.is_ge))
            link(nc.vector.tensor_reduce(rtile[:, :, :].rearrange("p t e -> p (t e)"), over_rank, axis=AX.X, op=ALU.add))
            link(nc.vector.tensor_scalar(rtile[:, :, :], rtile[:, :, :], -1.0, None, ALU.add))
            lane = rt[2]
            link(nc.vector.scalar_tensor_tensor(lane[:, :, :].rearrange("p t e -> p (t e)"),
                                                rtile[:, :, :].rearrange("p t e -> p (t e)"), -float(P),
                                                rank[:, :, :].rearrange("p t e -> p (t e)"), ALU.mult, ALU.add))
            link(nc.vector.tensor_tensor(rtile[:, :, :], rtile[:, :, :],
                                         start[:, :].unsqueeze(1).broadcast_to([P, NT, E]), ALU.add))
            lanes, tilenos = [rs1[0], rs1[1]], [rs1[2], rs1[3]]
            for k, onehot in enumerate((first, second)):
                for src, dst in ((lane, lanes[k]), (rtile, tilenos[k])):
                    link(nc.vector.tensor_tensor(rt[3][:, :, :], src[:, :, :], onehot[:, :, :], ALU.mult))
                    link(nc.vector.tensor_reduce(dst[:, :], rt[3][:, :, :], axis=AX.X, op=ALU.add))
            steps = [(k, t) for k in range(2) for t in range(NT)]
            for s, (k, t) in enumerate(steps):
                if s >= 2:
                    dve.wait_ge(pe_slot, s - 1)
                nc.vector.tensor_scalar(oh_lane[s % 2], tab[:, C_LANE:C_LANE + P], lanes[k][:, t:t + 1], None, ALU.is_equal)
                nc.vector.tensor_scalar(oh_tile[s % 2][:, 0:N_TILES], tab[:, C_TILE:C_TILE + N_TILES], tilenos[k][:, t:t + 1],
                                        tab[:, C_TOK1 + t:C_TOK1 + t + 1], ALU.is_equal, ALU.mult)
                nc.vector.tensor_scalar(oh_tile[s % 2][:, N_TILES:], tab[:, C_TILE:C_TILE + N_TILES], tilenos[k][:, t:t + 1],
                                        weight[k][:, t:t + 1], ALU.is_equal, ALU.mult).then_inc(v_oh, 1)
            dve.wait_ge(pe_slot, len(steps))
            link(nc.vector.tensor_copy(slot_t[0][:, :], bank[2][:, 0:N_TILES]))
            link(nc.vector.tensor_copy(slot_w[:, :], bank[2][:, N_TILES:2 * N_TILES]))
            link(nc.vector.tensor_scalar(slot_t[1][:, :], slot_t[0][:, :], 0.0, tab[:, C_DUMMY:C_DUMMY + 1],
                                         ALU.is_equal, ALU.mult))
            link(nc.vector.tensor_tensor(slot_t[2][:, :], slot_t[0][:, :], slot_t[1][:, :], ALU.add))
            nc.vector.tensor_scalar(slot_row[:, :], slot_t[2][:, :], -1.0, None, ALU.add).then_inc(v_rows, 1)
            dve.wait_ge(v_rows, 1)

            def low_slots(n, u):
                dve.wait_ge(a_xh, n + 1)
                nc.vector.tensor_tensor(xl[u][:, :, :].rearrange("p c t -> p (c t)"), bank[u][:, 0:D],
                                        xh[u][:, :, :].rearrange("p c t -> p (c t)"), ALU.subtract).then_inc(v_xl, 1)

            def split_hidden(n, u):
                for half in range(2):
                    dve.wait_ge(a_g, n * 2 + half + 1)
                    at = slice(4 * half, 4 * half + 4)
                    nc.vector.tensor_copy(ah[:, u, at, :], act[:, u, at, :]).then_inc(v_ah, 1)
                    dve.wait_ge(v_ah, n * 2 + half + 1)
                    nc.vector.tensor_tensor(al[:, u, at, :], act[:, u, at, :], ah[:, u, at, :], ALU.subtract).then_inc(v_al, 1)

            def weigh(n, u, e, after):
                dve.wait_ge(pe_y, n + 1)
                if after is not None:
                    dve.wait_ge(sc_st, after)
                nc.vector.scalar_tensor_tensor(yb[u], bank[6 + u][:, 0:D], 1.0 / W_SCALE,
                                               b2_sb[:, bass.ds(e * D, D)], ALU.mult, ALU.add).then_inc(v_yt, 1)
                dve.wait_ge(v_yt, n + 1)
                nc.vector.tensor_scalar(yb[u], yb[u], slot_w[:, bass.ds(n, 1)], None, ALU.mult).then_inc(v_y, 1)

            def expert(n):
                return dve.value_load(tile_e[0:1, bass.ds(n, 1)], min_val=0, max_val=E - 1)

            for j in range(LATE):
                split_low(j % 2, EARLY * PIECES + j)
            dve.wait_ge(b2_ld, 16)
            low_slots(0, 0)
            split_hidden(0, 0)
            low_slots(1, 1)
            split_hidden(1, 1)
            weigh(0, 0, expert(0), None)
            low_slots(2, 0)
            split_hidden(2, 0)
            weigh(1, 1, expert(1), None)
            with dve.Fori(0, (N_TILES - 3) // 2) as j:
                for u in range(2):
                    n = j * 2 + 3 + u
                    low_slots(n, (1 + u) % 2)
                    split_hidden(n, (1 + u) % 2)
                    weigh(n - 1, u % 2, expert(n - 1), (j * 2 + 1 + u) * 16)
            weigh(N_TILES - 1, (N_TILES - 1) % 2, expert(N_TILES - 1), (N_TILES - 2) * 16)

            for k in range(4):
                dve.wait_ge(f_ld, 16 * (k + 1))
                at = slice(4 * k, 4 * k + 4)
                for t in range(4 * k, 4 * k + 4):
                    last = nc.vector.bn_stats(fst[:, t, :], fin[:, t, :])
                link(last)
                for t in range(4 * k, 4 * k + 4):
                    last = nc.vector.bn_aggr(fmv[:, t, :], fst[:, t, :])
                link(last)
                nc.vector.tensor_scalar(frs[:, at], fmv[:, at, 1], LN_EPS, None, ALU.add).then_inc(v_var, 1)
                dve.wait_ge(p_rs, B * 3 + k + 1)
                for t in range(4 * k, 4 * k + 4):
                    last = nc.vector.tensor_scalar(fin[:, t, :], fin[:, t, :], fmv[:, t, 0:1], frs[:, t:t + 1],
                                                   ALU.subtract, ALU.mult)
                last.then_inc(v_f, 1)

        @block.tensor
        def _(pe):
            mm = nc.tensor.matmul
            pe.wait_ge(c_ld, 16 * N_LOADS)
            pe.wait_ge(c_bf, 1)

            def transpose_max(b, phase):
                pe.wait_ge(v_nm, b * 2 + phase + 1)
                out_b = ps_m[0][:, 0:T // 2].bitcast(BF16)
                for t in range(TT):
                    last = nc.tensor.transpose(out_b[:, t * P:(t + 1) * P], negm[:, t, :], ident_b[:, :])
                last.then_inc(pe_mT, 1)
                pe.wait_ge(v_mT, b * 2 + phase + 1)

            def weighted_values(b, phase, g, values, causal):
                pe.wait_ge(a_p, b * (2 * H) + phase * H + 4 * g + 4)
                if phase or g >= 2:
                    pe.wait_ge(v_o, b * 8 + phase * 4 + g - 1)
                for k in range(TT):
                    for j in range(4):
                        h = 4 * g + j
                        o = ps_o[g % 2][32 * j:32 * j + 32, :]
                        if k == 0 or not causal:
                            last = mm(o[:, 0:T], values[:, k, h, :], probs[:, h % 4, k * T:(k + 1) * T],
                                      start=(k == 0), stop=(k == 1), skip_group_check=True)
                        else:
                            last = mm(o[:, P:T], values[:, k, h, :], probs[:, h % 4, T:T + P],
                                      start=False, stop=True, skip_group_check=True)
                last.then_inc(pe_pv, 1)

            def project_heads(b, phase, w, done):
                pe.wait_ge(v_o, b * 8 + phase * 4 + 4)
                for t in range(TT):
                    for g in range(4):
                        last = mm(ps_m[1][:, t * D:(t + 1) * D], oT[:, g, t * P:(t + 1) * P], w[:, g, :],
                                  start=(g == 0), stop=(g == 3))
                last.then_inc(done, 1)

            with pe.Fori(0, B) as b:
                pe.wait_ge(x_ld, b * 16 + 16)
                for c in range(DC):
                    for t in range(TT):
                        last = nc.tensor.transpose(ps_m[0][:, c * T + t * P:c * T + (t + 1) * P],
                                                   x_sb[:, t, c * P:(c + 1) * P], ident)
                last.then_inc(pe_xT, 1)
                pe.wait_ge(v_xT, b + 1)
                for c in range(DC):
                    mm(ps_m[1][:, 0:T], w_q_sb[:, c, :], xT[:, c, :], start=(c == 0), stop=(c == DC - 1))
                for t in range(TT):
                    for c in range(DC):
                        last = mm(ps_m[0][:, t * KVR:(t + 1) * KVR], xT[:, c, t * P:(t + 1) * P], w_kv_sb[:, c, :],
                                  start=(c == 0), stop=(c == DC - 1))
                last.then_inc(pe_qkv, 1)
                pe.wait_ge(c_ld, 16 * N_LOADS)
                pe.wait_ge(v_kvn, b + 1)
                for t in range(TT):
                    last = nc.tensor.transpose(ps_m[0][0:KVR, t * P:(t + 1) * P], kvn[:, t, :], ident)
                last.then_inc(pe_kvT, 1)
                pe.wait_ge(a_qc, b + 1)
                pe.wait_ge(v_kvT, b + 1)
                for t in range(TT):
                    last = mm(ps_m[1][:, t * D:(t + 1) * D], kvcT[:, t * P:(t + 1) * P], wv_sb[:, :], start=True, stop=True)
                last.then_inc(pe_v, 1)
                for hp in range(H // 2):
                    at = slice(hp * P, (hp + 1) * P)
                    if hp >= 2:
                        pe.wait_ge(v_sw, b * (H // 2) + hp - 1)
                    mm(ps_s[hp % 2][:, 0:T], wq_sb[:, at], qcT[:, :], start=True, stop=True)
                    for c in range(DC):
                        mm(ps_s[hp % 2][:, T:2 * T], wkr_sb[:, c, at], xT[:, c, :], start=(c == 0), stop=False)
                    mm(ps_s[hp % 2][:, T:2 * T], wkc_sb[0:KVR, at], kvcT[:, :], start=False, stop=True).then_inc(pe_qk, 1)
                pe.wait_ge(v_sw, b * (H // 2) + H // 2)
                for h in range(H):
                    hp, r = h // 2, QK * (h % 2)
                    q, k = qk_b[r:r + QK, hp, 0, :], qk_b[r:r + QK, hp, 1, :]
                    s = ps_s[h % 2]
                    pe.wait_ge(a_qkb, b * (H // 2) + hp + 1)
                    if h >= 2:
                        pe.wait_ge(v_mx, b * (2 * H) + h - 1)
                    mm(s[:, 0:P], q[:, 0:P], k[:, 0:P], start=True, stop=False)
                    mm(s[:, 0:P], ident_b[:, :], mask_b[:, :], start=False, stop=True)
                    mm(s[:, P:3 * P], q[:, P:T], k[:, 0:T], start=True, stop=False, skip_group_check=True)
                    mm(s[:, 2 * P:3 * P], ident_b[:, :], mask_b[:, :], start=False, stop=True,
                       skip_group_check=True).then_inc(pe_s, 1)
                pe.wait_ge(a_v, b + 1)
                transpose_max(b, 0)
                for h in range(H):
                    hp, r = h // 2, QK * (h % 2)
                    q, k = qk[r:r + QK, hp, 0, :], qk[r:r + QK, hp, 1, :]
                    pick = ident_b[r:r + QK, r + hp:r + hp + 1].broadcast_to([QK, P])
                    s = ps_t[h % 2]
                    if h >= 2:
                        pe.wait_ge(a_p, b * (2 * H) + h - 1)
                    mm(s[:, 0:T], k[:, 0:P], q[:, :], start=True, stop=False, skip_group_check=True)
                    mm(s[:, 0:T], pick, mT[r:r + QK, :], start=False, stop=False, skip_group_check=True)
                    mm(s[:, 0:P], ident_b[:, :], maskt_b[:, :], start=False, stop=True, skip_group_check=True)
                    mm(s[:, T:T + P], k[:, P:T], q[:, P:T], start=True, stop=False, skip_group_check=True)
                    mm(s[:, T:T + P], pick, mT[r:r + QK, P:T], start=False, stop=False, skip_group_check=True)
                    mm(s[:, T:T + P], ident_b[:, :], maskt_b[:, :], start=False, stop=True,
                       skip_group_check=True).then_inc(pe_t, 1)
                    if h % 4 == 1 and h >= 4:
                        weighted_values(b, 0, h // 4 - 1, v_sb, True)
                weighted_values(b, 0, 3, v_sb, True)
                project_heads(b, 0, wo_sb, pe_wo)
                pe.wait_ge(ctx_ld, b * 32 + 32)
                pe.wait_ge(a_x1p, b + 1)
                for g in range(4):
                    if g >= 2:
                        pe.wait_ge(v_xc, b * 4 + g - 1)
                    for a, src in enumerate((x1p, c_sb)):
                        for t in range(TT):
                            last = nc.tensor.transpose(
                                ps_s[g % 2][:, a * T + t * P:a * T + (t + 1) * P],
                                src[:, t, 4 * g:4 * g + 4, :].rearrange("p h d -> p (h d)"), ident)
                    last.then_inc(pe_xc, 1)
                pe.wait_ge(v_xc, b * 4 + 4)
                for h in range(H):
                    g, r = h // 4, 32 * (h % 4)
                    q, k = xc_b[r:r + 32, g, 0, :], xc_b[r:r + 32, g, 1, :]
                    pe.wait_ge(a_xcb, b * 4 + g + 1)
                    if h >= 2:
                        pe.wait_ge(v_mx, b * (2 * H) + H + h - 1)
                    for t in range(TT):
                        last = mm(ps_s[h % 2][:, t * T:(t + 1) * T], q[:, t * P:(t + 1) * P], k[:, :], start=True, stop=True)
                    last.then_inc(pe_s, 1)
                transpose_max(b, 1)
                for h in range(H):
                    g, r = h // 4, 32 * (h % 4)
                    q, k = xc[r:r + 32, g, 0, :], xc[r:r + 32, g, 1, :]
                    pick = ident_b[r:r + 32, r + g:r + g + 1].broadcast_to([32, P])
                    pe.wait_ge(a_p, b * (2 * H) + H + h - 1)
                    for t in range(TT):
                        mm(ps_t[h % 2][:, t * T:(t + 1) * T], k[:, t * P:(t + 1) * P], q[:, :], start=True, stop=False)
                        last = mm(ps_t[h % 2][:, t * T:(t + 1) * T], pick, mT[r:r + 32, :], start=False, stop=True)
                    last.then_inc(pe_t, 1)
                    if h % 4 == 1 and h >= 4:
                        weighted_values(b, 1, h // 4 - 1, c_sb, False)
                weighted_values(b, 1, 3, c_sb, False)
                project_heads(b, 1, wx_sb, pe_wx)
                pe.wait_ge(v_x2, b + 2)
                for c in range(DC):
                    for t in range(TT):
                        last = nc.tensor.transpose(ps_m[0][:, c * T + t * P:c * T + (t + 1) * P],
                                                   x2[:, t, c * P:(c + 1) * P], ident)
                last.then_inc(pe_x2T, 1)
                pe.wait_ge(a_x2T, b + 1)
                for t in range(TT):
                    for c in range(DC):
                        last = mm(ps_m[1][:, t * E:(t + 1) * E], x2T[:, c, t * P:(t + 1) * P], wg_sb[:, c, :],
                                  start=(c == 0), stop=(c == DC - 1))
                last.then_inc(pe_lg, 1)

            pe.wait_ge(v_m, 1)
            m_flat = m_b[:, :, :].rearrange("p t e -> p (t e)")
            mm(bank[0][:, 0:NT * E], up_b[:, :], m_flat, start=True, stop=False, skip_group_check=True)
            for t in range(NT - 1):
                mm(bank[0][:, (t + 1) * E:NT * E].rearrange("p (t e) -> p t e", e=E), ones_b[:, :],
                   m_b[:, t:t + 1, :].broadcast_to([P, NT - 1 - t, E]), start=False, stop=(t == NT - 2), skip_group_check=True)
            for t in range(NT):
                last = mm(bank[1][:, 0:E], ones_b[:, :], m_b[:, t, :], start=(t == 0), stop=(t == NT - 1))
            last.then_inc(pe_rank, 1)
            for s in range(2 * NT):
                pe.wait_ge(v_oh, s + 1)
                mm(bank[2][:, 0:2 * N_TILES], oh_lane[s % 2], oh_tile[s % 2], start=(s == 0),
                   stop=(s == 2 * NT - 1)).then_inc(pe_slot, 1)

            pe.wait_ge(v_rows, 1)

            def up(n, u, e, loaded):
                pe.wait_ge(g_ld[u], loaded)
                for c in range(DC):
                    last = nc.tensor.transpose(bank[u][:, c * P:(c + 1) * P], xg[u][:, c * P:(c + 1) * P], ident)
                last.then_inc(pe_ft, 1)
                pe.wait_ge(v_xl, n + 1)
                for half in range(2):
                    for f in range(4 * half, 4 * half + 4):
                        o = bank[2 + 2 * u + half][:, (f % 4) * P:(f % 4 + 1) * P]
                        for c in range(DC):
                            at = bass.ds(e * EW + c * F + f * P, P)
                            mm(o, whi[:, at], xh[u][:, c, :], start=(c == 0), stop=False)
                            mm(o, whi[:, at], xl[u][:, c, :], start=False, stop=False)
                            last = mm(o, wlo[:, at], xh[u][:, c, :], start=False, stop=(c == DC - 1))
                    last.then_inc(pe_h, 1)

            def down(n, u, e):
                pe.wait_ge(v_al, n * 2 + 2)
                for f in range(FC):
                    at = bass.ds(e * EW + (DC * F + f * D), D)
                    o = bank[6 + u][:, 0:D]
                    mm(o, ah[:, u, f, :], whi[:, at], start=(f == 0), stop=False)
                    mm(o, ah[:, u, f, :], wlo[:, at], start=False, stop=False)
                    last = mm(o, al[:, u, f, :], whi[:, at], start=False, stop=(f == FC - 1))
                last.then_inc(pe_y, 1)

            def expert(n):
                return pe.value_load(tile_e[0:1, bass.ds(n, 1)], min_val=0, max_val=E - 1)

            pe.wait_ge(w_lo, E * PIECES + 1)
            up(0, 0, expert(0), 16)
            up(1, 1, expert(1), 16)
            down(0, 0, expert(0))
            pe.wait_ge(a_g, 2)
            up(2, 0, expert(2), 32)
            down(1, 1, expert(1))
            with pe.Fori(0, (N_TILES - 3) // 2) as j:
                for u in range(2):
                    n = j * 2 + 3 + u
                    e, e_before = expert(n), expert(n - 1)
                    pe.wait_ge(a_g, j * 4 + 2 * u + 4)
                    up(n, (1 + u) % 2, e, j * 16 + 32 + 16 * u)
                    pe.wait_ge(v_y, j * 2 + u + 1)
                    down(n - 1, u % 2, e_before)
            pe.wait_ge(v_y, N_TILES - 2)
            down(N_TILES - 1, (N_TILES - 1) % 2, expert(N_TILES - 1))


def _table():
    import numpy as np
    t = np.zeros((P, C_ALL), np.float32)
    lane = np.arange(P)
    inv = 1.0 / 10000.0 ** (np.arange(0, RD, 2, dtype=np.float32) / RD)
    freqs = np.outer(np.arange(T, dtype=np.float32), inv).astype(np.float32)
    r = lane % QK - (QK - RD)
    rot = r >= 0
    i = np.where(rot, r, 0) % (RD // 2)
    sign = np.where(r < RD // 2, -1.0, 1.0)
    t[:, C_COS:C_COS + T] = np.where(rot[:, None], np.cos(freqs).T[i], 1.0)
    t[:, C_SIN:C_SIN + T] = np.where(rot[:, None], np.sin(freqs).T[i] * sign[:, None], 0.0)
    t[:, C_ID:C_ID + P] = np.eye(P)
    t[:, C_MASK:C_MASK + P] = np.where(lane[None, :] > lane[:, None], -1e30, 0.0)
    t[:, C_MASKT:C_MASKT + P] = np.where(lane[:, None] > lane[None, :], -1e30, 0.0)
    t[:, C_UP:C_UP + P] = lane[:, None] < lane[None, :]
    t[:, C_REV:C_REV + E] = E - np.arange(E)
    t[:, C_CNT:C_CNT + NT] = P * np.arange(NT)
    t[:, C_LT:C_LT + E * E] = (np.arange(E)[None, :] < np.arange(E)[:, None]).reshape(-1)
    t[:, C_TILE:C_TILE + N_TILES] = np.arange(N_TILES)
    t[:, C_LANE:C_LANE + P] = lane
    t[:, C_TOK1:C_TOK1 + NT] = P * np.arange(NT)[None, :] + lane[:, None] + 1
    t[:, C_DUMMY] = TOK + 1 + lane
    return t


def kernel(**inputs):
    import numpy as np
    import concourse.bacc as bacc
    from concourse.bass_utils import run_bass_kernel_spmd as run

    a = {k: np.asarray(v) for k, v in inputs.items()}

    def heads(w, at, width):
        o = np.zeros((w.shape[0], H, QK), np.float32)
        o[:, :, at:at + width] = w.reshape(w.shape[0], H, width)
        return o.reshape(w.shape[0], H * QK)

    def rows32(w):
        o = np.zeros((H, 32, D), np.float32)
        o[:, 0:HD, :] = w.reshape(H, HD, D)
        return o.reshape(H * 32, D)

    wq = heads(a["L0_attn_W_qdec"], 0, HD)
    wq.reshape(QR, H, QK)[:, :, QK - RD:] = a["L0_attn_W_qrope"].reshape(QR, H, RD)
    w2 = a["L0_ffn_W2"].reshape(E, 2, FC // 2, P, D).transpose(0, 1, 3, 2, 4).reshape(E, 2, P, PIECE)
    w_exp = np.concatenate([a["L0_ffn_W1"].reshape(E, DC, P, F), w2], 1).reshape(E * PIECES, P, PIECE)
    arrays = {
        "x": a["x"], "ctx": a["ctx_1024"], "w_kv": a["L0_attn_W_kv"], "g_kv": a["L0_attn_g_kv"], "w_q": a["L0_attn_W_q"],
        "wq_heads": wq, "wk_content": heads(a["L0_attn_W_kdec"], 0, HD), "wk_rope": heads(a["L0_attn_W_krope"], QK - RD, RD),
        "wv": a["L0_attn_W_vdec"], "wo_heads": rows32(a["L0_attn_W_o"]), "wx_heads": rows32(a["L0_xattn_W"].T),
        "xb": a["L0_xattn_b"], "wg": a["L0_ffn_Wg"], "bg": a["L0_ffn_bg"], "w_exp": w_exp,
        "b1t": a["L0_ffn_b1"].reshape(E, FC, P).transpose(2, 0, 1).reshape(P, E * FC),
        "b2": a["L0_ffn_b2"], "table": _table()}
    arrays = {"in_" + k: np.ascontiguousarray(v) for k, v in arrays.items()}
    nc = bacc.Bacc("TRN2", target_bir_lowering=False, num_devices=1)
    aps = [nc.dram_tensor(k, v.shape, F32, kind="ExternalInput").ap() for k, v in arrays.items()]
    out = nc.dram_tensor("out", (B, T, D), F32, kind="ExternalOutput").ap()
    x2_rows = nc.dram_tensor("x2_rows", (ROWS, D), F32, kind="Internal").ap()
    acc_rows = nc.dram_tensor("acc_rows", (ROWS, D), F32, kind="Internal").ap()
    decoder_layer(nc, *aps, out, x2_rows, acc_rows)
    return run(nc, [arrays], core_ids=[0]).results[0]["out"]
```

```python
import concourse.bass as bass
from concourse import mybir
from contextlib import ExitStack

F32 = mybir.dt.float32
F16 = mybir.dt.float16
BF16 = mybir.dt.bfloat16
I32 = mybir.dt.int32
ACT = mybir.ActivationFunctionType
ALU = mybir.AluOpType
AX = mybir.AxisListType

P = 128
B, T, D = 8, 256, 256
TT = T // P
DC = D // P
H = 16
HD = D // H
RD = 32
QK = 64
KVR, QR = 64, 128
E, F = 8, 1024
EW = 2 * D * F // P
PIECE = F
PIECES = EW // PIECE
EARLY = 5
FIRST, PER_ROW = 1, 3
FC = F // P
NT = B * TT
TOK = B * T
N_TILES = (2 * TOK + E * (P - 1)) // P
ROWS = TOK + P
W_SCALE = 64.0
RMS_EPS, LN_EPS = 1e-6, 1e-5
SELF_SCALE = float(HD + RD) ** -0.5
CROSS_SCALE = float(HD) ** -0.5

C_COS = 0
C_SIN = C_COS + T
C_ID = C_SIN + T
C_MASK = C_ID + P
C_MASKT = C_MASK + P
C_UP = C_MASKT + P
C_REV = C_UP + P
C_CNT = C_REV + E
C_LT = C_CNT + NT
C_TILE = C_LT + E * E
C_LANE = C_TILE + N_TILES
C_TOK1 = C_LANE + P
C_DUMMY = C_TOK1 + NT
C_ALL = C_DUMMY + 1


HEADS_QK = [("qk", hp) for hp in range(H // 2)]
SLOT1 = [("x_transpose", 0), ("self_norm", 0), ("latents", 0), ("self_back", 0), ("kv_transpose", 0), ("values", 0)] \
    + HEADS_QK[:2] + [("self_out", 0)] + HEADS_QK[2:]
SLOT2 = [("context", 0)]
for _h in range(H):
    SLOT2 += [("cross_exp", _h), ("self_max", _h)]
    if _h % 4 == 1 and _h > 4:
        SLOT2 += [("cross_pv", _h // 4 - 1)]
SLOT2 += [("self_maxT", 0), ("cross_pv", 3)]
SLOT3 = []
_AFTER = {0: [], 1: [("values_in", 0), ("stack_transpose", 0), ("cross_norm", 0)], 2: [("stack_transpose", 1)],
          3: [("cross_back", 0)], 4: [("stack_transpose", 2)], 5: [("self_pv", 0), ("cross_out", 0)],
          6: [("stack_transpose", 3)], 9: [("self_pv", 1), ("x2_transpose", 0)], 11: [("logits", 0)], 13: [("self_pv", 2)]}
for _h in range(H):
    SLOT3 += [("self_exp", _h)] + _AFTER.get(_h, [])
    if _h >= 7:
        SLOT3 += [("cross_max", _k) for _k in range(2 * (_h - 7), min(2 * (_h - 7) + 2, H))]
SLOT3 += [("cross_maxT", 0), ("self_pv", 3)]
STEP = SLOT1 + SLOT2 + SLOT3
BEHIND = {"self_norm": 1, "self_back": 1, "self_out": 1, "context": 1, "stack_transpose": 1, "cross_max": 1, "cross_maxT": 1,
          "values_in": 1, "cross_exp": 2, "cross_pv": 2, "cross_norm": 2, "cross_back": 2, "cross_out": 2,
          "x2_transpose": 2, "logits": 2}


def units(i0):
    return [(u, k) for u, k in STEP if i0 is None or 0 <= i0 - BEHIND.get(u, 0) < B]


def decoder_layer(nc, x, ctx_in, w_kv, g_kv, w_q, wq_heads, wk_content, wk_rope, wv, wo, wx,
                  xb, wg, bg, w_exp, b1t, b2, table, out, x2_rows, acc_rows):
    stack = ExitStack()
    with stack:
        def sb(name, shape, dt=F32):
            return stack.enter_context(nc.sbuf_tensor(name, shape, dt))

        def sem(name):
            return stack.enter_context(nc.semaphore(name))

        tab = sb("tab", [P, C_ALL])
        ident = tab[:, C_ID:C_ID + P]
        ident_b = sb("ident_b", [P, P], BF16)
        ident_h = sb("ident_h", [P, P], F16)
        mask_b = sb("mask_b", [P, P], BF16)
        maskt_b = sb("maskt_b", [P, P], BF16)
        up_b = sb("up_b", [P, P], BF16)
        ones_b = sb("ones_b", [P, P], BF16)
        W_KV, W_Q, W_QH = 0, DC * KVR, DC * (KVR + QR)
        W_KR = W_QH + H * QK
        W_KC = W_KR + DC * H * QK
        W_V = W_KC + H * QK
        W_ALL = W_V + D
        wph = sb("wph", [P, W_ALL], F16)
        wpl = sb("wpl", [P, W_ALL], F16)
        wo_sb = sb("wo_sb", [P, DC, D])
        wx_sb = sb("wx_sb", [P, DC, D])
        wg_sb = sb("wg_sb", [P, DC, E])
        g_sb = sb("g_sb", [KVR, 1])
        xb_sb = sb("xb_sb", [P, D])
        bg_sb = sb("bg_sb", [P, E])
        b1_sb = sb("b1_sb", [P, E * FC])
        whi = sb("whi", [P, E * EW], F16)
        wlo = sb("wlo", [P, E * EW], F16)
        hi_tail = whi[:, EARLY * EW:E * EW].bitcast(F32)
        lo_tail = wlo[:, EARLY * EW:E * EW].bitcast(F32)

        x_sb = sb("x_sb", [P, TT, D])
        x_res = sb("x_res", [P, TT, D])
        xT = sb("xT", [P, DC * T])
        xTh = xT[:, 0:T].bitcast(F16).rearrange("p (c t) -> p c t", c=DC)
        xTl = xT[:, T:2 * T].bitcast(F16).rearrange("p (c t) -> p c t", c=DC)
        x2T = xT[:, :].rearrange("p (c t) -> p c t", c=DC)
        qch, qcl = sb("qch", [P, T], F16), sb("qcl", [P, T], F16)
        kvn = sb("kvn", [P, TT, KVR])
        kvh, kvl = sb("kvh", [KVR, T], F16), sb("kvl", [KVR, T], F16)
        v_sb = lo_tail[:, 2048:3072].rearrange("p (t h d) -> p t h d", t=TT, h=H)
        sq = sb("sq", [P, KVR])
        ss = sb("ss", [P, TT])
        rs = sb("rs", [P, TT])
        swap = [sb(f"swap{i}", [P, 2, T]) for i in range(2)]
        qk = hi_tail[:, 0:4096].rearrange("p (g a t) -> p g a t", g=H // 2, a=2)
        qk_b = lo_tail[:, 0:2048].bitcast(BF16).rearrange("p (g a t) -> p g a t", g=H // 2, a=2)
        mx = sb("mx", [P, H, 3])
        mx2 = sb("mx2", [P, H])
        ctx_raw = sb("ctx_raw", [P, TT, D])
        c_sb = lo_tail[:, 3072:4096].rearrange("p (t h d) -> p t h d", t=TT, h=H)
        x1s = lo_tail[:, 4096:5120].bitcast(F16).rearrange("p (t h d) -> p t h d", t=TT, h=H)
        cs = lo_tail[:, 5120:6144].bitcast(F16).rearrange("p (t h d) -> p t h d", t=TT, h=H)
        xc = hi_tail[:, 4096:6144].bitcast(F16).rearrange("p (g a t) -> p g a t", g=H // 2, a=2)
        mxc = sb("mxc", [P, H, 2])
        negm = [sb(f"negm{i}", [P, TT, P], BF16) for i in range(2)]
        mT = [sb(f"mT{i}", [P, T], BF16) for i in range(2)]
        probs = sb("probs", [P, 4, 2 * T])
        oP = sb("oP", [P, 4, T])
        rec = sb("rec", [P, TT, H])
        o_tok = sb("o_tok", [P, TT, D])
        oT = sb("oT", [P, DC, T])
        stats = sb("stats", [P, TT, 6])
        mv = sb("mv", [P, TT, 2])
        rstd = sb("rstd", [P, TT])
        spare = sb("spare", [P, 1])
        minus_half = sb("minus_half", [P, 4])
        x1 = sb("x1", [P, TT, D])
        x1_prev = sb("x1_prev", [P, TT, D])
        x2 = sb("x2", [P, TT, D])
        logits = sb("logits", [P, NT, E])
        wstage0 = sb("wstage0", [P, PIECE])

        rt = [(oP[:, i // 2, (i % 2) * P:(i % 2 + 1) * P]).rearrange("p (t e) -> p t e", e=E) for i in range(8)]
        oh_lane = [x1[:, i, 0:P] for i in range(2)]
        oh_tile = [x1[:, i, P:P + 2 * N_TILES] for i in range(2)]
        over_rank = probs[:, :, :].rearrange("p a n -> p (a n)").rearrange("p (m k) -> p m k", k=NT)
        flat = swap[0][:, :, :].rearrange("p a t -> p (a t)")
        ttmp = flat[:, 0:N_TILES * E].rearrange("p (i e) -> p i e", e=E)
        ltmp = flat[:, 320:320 + E * NT]
        rs1 = [sb(f"rs1_{i}", [P, NT]) for i in range(8)]
        m_b = sb("m_b", [P, NT, E], BF16)
        ex = [sb(f"ex{i}", [P, E]) for i in range(4)]
        slot_w = sb("slot_w", [P, N_TILES])
        slot_t = [sb(f"slot_t{i}", [P, N_TILES]) for i in range(3)]
        slot_row = sb("slot_row", [P, N_TILES], I32)
        tile_e = sb("tile_e", [P, N_TILES], I32)
        wstage = [wstage0[:, :], wpl[:, 0:2 * PIECE].bitcast(F32)]

        b2_sb = wph[:, 0:2 * E * D].bitcast(F32)
        xg = [x_sb[:, i, :] for i in range(2)]
        idx_g = [sb(f"idx_g{i}", [P, 1], I32) for i in range(2)]
        idx_s = [sb(f"idx_s{i}", [P, 1], I32) for i in range(2)]
        xparts = xT[:, :].bitcast(F16).rearrange("p (u k c t) -> p u k c t", u=2, k=2, c=DC)
        xh = [xparts[:, i, 0, :, :] for i in range(2)]
        xl = [xparts[:, i, 1, :, :] for i in range(2)]
        act = probs[:, :, :].rearrange("p a n -> p (a n)").rearrange("p (u f t) -> p u f t", u=2, f=FC)
        ah = wpl[:, 0:2 * FC * P].rearrange("p (u f t) -> p u f t", u=2, f=FC)
        al = wpl[:, 2 * FC * P:4 * FC * P].rearrange("p (u f t) -> p u f t", u=2, f=FC)
        yb = [x_res[:, i, :] for i in range(2)]
        fin = whi[:, 0:NT * D * 2].bitcast(F32).rearrange("p (t d) -> p t d", d=D)
        fst = sb("fst", [P, NT, 6])
        fmv = sb("fmv", [P, NT, 2])
        frs = sb("frs", [P, NT])

        W_RAW = [(W_KV, W_KR), (W_KR, W_KC), (W_KC, W_ALL)]
        wraw = hi_tail[:, 0:W_ALL]

        bank = [stack.enter_context(nc.psum_tensor(f"bank{i}", [P, 512], F32)) for i in range(8)]
        ps_s, ps_t, ps_o, ps_m = bank[0:2], bank[2:4], bank[4:6], bank[6:8]
        ps_sh = [ps_s[i][:, :].bitcast(F16) for i in range(2)]

        c_ld, r_ld = sem("consts_loaded"), sem("raw_weights_loaded")
        c_ms, c_bf = sem("pads_set"), sem("bf16_consts")
        pw_hi, pw_lo = sem("projections_high"), sem("projections_low")
        x_ld, xr_ld, ctx_ld = sem("x_loaded"), sem("x_residual_loaded"), sem("ctx_loaded")
        w_ld = [sem(f"wstage_loaded{i}") for i in range(2)]
        w_hi, w_lo = sem("w_high_done"), sem("w_low_done")
        pe_xT, a_xT, v_xT = sem("pe_x_transposed"), sem("xT_high"), sem("xT_low")
        pe_qkv, a_qc, v_qc = sem("pe_latents"), sem("qc_high"), sem("qc_low")
        a_ss, v_kvn = sem("kv_squares"), sem("kv_normed")
        pe_kvT, v_kvh, v_kvT = sem("pe_kv_transposed"), sem("kv_high"), sem("kv_low")
        pe_v, a_v = sem("pe_values"), sem("values_ready")
        s_full, s_used = sem("score_bank_filled"), sem("score_bank_used")
        p_sin, v_qk, a_qkb = sem("qk_sin_done"), sem("qk_ready"), sem("qk_bf16_ready")
        v_sw = sem("qk_swapped")
        v_nm = [sem(f"neg_max_ready{i}") for i in range(2)]
        pe_mT = [sem(f"pe_max_transposed{i}") for i in range(2)]
        v_mT = [sem(f"maxT_ready{i}") for i in range(2)]
        pe_t, a_p = sem("pe_scoresT"), sem("probs_ready")
        pe_pv, a_o = sem("pe_pv"), sem("pv_copied")
        pe_n1 = [sem(f"pe_out_by_token{i}") for i in range(2)]
        v_n1 = [sem(f"out_normed{i}") for i in range(2)]
        pe_n2 = [sem(f"pe_out_transposed{i}") for i in range(2)]
        v_n2 = [sem(f"outT_ready{i}") for i in range(2)]
        pe_w = [sem(f"pe_out_projected{i}") for i in range(2)]
        v_r = [sem(f"residual_added{i}") for i in range(2)]
        v_x1, a_x1h, p_x1l, p_prev = sem("x1_ready"), sem("x1_high"), sem("x1_low"), sem("x1_kept")
        a_ch, p_cl, a_cv = sem("ctx_high"), sem("ctx_low"), sem("ctx_values")
        pe_xc, a_xc = sem("pe_stacks_transposed"), sem("stacks_ready")
        v_x2, x2_st = sem("x2_ready"), sem("x2_stored")
        pe_x2T, a_x2T = sem("pe_x2_transposed"), sem("x2T_ready")
        pe_lg, v_lg = sem("pe_logits"), sem("logits_ready")
        v_var, p_rs = sem("variance_ready"), sem("inverse_root_ready")
        v_ch = sem("vector_chain")
        b2_ld = sem("b2_loaded")
        v_rl, a_re, v_m = sem("shifted_logits"), sem("gate_exp"), sem("choices_ready")
        pe_rank, v_oh, pe_slot = sem("pe_ranks"), sem("onehots_ready"), sem("pe_slots")
        v_te, v_rows = sem("tile_experts_ready"), sem("slot_rows_ready")
        p_ix0, p_ix, p_ixs = sem("first_gather_index_ready"), sem("gather_index_ready"), sem("scatter_index_ready")
        g_ld = [sem(f"slots_gathered{i}") for i in range(2)]
        pe_ft, a_xh, v_xl = sem("pe_slots_transposed"), sem("slots_high"), sem("slots_low")
        pe_h, a_g = sem("pe_hidden"), sem("hidden_act")
        v_ah, v_al = sem("hidden_high"), sem("hidden_low")
        pe_y, v_yt, v_y = sem("pe_expert_out"), sem("expert_biased"), sem("expert_weighted")
        sc_st = sem("scatter_added")
        f_ld = [sem(f"sums_loaded{i}") for i in range(4)]
        v_f, f_st = sem("final_ready"), sem("out_stored")

        def raw(at, n, rows=P):
            return wraw[0:rows, at:at + n]

        raw_loads = [
            (raw(W_KV, DC * KVR).rearrange("p (c n) -> p c n", c=DC), w_kv.rearrange("(c p) n -> p c n", p=P)),
            (raw(W_Q, DC * QR).rearrange("p (c n) -> p c n", c=DC), w_q.rearrange("(c p) n -> p c n", p=P)),
            (raw(W_QH, H * QK), wq_heads[:, :]),
            (raw(W_KR, DC * H * QK).rearrange("p (c n) -> p c n", c=DC), wk_rope.rearrange("(c p) n -> p c n", p=P)),
            (raw(W_KC, H * QK, KVR), wk_content[:, :]),
            (raw(W_V, D, KVR), wv[:, :])]
        loads = [(tab[:, :], table[:, :]),
                 (wo_sb[:, :, :], wo.rearrange("(c p) n -> p c n", p=P)),
                 (wx_sb[:, :, :], wx.rearrange("(c p) n -> p c n", p=P)),
                 (wg_sb[:, :, :], wg.rearrange("(c p) n -> p c n", p=P)),
                 (g_sb[:, :], g_kv.rearrange("(r a) -> r a", a=1)),
                 (xb_sb[:, :], xb.partition_broadcast(P)), (bg_sb[:, :], bg.partition_broadcast(P)),
                 (b1_sb[:, :], b1t[:, :])]
        N_LOADS, N_RAW = len(loads), len(raw_loads)
        LATE = (E - EARLY) * PIECES

        x_rows = x.rearrange("b (t p) d -> p (b t) d", p=P)
        c_rows = ctx_in.rearrange("b (t p) d -> p (b t) d", p=P)
        w_pieces = w_exp.rearrange("n p f -> p n f")
        x2_st_rows = x2_rows[0:TOK, :].rearrange("(t p) d -> p t d", p=P)
        acc_st_rows = acc_rows[0:TOK, :].rearrange("(t p) d -> p t d", p=P)
        out_rows = out.rearrange("b (t p) d -> p (b t) d", p=P)

        LOOP0, LOOP1 = 2, B

        def score_base(i):
            return 0 if isinstance(i, int) and i == 0 else i * 40 - 16

        def used_base(i):
            return 0 if isinstance(i, int) and i == 0 else i * 32 - 16

        def cross_used_at(i):
            return used_base(i) + (H if not isinstance(i, int) or i < B else 0)

        def cross_max_at(i, h):
            return score_base(i) + (24 if not isinstance(i, int) or i < B else 0) + h

        def exp_base(i):
            if isinstance(i, int):
                return H * (min(i, B) + max(i - 2, 0))
            return i * 32 - 32

        def self_exp_at(i, h):
            return exp_base(i) + (H if not isinstance(i, int) or i >= 2 else 0) + h

        def pieces_at(i):
            if isinstance(i, int):
                return (i * FIRST, FIRST) if i < 2 else (2 * FIRST + (i - 2) * PER_ROW, PER_ROW if i < B else 0)
            return i * PER_ROW + (2 * FIRST - 2 * PER_ROW), PER_ROW

        def each_step(engine, step):
            for i in range(LOOP0):
                step(i, i)
            with engine.Fori(LOOP0, LOOP1) as i:
                step(i, None)
            for i in range(LOOP1, LOOP1 + 2):
                step(i, i)

        block = stack.enter_context(nc.Block())

        @block.sync
        def _(sp):
            sp.dma_start(x_sb[:, :, :], x_rows[:, 0:TT, :]).then_inc(x_ld, 16)
            sp.dma_start(loads[0][0], loads[0][1]).then_inc(c_ld, 16)
            for dst, src in raw_loads:
                sp.dma_start(dst, src).then_inc(r_ld, 16)
            for dst, src in loads[1:]:
                sp.dma_start(dst, src).then_inc(c_ld, 16)
            sp.wait_ge(c_ms, 1)
            sp.dma_start(x2_rows[TOK:ROWS, :], oP[:, 0, :]).then_inc(x2_st, 16)
            sp.dma_start(acc_rows[TOK:ROWS, :], oP[:, 0, :]).then_inc(x2_st, 16)
            sp.wait_ge(x2_st, 32)

            def step(i, i0):
                if i0 is None or 1 <= i0 < B:
                    sp.wait_ge(pe_xT, i)
                    sp.dma_start(x_sb[:, :, :], x_rows[:, bass.ds(i * TT, TT), :]).then_inc(x_ld, 16)
                before, n = pieces_at(i)
                for j in range(n):
                    sp.wait_ge(w_lo, before + j + 1)
                    sp.dma_start(wstage[0].unsqueeze(1), w_pieces[:, bass.ds(before + j, 1), :]).then_inc(w_ld[0], 16)
                if i0 is None or i0 < B:
                    sp.wait_ge(v_r[0], i + 1)
                    sp.dma_start(x_res[:, :, :], x_rows[:, bass.ds(i * TT, TT), :]).then_inc(xr_ld, 16)
                    sp.wait_ge(a_cv, i + 1)
                    sp.wait_ge(p_cl, i + 1)
                    sp.dma_start(ctx_raw[:, :, :], c_rows[:, bass.ds(i * TT, TT), :]).then_inc(ctx_ld, 16)

            each_step(sp, step)
            sp.wait_ge(x2_st, 32 * (B + 1))
            sp.dma_start(b2_sb, b2.rearrange("e d -> (e d)").partition_broadcast(P)).then_inc(b2_ld, 16)
            for j in range(LATE):
                sp.wait_ge(w_lo, EARLY * PIECES + 1 + max(j - 1, 0))
                sp.dma_start(wstage[j % 2].unsqueeze(1), w_pieces[:, EARLY * PIECES + j:EARLY * PIECES + j + 1, :]).then_inc(w_ld[j % 2], 16)
            sp.wait_ge(sc_st, 16 * N_TILES)
            for k in range(4):
                sp.dma_start(fin[:, 4 * k:4 * k + 4, :], acc_st_rows[:, 4 * k:4 * k + 4, :]).then_inc(f_ld[k], 16)
            for k in range(4):
                sp.wait_ge(v_f, k + 1)
                sp.dma_start(out_rows[:, 4 * k:4 * k + 4, :], fin[:, 4 * k:4 * k + 4, :]).then_inc(f_st, 16)
            sp.wait_ge(f_st, 64)

        @block.gpsimd
        def _(pool):
            nc.gpsimd.memset(minus_half[:, :], -0.5)
            nc.gpsimd.memset(oP[:, 0, :], 0.0)
            nc.gpsimd.memset(x1s[:, :, :, 3 * HD:], 0.0)
            nc.gpsimd.memset(cs[:, :, :, 3 * HD:], 0.0)
            nc.gpsimd.memset(v_sb[:, :, :, :], 1.0)
            nc.gpsimd.memset(c_sb[:, :, :, :], 1.0).then_inc(c_ms, 1)
            nc.gpsimd.memset(rec[:, 0, 0:1], 0.0).then_inc(p_cl, 1)
            pool.wait_ge(c_ld, 16 * N_LOADS)
            roots = {"n": 0, "base": 0}

            def inverse_root(value):
                roots["n"] += 1
                pool.wait_ge(v_var, roots["base"] + roots["n"])
                nc.gpsimd.tensor_tensor(value, value, minus_half[:, 0:value.shape[1]], ALU.pow).then_inc(p_rs, 1)

            def step(i, i0):
                if i0 is None:
                    start, roots["base"], roots["n"] = roots["n"], i * 3 + (roots["n"] - 3 * LOOP0), 0
                for u, k in units(i0):
                    b = i - BEHIND.get(u, 0)
                    if u == "latents":
                        inverse_root(rs[:, :])
                    elif u == "qk":
                        pool.wait_ge(v_sw, b * (H // 2) + k + 1)
                        nc.gpsimd.tensor_tensor(
                            swap[k % 2][:, :, :], swap[k % 2][:, :, :],
                            tab[:, C_SIN:C_SIN + T].unsqueeze(1).broadcast_to([P, 2, T]), ALU.mult).then_inc(p_sin, 1)
                    elif u == "self_out":
                        inverse_root(rstd[:, :])
                        pool.wait_ge(v_x1, b + 1)
                        pool.wait_ge(a_x1h, b + 1)
                        nc.gpsimd.tensor_tensor(
                            x1s[:, :, :, HD:2 * HD].rearrange("p t h d -> p (t h) d"),
                            x1[:, :, :].rearrange("p t (h d) -> p (t h) d", d=HD),
                            x1s[:, :, :, 0:HD].rearrange("p t h d -> p (t h) d"), ALU.subtract).then_inc(p_x1l, 1)
                    elif u == "context":
                        pool.wait_ge(a_ch, b + 1)
                        nc.gpsimd.tensor_tensor(
                            cs[:, :, :, 2 * HD:3 * HD].rearrange("p t h d -> p (t h) d"),
                            ctx_raw[:, :, :].rearrange("p t (h d) -> p (t h) d", d=HD),
                            cs[:, :, :, 0:HD].rearrange("p t h d -> p (t h) d"), ALU.subtract).then_inc(p_cl, 1)
                    elif u == "cross_out":
                        inverse_root(rstd[:, :])
                    elif u == "cross_maxT":
                        if i0 is None or i0 >= 2:
                            pool.wait_ge(v_r[1], i - 1)
                        nc.gpsimd.tensor_tensor(x1_prev[:, :, :], x1[:, :, :], xb_sb[:, :].unsqueeze(1).broadcast_to([P, TT, D]),
                                                ALU.add).then_inc(p_prev, 1)
                if i0 is None:
                    assert roots["n"] == 3
                    roots["n"], roots["base"] = start + 3 * (LOOP1 - LOOP0), 0

            each_step(pool, step)
            pool.wait_ge(v_rows, 1)

            def gather(n, u, gate):
                if gate is not None:
                    pool.wait_ge(pe_ft, gate)
                first = gate is None
                nc.gpsimd.tensor_copy(idx_g[u][:, :], slot_row[:, bass.ds(n, 1)]).then_inc(p_ix0 if first else p_ix, 1)
                pool.wait_ge(x2_st, 32 * (B + 1))
                pool.wait_ge(p_ix0 if first else p_ix, n + 1 if first else gate)
                nc.gpsimd.indirect_dma_start(
                    out=xg[u], out_offset=None, in_=x2_rows[:, :],
                    in_offset=bass.IndirectOffsetOnAxis(ap=idx_g[u][:, 0:1], axis=0)).then_inc(g_ld[u], 16)

            def scatter(n, u, after):
                pool.wait_ge(v_y, n + 1)
                if after is not None:
                    pool.wait_ge(sc_st, after)
                nc.gpsimd.tensor_copy(idx_s[u][:, :], slot_row[:, bass.ds(n, 1)]).then_inc(p_ixs, 1)
                pool.wait_ge(x2_st, 32 * (B + 1))
                pool.wait_ge(p_ixs, n + 1)
                nc.gpsimd.indirect_dma_start(
                    out=acc_rows[:, :], out_offset=bass.IndirectOffsetOnAxis(ap=idx_s[u][:, 0:1], axis=0),
                    in_=yb[u], in_offset=None, compute_op=ALU.add).then_inc(sc_st, 16)

            gather(0, 0, None)
            gather(1, 1, None)
            gather(2, 0, 1)
            gather(3, 1, 2)
            scatter(0, 0, None)
            with pool.Fori(0, (N_TILES - 5) // 2) as j:
                for u in range(2):
                    gather(j * 2 + 4 + u, u, j * 2 + 3 + u)
                    scatter(j * 2 + 1 + u, (1 + u) % 2, (j * 2 + 1 + u) * 16)
            gather(N_TILES - 1, 0, N_TILES - 2)
            for n in range(N_TILES - 4, N_TILES):
                scatter(n, n % 2, 16 * n)
            pool.wait_ge(sc_st, 16 * N_TILES)
            for k in range(4):
                inverse_root(frs[:, 4 * k:4 * k + 4])

        @block.scalar
        def _(act_e):
            act_e.wait_ge(r_ld, 16 * N_RAW)
            for at, end in W_RAW:
                rows = KVR if at == W_KC else P
                nc.scalar.activation(wph[0:rows, at:end], wraw[0:rows, at:end], ACT.Copy, scale=W_SCALE).then_inc(pw_hi, 1)
            act_e.wait_ge(c_ld, 16 * N_LOADS)
            act_e.wait_ge(c_ms, 1)
            act_e.wait_ge(pw_lo, 3)

            def split_high(stage, loaded, p):
                act_e.wait_ge(w_ld[stage], loaded)
                nc.scalar.activation(whi[:, bass.ds(p * PIECE, PIECE)], wstage[stage], ACT.Copy, scale=W_SCALE).then_inc(w_hi, 1)

            def by_head(a):
                return a.rearrange("p t (h d) -> p (t h) d", d=HD)

            def part(a, n):
                return a[:, :, :, n * HD:(n + 1) * HD].rearrange("p t h d -> p (t h) d")

            def step(i, i0):
                has = {u for u, _ in units(i0)}
                before, n = pieces_at(i)
                for u, k in units(i0):
                    b = i - BEHIND.get(u, 0)
                    if u == "x_transpose":
                        act_e.wait_ge(pe_xT, b + 1)
                        nc.scalar.activation(xTh.rearrange("p c t -> p (c t)"), ps_m[0][:, :], ACT.Copy).then_inc(a_xT, 1)
                    elif u == "latents":
                        act_e.wait_ge(pe_qkv, b + 1)
                        for t in range(TT):
                            if t:
                                act_e.wait_ge(a_ss, b * TT + t)
                            nc.scalar.activation(sq[:, :], ps_m[0][:, t * KVR:(t + 1) * KVR], ACT.Square, scale=1.0 / W_SCALE,
                                                 accum_out=ss[:, t:t + 1]).then_inc(a_ss, 1)
                        nc.scalar.activation(qch[:, :], ps_m[1][:, 0:T], ACT.Copy, scale=1.0 / W_SCALE).then_inc(a_qc, 1)
                    elif u == "values":
                        act_e.wait_ge(pe_v, b + 1)
                        nc.scalar.activation(part(v_sb, 0), ps_m[1][:, :].rearrange("p (s d) -> p s d", d=HD), ACT.Copy,
                                             scale=1.0 / W_SCALE).then_inc(a_v, 1)
                    elif u == "qk":
                        act_e.wait_ge(v_qk, b * (H // 2) + k + 1)
                        nc.scalar.activation(qk_b[:, k, :, :], qk[:, k, :, :], ACT.Copy).then_inc(a_qkb, 1)
                    elif u == "self_out":
                        act_e.wait_ge(v_x1, b + 1)
                        nc.scalar.activation(part(x1s, 2), by_head(x1[:, :, :]), ACT.Copy)
                        nc.scalar.activation(part(x1s, 0), by_head(x1[:, :, :]), ACT.Copy).then_inc(a_x1h, 1)
                    elif u == "context":
                        act_e.wait_ge(ctx_ld, b * 16 + 16)
                        nc.scalar.activation(part(cs, 1), by_head(ctx_raw[:, :, :]), ACT.Copy)
                        nc.scalar.activation(part(cs, 0), by_head(ctx_raw[:, :, :]), ACT.Copy).then_inc(a_ch, 1)
                    elif u == "values_in":
                        if i0 is None or i0 >= 2:
                            act_e.wait_ge(pe_pv, exp_base(i) // 4 + 4 if isinstance(i, int) else i * 8 - 4)
                        nc.scalar.activation(part(c_sb, 0), by_head(ctx_raw[:, :, :]), ACT.Copy).then_inc(a_cv, 1)
                    elif u in ("cross_exp", "self_exp"):
                        cross = u == "cross_exp"
                        at = exp_base(i) + k if cross else self_exp_at(i, k)
                        act_e.wait_ge(pe_t, at + 1)
                        if k % 4 == 0 and not (i0 == 0 and k == 0):
                            group = i * 8 - 8 + (0 if cross else 4) + k // 4 if i0 is None else at // 4
                            act_e.wait_ge(pe_pv, group)
                        cols = 2 * T if cross else 3 * P
                        nc.scalar.activation(probs[:, k % 4, 0:cols], ps_t[k % 2][:, 0:cols], ACT.Exp,
                                             scale=CROSS_SCALE if cross else SELF_SCALE).then_inc(a_p, 1)
                    elif u == "self_max" and k % 4 == 2 and k // 4 < n:
                        split_high(0, (before + k // 4) * 16 + 16, before + k // 4)
                    elif u in ("cross_pv", "self_pv"):
                        cross = u == "cross_pv"
                        group = (i * 8 - 8 + (0 if cross else 4) if i0 is None else (exp_base(i) if cross else self_exp_at(i, 0)) // 4) + k
                        act_e.wait_ge(pe_pv, group + 1)
                        if k == 0 and cross and "self_norm" in has:
                            act_e.wait_ge(pe_n1[0], i)
                        if k == 0 and not cross and "cross_norm" in has:
                            act_e.wait_ge(pe_n1[1], i - 1)
                        if k == 0 and not cross and i0 == 1:
                            act_e.wait_ge(pe_n1[0], 1)
                        nc.scalar.activation(oP[:, k, :], ps_o[k % 2][:, 0:T], ACT.Copy).then_inc(a_o, 1)
                    elif u == "stack_transpose":
                        act_e.wait_ge(pe_xc, b * 4 + k + 1)
                        nc.scalar.activation(xc[:, 2 * k:2 * k + 2, :, :].rearrange("p g a t -> p (g a t)"), ps_sh[k % 2],
                                             ACT.Copy).then_inc(a_xc, 1)
                    elif u == "x2_transpose":
                        act_e.wait_ge(pe_x2T, b + 1)
                        nc.scalar.activation(xT[:, :], ps_m[0][:, :], ACT.Copy).then_inc(a_x2T, 1)
                        act_e.wait_ge(v_x2, b + 1)
                        rows = bass.ds(b * TT, TT)
                        act_e.dma_start(x2_st_rows[:, rows, :], x2[:, :, :]).then_inc(x2_st, 16)
                        act_e.dma_start(acc_st_rows[:, rows, :], x2[:, :, :]).then_inc(x2_st, 16)

            each_step(act_e, step)

            act_e.wait_ge(v_rl, 1)
            nc.scalar.activation(rt[1], rt[0], ACT.Exp).then_inc(a_re, 1)
            for j in range(LATE):
                split_high(j % 2, ((EARLY * PIECES if j % 2 == 0 else 0) + j // 2 + 1) * 16, EARLY * PIECES + j)
            act_e.wait_ge(v_te, 1)

            def slots_high(n, u):
                act_e.wait_ge(pe_ft, n + 1)
                nc.scalar.activation(xh[u].rearrange("p c t -> p (c t)"), bank[u][:, 0:D], ACT.Copy).then_inc(a_xh, 1)

            def hidden(n, u, e, half):
                act_e.wait_ge(pe_h, n * 2 + half + 1)
                for f in range(4 * half, 4 * half + 4):
                    last = nc.scalar.activation(
                        act[:, u, f, :], bank[2 + 2 * u + half][:, (f % 4) * P:(f % 4 + 1) * P], ACT.Gelu,
                        bias=b1_sb[:, bass.ds(e * FC + f, 1)], scale=1.0 / W_SCALE)
                last.then_inc(a_g, 1)

            def tile(n, u, split, following=True):
                e = act_e.value_load(tile_e[0:1, bass.ds(n, 1)], min_val=0, max_val=E - 1)
                if split is not None:
                    act_e.wait_ge(v_al, split)
                hidden(n, u, e, 0)
                if following:
                    slots_high(n + 1, 1 - u)
                hidden(n, u, e, 1)

            slots_high(0, 0)
            slots_high(1, 1)
            tile(0, 0, None, False)
            tile(1, 1, None)
            tile(2, 0, 2)
            with act_e.Fori(0, (N_TILES - 5) // 2) as j:
                for u in range(2):
                    tile(j * 2 + 3 + u, (1 + u) % 2, j * 4 + 2 * u + 4)
            tile(N_TILES - 2, 1, 2 * (N_TILES - 3))
            tile(N_TILES - 1, 0, 2 * (N_TILES - 2), False)

        @block.vector
        def _(dve):
            chain = {"n": 0, "base": 0}
            roots = {"n": 0, "base": 0}

            def link(ins, plain=False):
                chain["n"] += 1
                ins.then_inc(v_ch, 1)
                dve.wait_ge(v_ch, chain["base"] + chain["n"])
                if plain:
                    nc.vector.memset(spare[:, :], 0.0)

            def inverse_root(ins):
                roots["n"] += 1
                ins.then_inc(v_var, 1)
                dve.wait_ge(p_rs, roots["base"] + roots["n"])

            nc.vector.memset(ones_b[:, :], 1.0)
            for m in negm:
                nc.vector.memset(m[:, :, :], 0.0)
            nc.vector.memset(rs[:, :], 0.0).then_inc(v_r[0], 1)
            nc.vector.memset(rstd[:, :], 0.0).then_inc(v_lg, 1)
            nc.vector.memset(mx2[:, :], 0.0).then_inc(w_lo, 1)
            link(nc.vector.memset(mx[:, :, :], 0.0))
            nc.vector.memset(mxc[:, :, :], 0.0).then_inc(a_cv, 1)
            dve.wait_ge(c_ld, 16 * N_LOADS)
            nc.vector.tensor_copy(ident_b[:, :], ident)
            nc.vector.tensor_copy(ident_h[:, :], ident)
            nc.vector.tensor_copy(mask_b[:, :], tab[:, C_MASK:C_MASK + P])
            nc.vector.tensor_copy(maskt_b[:, :], tab[:, C_MASKT:C_MASKT + P])
            nc.vector.tensor_copy(up_b[:, :], tab[:, C_UP:C_UP + P]).then_inc(c_bf, 1)
            for n, (at, end) in enumerate(W_RAW):
                dve.wait_ge(pw_hi, n + 1)
                rows = KVR if at == W_KC else P
                nc.vector.scalar_tensor_tensor(wpl[0:rows, at:end], wraw[0:rows, at:end], W_SCALE, wph[0:rows, at:end],
                                               ALU.mult, ALU.subtract).then_inc(pw_lo, 1)
            dve.wait_ge(pw_lo, 3)

            def split_low(stage, p):
                dve.wait_ge(w_hi, p + 1)
                at = bass.ds(p * PIECE, PIECE)
                nc.vector.scalar_tensor_tensor(wlo[:, at], wstage[stage], W_SCALE, whi[:, at],
                                               ALU.mult, ALU.subtract).then_inc(w_lo, 1)

            def layer_norm(a, done):
                for t in range(TT):
                    last = nc.vector.bn_stats(stats[:, t, :], a[:, t, :])
                link(last, plain=True)
                for t in range(TT):
                    last = nc.vector.bn_aggr(mv[:, t, :], stats[:, t, :])
                link(last)
                inverse_root(nc.vector.tensor_scalar(rstd[:, :], mv[:, :, 1], LN_EPS, None, ALU.add))
                for t in range(TT):
                    last = nc.vector.tensor_scalar(a[:, t, :], a[:, t, :], mv[:, t, 0:1], rstd[:, t:t + 1],
                                                   ALU.subtract, ALU.mult)
                last.then_inc(done, 1)

            def normalise(a, b, banks):
                dve.wait_ge(pe_n1[a], b + 1)
                for t in range(TT):
                    o = banks[t][:, :].rearrange("p (h d) -> p h d", d=32)
                    last = nc.vector.reciprocal(rec[:, t, :], o[:, :, HD])
                link(last)
                for t in range(TT):
                    o = banks[t][:, :].rearrange("p (h d) -> p h d", d=32)
                    last = nc.vector.tensor_tensor(o_tok[:, t, :].rearrange("p (h d) -> p h d", d=HD), o[:, :, 0:HD],
                                                   rec[:, t, :].unsqueeze(2).broadcast_to([P, H, HD]), ALU.mult)
                last.then_inc(v_n1[a], 1)

            def max_transposed(a, b):
                dve.wait_ge(pe_mT[a], b + 1)
                nc.vector.tensor_copy(mT[a][:, :], ps_m[0][:, 0:T // 2].bitcast(BF16)).then_inc(v_mT[a], 1)

            VCH, VROOT = 7, 3

            def step(i, i0):
                if i0 is None:
                    chain0, roots0 = chain["n"], roots["n"]
                    chain["base"], chain["n"] = i * VCH + (chain0 - VCH * LOOP0), 0
                    roots["base"], roots["n"] = i * VROOT + (roots0 - VROOT * LOOP0), 0
                before, n = pieces_at(i)
                has = {u for u, _ in units(i0)}
                for u, k in units(i0):
                    b = i - BEHIND.get(u, 0)
                    if u == "x_transpose":
                        dve.wait_ge(a_xT, b + 1)
                        nc.vector.tensor_tensor(xTl.rearrange("p c t -> p (c t)"), ps_m[0][:, :],
                                                xTh.rearrange("p c t -> p (c t)"), ALU.subtract).then_inc(v_xT, 1)
                    elif u == "latents":
                        dve.wait_ge(a_ss, b * TT + TT)
                        inverse_root(nc.vector.tensor_scalar(rs[:, :], ss[:, :], 1.0 / KVR, RMS_EPS, ALU.mult, ALU.add))
                        for t in range(TT):
                            last = nc.vector.tensor_scalar(kvn[:, t, :], ps_m[0][:, t * KVR:(t + 1) * KVR], rs[:, t:t + 1],
                                                           1.0 / W_SCALE, ALU.mult, ALU.mult)
                        last.then_inc(v_kvn, 1)
                        dve.wait_ge(a_qc, b + 1)
                        nc.vector.scalar_tensor_tensor(qcl[:, :], ps_m[1][:, 0:T], 1.0 / W_SCALE, qch[:, :], ALU.mult,
                                                       ALU.subtract).then_inc(v_qc, 1)
                    elif u == "kv_transpose":
                        dve.wait_ge(pe_kvT, b + 1)
                        nc.vector.tensor_scalar(kvh[:, :], ps_m[0][0:KVR, 0:T], g_sb[:, 0:1], None, ALU.mult).then_inc(v_kvh, 1)
                        dve.wait_ge(v_kvh, b + 1)
                        nc.vector.scalar_tensor_tensor(kvl[:, :], ps_m[0][0:KVR, 0:T], g_sb[:, 0:1], kvh[:, :], ALU.mult,
                                                       ALU.subtract).then_inc(v_kvT, 1)
                    elif u == "qk":
                        dve.wait_ge(s_full, score_base(i) + k + 1)
                        nc.vector.tensor_tensor(qk[:, k, :, :], ps_s[k % 2][:, :].rearrange("p (a t) -> p a t", a=2),
                                                tab[:, C_COS:C_COS + T].unsqueeze(1).broadcast_to([P, 2, T]), ALU.mult)
                        nc.vector.stream_shuffle(swap[k % 2][:, :, :].rearrange("p a t -> p (a t)"), ps_s[k % 2][:, :],
                                                 [(j + 16) % 32 for j in range(32)]).then_inc(v_sw, 1)
                        dve.wait_ge(p_sin, b * (H // 2) + k + 1)
                        nc.vector.tensor_tensor(qk[:, k, :, :], qk[:, k, :, :], swap[k % 2][:, :, :],
                                                ALU.add).then_inc(v_qk, 1)
                    elif u == "self_max":
                        dve.wait_ge(s_full, score_base(i) + 8 + k + 1)
                        nc.vector.tensor_reduce(mx[:, k, :], ps_s[k % 2][:, 0:3 * P].rearrange("p (a k) -> p a k", a=3),
                                                axis=AX.X, op=ALU.max).then_inc(s_used, 1)
                        if k % 4 == 3 and k // 4 < n:
                            split_low(0, before + k // 4)
                    elif u == "self_maxT":
                        dve.wait_ge(s_used, used_base(i) + H)
                        nm = negm[0][:, :, :].rearrange("p t (a n) -> p t a n", a=2)[:, :, :, 0:H // 2]
                        nc.vector.tensor_scalar(nm[:, 0], mx[:, :, 0].rearrange("p (n a) -> p a n", a=2), -1.0, None, ALU.mult)
                        link(nc.vector.tensor_tensor(mx2[:, :], mx[:, :, 1], mx[:, :, 2], ALU.max))
                        nc.vector.tensor_scalar(nm[:, 1], mx2[:, :].rearrange("p (n a) -> p a n", a=2), -1.0, None,
                                                ALU.mult).then_inc(v_nm[0], 1)
                        max_transposed(0, b)
                    elif u == "self_norm":
                        normalise(0, b, ps_t)
                    elif u == "cross_norm":
                        normalise(1, b, ps_m)
                    elif u in ("self_back", "cross_back"):
                        a = 0 if u == "self_back" else 1
                        dve.wait_ge(pe_n2[a], b + 1)
                        nc.vector.tensor_copy(oT[:, :, :].rearrange("p c t -> p (c t)"),
                                              (ps_t if a == 0 else ps_m)[0][:, :]).then_inc(v_n2[a], 1)
                    elif u == "self_out":
                        dve.wait_ge(pe_w[0], b + 1)
                        dve.wait_ge(xr_ld, b * 16 + 16)
                        if i0 is None or i0 >= 2:
                            dve.wait_ge(p_prev, i - 1)
                        nc.vector.tensor_tensor(x1[:, :, :].rearrange("p t d -> p (t d)"), ps_t[1][:, :],
                                                x_res[:, :, :].rearrange("p t d -> p (t d)"), ALU.add).then_inc(v_r[0], 1)
                        dve.wait_ge(v_r[0], b + 2)
                        layer_norm(x1, v_x1)
                    elif u == "cross_max":
                        dve.wait_ge(s_full, cross_max_at(i, k) + 1)
                        nc.vector.tensor_reduce(mxc[:, k, :], ps_s[k % 2][:, :].rearrange("p (a k) -> p a k", a=2),
                                                axis=AX.X, op=ALU.max).then_inc(s_used, 1)
                    elif u == "cross_maxT":
                        dve.wait_ge(s_used, cross_used_at(i) + H)
                        nm = negm[1][:, :, :].rearrange("p t (a n) -> p t a n", a=2)[:, :, :, 0:H // 2]
                        for t in range(TT):
                            last = nc.vector.tensor_scalar(nm[:, t], mxc[:, :, t].rearrange("p (n a) -> p a n", a=2), -1.0,
                                                           None, ALU.mult)
                        last.then_inc(v_nm[1], 1)
                        max_transposed(1, b)
                    elif u == "cross_out":
                        dve.wait_ge(pe_w[1], b + 1)
                        dve.wait_ge(x2_st, b * 32 + 32)
                        dve.wait_ge(p_prev, b + 1)
                        nc.vector.tensor_tensor(x2[:, :, :].rearrange("p t d -> p (t d)"), ps_m[1][:, :],
                                                x1_prev[:, :, :].rearrange("p t d -> p (t d)"), ALU.add).then_inc(v_r[1], 1)
                        dve.wait_ge(v_r[1], b + 1)
                        layer_norm(x2, v_x2)
                    elif u == "logits":
                        dve.wait_ge(pe_lg, b + 1)
                        nc.vector.tensor_tensor(logits[:, bass.ds(b * TT, TT), :],
                                                ps_m[1][:, 0:TT * E].rearrange("p (t e) -> p t e", e=E),
                                                bg_sb[:, :].unsqueeze(1).broadcast_to([P, TT, E]), ALU.add).then_inc(v_lg, 1)
                if i0 is None:
                    assert (chain["n"], roots["n"]) == (VCH, VROOT), (chain, roots)
                    chain["n"], chain["base"] = chain0 + VCH * (LOOP1 - LOOP0), 0
                    roots["n"], roots["base"] = roots0 + VROOT * (LOOP1 - LOOP0), 0

            each_step(dve, step)

            def over_e(a):
                return a[:, :].unsqueeze(2).broadcast_to([P, NT, E])

            def tab_e(col):
                return tab[:, col:col + E].unsqueeze(1).broadcast_to([P, NT, E])

            dve.wait_ge(v_lg, B + 1)
            top, total, best1, best2 = rs1[0], rs1[1], rs1[2], rs1[3]
            link(nc.vector.tensor_reduce(top[:, :], logits[:, :, :], axis=AX.X, op=ALU.max))
            nc.vector.tensor_tensor(rt[0], logits[:, :, :], over_e(top), ALU.subtract).then_inc(v_rl, 1)
            dve.wait_ge(a_re, 1)
            link(nc.vector.tensor_reduce(total[:, :], rt[1], axis=AX.X, op=ALU.add))
            prob = rt[2]
            link(nc.vector.reciprocal(total[:, :], total[:, :]))
            link(nc.vector.tensor_tensor(prob, rt[1], over_e(total), ALU.mult))

            def choose(src, best, rank, onehot, tmp):
                link(nc.vector.tensor_reduce(best[:, :], src, axis=AX.X, op=ALU.max))
                link(nc.vector.tensor_tensor(tmp, src, over_e(best), ALU.is_equal))
                link(nc.vector.tensor_tensor(tmp, tmp, tab_e(C_REV), ALU.mult))
                link(nc.vector.tensor_reduce(rank[:, :], tmp, axis=AX.X, op=ALU.max))
                link(nc.vector.tensor_tensor(onehot, tmp, over_e(rank), ALU.is_equal))

            first, second = rt[4], rt[5]
            choose(prob, best1, rs1[4], first, rt[3])
            rest = rt[6]
            link(nc.vector.scalar_tensor_tensor(rest.rearrange("p t e -> p (t e)"),
                                                first.rearrange("p t e -> p (t e)"), -2.0,
                                                prob.rearrange("p t e -> p (t e)"), ALU.mult, ALU.add))
            choose(rest, best2, rs1[5], second, rt[3])
            nc.vector.tensor_tensor(m_b[:, :, :], first, second, ALU.add).then_inc(v_m, 1)
            link(nc.vector.tensor_tensor(rs1[6][:, :], best1[:, :], best2[:, :], ALU.add))
            weight = [rs1[7], rs1[4]]
            link(nc.vector.reciprocal(rs1[6][:, :], rs1[6][:, :]))
            link(nc.vector.tensor_tensor(weight[0][:, :], best1[:, :], rs1[6][:, :], ALU.mult))
            link(nc.vector.tensor_tensor(weight[1][:, :], best2[:, :], rs1[6][:, :], ALU.mult))

            dve.wait_ge(pe_rank, 1)
            count, tiles, start, end = ex[0], ex[1], ex[2], ex[3]
            link(nc.vector.tensor_copy(count[:, :], bank[1][:, 0:E]))
            over = ltmp.rearrange("p (e k) -> p e k", e=E)
            link(nc.vector.tensor_tensor(over, count[:, :].unsqueeze(2).broadcast_to([P, E, NT]),
                                         tab[:, C_CNT:C_CNT + NT].unsqueeze(1).broadcast_to([P, E, NT]), ALU.is_gt))
            link(nc.vector.tensor_reduce(tiles[:, :], over, axis=AX.X, op=ALU.add))
            before = ltmp[:, 0:E * E].rearrange("p (e k) -> p e k", e=E)
            link(nc.vector.tensor_tensor(before, tiles[:, :].unsqueeze(1).broadcast_to([P, E, E]),
                                         tab[:, C_LT:C_LT + E * E].rearrange("p (e k) -> p e k", e=E), ALU.mult))
            link(nc.vector.tensor_reduce(start[:, :], before, axis=AX.X, op=ALU.add))
            link(nc.vector.tensor_tensor(end[:, :], start[:, :], tiles[:, :], ALU.add))
            link(nc.vector.tensor_tensor(ttmp,
                                         tab[:, C_TILE:C_TILE + N_TILES].unsqueeze(2).broadcast_to([P, N_TILES, E]),
                                         end[:, :].unsqueeze(1).broadcast_to([P, N_TILES, E]), ALU.is_ge))
            link(nc.vector.tensor_reduce(slot_t[0][:, :], ttmp, axis=AX.X, op=ALU.add))
            nc.vector.tensor_scalar(tile_e[:, :], slot_t[0][:, :], float(E - 1), None, ALU.min).then_inc(v_te, 1)
            rank = rt[0]
            link(nc.vector.tensor_copy(rank.rearrange("p t e -> p (t e)"), bank[0][:, 0:NT * E]))
            rtile = rt[1]
            link(nc.vector.tensor_tensor(over_rank, rank.rearrange("p t e -> p (t e)").unsqueeze(2).broadcast_to([P, NT * E, NT]),
                                         tab[:, C_CNT:C_CNT + NT].unsqueeze(1).broadcast_to([P, NT * E, NT]), ALU.is_ge))
            link(nc.vector.tensor_reduce(rtile.rearrange("p t e -> p (t e)"), over_rank, axis=AX.X, op=ALU.add))
            link(nc.vector.tensor_scalar(rtile, rtile, -1.0, None, ALU.add))
            lane = rt[2]
            link(nc.vector.scalar_tensor_tensor(lane.rearrange("p t e -> p (t e)"),
                                                rtile.rearrange("p t e -> p (t e)"), -float(P),
                                                rank.rearrange("p t e -> p (t e)"), ALU.mult, ALU.add))
            link(nc.vector.tensor_tensor(rtile, rtile,
                                         start[:, :].unsqueeze(1).broadcast_to([P, NT, E]), ALU.add))
            lanes, tilenos = [rs1[0], rs1[1]], [rs1[2], rs1[3]]
            for k, onehot in enumerate((first, second)):
                for src, dst in ((lane, lanes[k]), (rtile, tilenos[k])):
                    link(nc.vector.tensor_tensor(rt[3], src, onehot, ALU.mult))
                    link(nc.vector.tensor_reduce(dst[:, :], rt[3], axis=AX.X, op=ALU.add))
            steps = [(k, t) for k in range(2) for t in range(NT)]
            for s, (k, t) in enumerate(steps):
                if s >= 2:
                    dve.wait_ge(pe_slot, s - 1)
                nc.vector.tensor_scalar(oh_lane[s % 2], tab[:, C_LANE:C_LANE + P], lanes[k][:, t:t + 1], None, ALU.is_equal)
                nc.vector.tensor_scalar(oh_tile[s % 2][:, 0:N_TILES], tab[:, C_TILE:C_TILE + N_TILES], tilenos[k][:, t:t + 1],
                                        tab[:, C_TOK1 + t:C_TOK1 + t + 1], ALU.is_equal, ALU.mult)
                nc.vector.tensor_scalar(oh_tile[s % 2][:, N_TILES:], tab[:, C_TILE:C_TILE + N_TILES], tilenos[k][:, t:t + 1],
                                        weight[k][:, t:t + 1], ALU.is_equal, ALU.mult).then_inc(v_oh, 1)
            dve.wait_ge(pe_slot, len(steps))
            link(nc.vector.tensor_copy(slot_t[0][:, :], bank[2][:, 0:N_TILES]))
            link(nc.vector.tensor_copy(slot_w[:, :], bank[2][:, N_TILES:2 * N_TILES]))
            link(nc.vector.tensor_scalar(slot_t[1][:, :], slot_t[0][:, :], 0.0, tab[:, C_DUMMY:C_DUMMY + 1],
                                         ALU.is_equal, ALU.mult))
            link(nc.vector.tensor_tensor(slot_t[2][:, :], slot_t[0][:, :], slot_t[1][:, :], ALU.add))
            nc.vector.tensor_scalar(slot_row[:, :], slot_t[2][:, :], -1.0, None, ALU.add).then_inc(v_rows, 1)
            dve.wait_ge(v_rows, 1)

            def low_slots(n, u):
                dve.wait_ge(a_xh, n + 1)
                nc.vector.tensor_tensor(xl[u].rearrange("p c t -> p (c t)"), bank[u][:, 0:D],
                                        xh[u].rearrange("p c t -> p (c t)"), ALU.subtract).then_inc(v_xl, 1)

            def split_hidden(n, u, half):
                dve.wait_ge(a_g, n * 2 + half + 1)
                at = slice(4 * half, 4 * half + 4)
                nc.vector.tensor_copy(ah[:, u, at, :], act[:, u, at, :]).then_inc(v_ah, 1)
                dve.wait_ge(v_ah, n * 2 + half + 1)
                nc.vector.tensor_tensor(al[:, u, at, :], act[:, u, at, :], ah[:, u, at, :], ALU.subtract).then_inc(v_al, 1)

            def weigh(n, u, after):
                e = dve.value_load(tile_e[0:1, bass.ds(n, 1)], min_val=0, max_val=E - 1)
                dve.wait_ge(pe_y, n + 1)
                if after is not None:
                    dve.wait_ge(sc_st, after)
                nc.vector.scalar_tensor_tensor(yb[u], bank[6 + u][:, 0:D], 1.0 / W_SCALE,
                                               b2_sb[:, bass.ds(e * D, D)], ALU.mult, ALU.add).then_inc(v_yt, 1)
                dve.wait_ge(v_yt, n + 1)
                nc.vector.tensor_scalar(yb[u], yb[u], slot_w[:, bass.ds(n, 1)], None, ALU.mult).then_inc(v_y, 1)

            def tile(n, u, following=True):
                split_hidden(n, u, 0)
                if following:
                    low_slots(n + 1, 1 - u)
                split_hidden(n, u, 1)

            for j in range(LATE):
                split_low(j % 2, EARLY * PIECES + j)
            dve.wait_ge(b2_ld, 16)
            low_slots(0, 0)
            low_slots(1, 1)
            tile(0, 0, False)
            tile(1, 1)
            weigh(0, 0, None)
            tile(2, 0)
            weigh(1, 1, None)
            with dve.Fori(0, (N_TILES - 5) // 2) as j:
                for u in range(2):
                    tile(j * 2 + 3 + u, (1 + u) % 2)
                    weigh(j * 2 + 2 + u, u % 2, (j * 2 + 1 + u) * 16)
            tile(N_TILES - 2, 1)
            weigh(N_TILES - 3, 0, (N_TILES - 4) * 16)
            tile(N_TILES - 1, 0, False)
            weigh(N_TILES - 2, 1, (N_TILES - 3) * 16)
            weigh(N_TILES - 1, 0, (N_TILES - 2) * 16)

            for k in range(4):
                dve.wait_ge(f_ld[k], 16)
                at = slice(4 * k, 4 * k + 4)
                for t in range(4 * k, 4 * k + 4):
                    last = nc.vector.bn_stats(fst[:, t, :], fin[:, t, :])
                link(last)
                for t in range(4 * k, 4 * k + 4):
                    last = nc.vector.bn_aggr(fmv[:, t, :], fst[:, t, :])
                link(last)
                inverse_root(nc.vector.tensor_scalar(frs[:, at], fmv[:, at, 1], LN_EPS, None, ALU.add))
                for t in range(4 * k, 4 * k + 4):
                    last = nc.vector.tensor_scalar(fin[:, t, :], fin[:, t, :], fmv[:, t, 0:1], frs[:, t:t + 1],
                                                   ALU.subtract, ALU.mult)
                last.then_inc(v_f, 1)

        @block.tensor
        def _(pe):
            mm = nc.tensor.matmul
            pe.wait_ge(c_ld, 16 * N_LOADS)
            pe.wait_ge(c_bf, 1)
            pe.wait_ge(pw_lo, 3)

            def three(o, lhs, rhs, first=True, final=True):
                mm(o, lhs[0], rhs[0], start=first, stop=False, skip_group_check=True)
                mm(o, lhs[0], rhs[1], start=False, stop=False, skip_group_check=True)
                return mm(o, lhs[1], rhs[0], start=False, stop=final, skip_group_check=True)

            def w_part(at, n, rows=P):
                return wph[0:rows, at:at + n], wpl[0:rows, at:at + n]

            def transpose_max(a, b):
                pe.wait_ge(v_nm[a], b + 1)
                out_b = ps_m[0][:, 0:T // 2].bitcast(BF16)
                for t in range(TT):
                    last = nc.tensor.transpose(out_b[:, t * P:(t + 1) * P], negm[a][:, t, :], ident_b[:, :])
                last.then_inc(pe_mT[a], 1)

            def weighted_values(group, g, values, causal):
                for k in range(TT):
                    for j in range(4):
                        h = 4 * g + j
                        o = ps_o[g % 2][32 * j:32 * j + 32, :]
                        if k == 0 or not causal:
                            last = mm(o[:, 0:T], values[:, k, h, :], probs[:, j, k * T:(k + 1) * T],
                                      start=(k == 0), stop=(k == 1), skip_group_check=True)
                        else:
                            last = mm(o[:, P:T], values[:, k, h, :], probs[:, j, T:T + P],
                                      start=False, stop=True, skip_group_check=True)
                last.then_inc(pe_pv, 1)

            def by_token(a, banks):
                for t in range(TT):
                    for g in range(4):
                        last = nc.tensor.transpose(banks[t][:, g * P:(g + 1) * P], oP[:, g, t * P:(t + 1) * P], ident)
                last.then_inc(pe_n1[a], 1)

            def back(a, bank_):
                for c in range(DC):
                    for t in range(TT):
                        last = nc.tensor.transpose(bank_[:, c * T + t * P:c * T + (t + 1) * P],
                                                   o_tok[:, t, c * P:(c + 1) * P], ident)
                last.then_inc(pe_n2[a], 1)

            def project_heads(a, bank_, w):
                for t in range(TT):
                    for c in range(DC):
                        last = mm(bank_[:, t * D:(t + 1) * D], oT[:, c, t * P:(t + 1) * P], w[:, c, :],
                                  start=(c == 0), stop=(c == DC - 1))
                last.then_inc(pe_w[a], 1)

            def step(i, i0):
                has = {u for u, _ in units(i0)}
                for u, k in units(i0):
                    b = i - BEHIND.get(u, 0)
                    if u == "x_transpose":
                        if i0 is None or i0 >= 2:
                            pe.wait_ge(v_mT[1], i - 1)
                        pe.wait_ge(x_ld, b * 16 + 16)
                        for c in range(DC):
                            for t in range(TT):
                                last = nc.tensor.transpose(ps_m[0][:, c * T + t * P:c * T + (t + 1) * P],
                                                           x_sb[:, t, c * P:(c + 1) * P], ident)
                        last.then_inc(pe_xT, 1)
                    elif u == "latents":
                        pe.wait_ge(v_xT, b + 1)
                        if i0 is None or i0 >= 2:
                            pe.wait_ge(v_lg, i - 1)
                        for t in range(TT):
                            at = slice(t * P, (t + 1) * P)
                            for c in range(DC):
                                three(ps_m[0][:, t * KVR:(t + 1) * KVR], (xTh[:, c, at], xTl[:, c, at]),
                                      w_part(W_KV + c * KVR, KVR), c == 0, c == DC - 1)
                        for c in range(DC):
                            last = three(ps_m[1][:, 0:T], w_part(W_Q + c * QR, QR), (xTh[:, c, :], xTl[:, c, :]),
                                         c == 0, c == DC - 1)
                        last.then_inc(pe_qkv, 1)
                    elif u == "kv_transpose":
                        pe.wait_ge(c_ld, 16 * N_LOADS)
                        pe.wait_ge(v_kvn, b + 1)
                        for t in range(TT):
                            last = nc.tensor.transpose(ps_m[0][0:KVR, t * P:(t + 1) * P], kvn[:, t, :], ident)
                        last.then_inc(pe_kvT, 1)
                    elif u == "values":
                        pe.wait_ge(v_qc, b + 1)
                        pe.wait_ge(v_kvT, b + 1)
                        for t in range(TT):
                            at = slice(t * P, (t + 1) * P)
                            last = three(ps_m[1][:, t * D:(t + 1) * D], (kvh[:, at], kvl[:, at]), w_part(W_V, D, KVR))
                        last.then_inc(pe_v, 1)
                    elif u == "qk":
                        s = ps_s[k % 2]
                        if k >= 2:
                            pe.wait_ge(v_sw, b * (H // 2) + k - 1)
                        elif i0 is None or i0 >= 1:
                            pe.wait_ge(s_used, used_base(i) - 1 + k)
                        three(s[:, 0:T], w_part(W_QH + k * P, P), (qch[:, :], qcl[:, :]))
                        for c in range(DC):
                            three(s[:, T:2 * T], w_part(W_KR + c * H * QK + k * P, P), (xTh[:, c, :], xTl[:, c, :]), c == 0, False)
                        three(s[:, T:2 * T], w_part(W_KC + k * P, P, KVR), (kvh[:, :], kvl[:, :]), False, True).then_inc(s_full, 1)
                    elif u == "self_max":
                        hp, r = k // 2, QK * (k % 2)
                        q, key = qk_b[r:r + QK, hp, 0, :], qk_b[r:r + QK, hp, 1, :]
                        s = ps_s[k % 2]
                        pe.wait_ge(a_qkb, b * (H // 2) + hp + 1)
                        if k == 0:
                            pe.wait_ge(v_sw, b * (H // 2) + H // 2)
                        if k >= 2:
                            pe.wait_ge(s_used, used_base(i) + k - 1)
                        mm(s[:, 0:P], q[:, 0:P], key[:, 0:P], start=True, stop=False)
                        mm(s[:, 0:P], ident_b[:, :], mask_b[:, :], start=False, stop=True)
                        mm(s[:, P:3 * P], q[:, P:T], key[:, 0:T], start=True, stop=False, skip_group_check=True)
                        mm(s[:, 2 * P:3 * P], ident_b[:, :], mask_b[:, :], start=False, stop=True,
                           skip_group_check=True).then_inc(s_full, 1)
                    elif u == "self_maxT":
                        transpose_max(0, b)
                    elif u == "self_exp":
                        hp, r = k // 2, QK * (k % 2)
                        q, key = qk[r:r + QK, hp, 0, :], qk[r:r + QK, hp, 1, :]
                        pick = ident_b[r:r + QK, r + hp:r + hp + 1].broadcast_to([QK, P])
                        s = ps_t[k % 2]
                        at = self_exp_at(i, k)
                        if k == 0:
                            pe.wait_ge(v_mT[0], b + 1)
                        if not (i0 == 0 and k < 2):
                            pe.wait_ge(a_p, at - 1)
                        if i0 == 1 and k < 2:
                            pe.wait_ge(v_n2[0] if k == 0 else v_r[0], 1 + k)
                        mm(s[:, 0:T], key[:, 0:P], q[:, :], start=True, stop=False, skip_group_check=True)
                        mm(s[:, 0:T], pick, mT[0][r:r + QK, :], start=False, stop=False, skip_group_check=True)
                        mm(s[:, 0:P], ident_b[:, :], maskt_b[:, :], start=False, stop=True, skip_group_check=True)
                        mm(s[:, T:T + P], key[:, P:T], q[:, P:T], start=True, stop=False, skip_group_check=True)
                        mm(s[:, T:T + P], pick, mT[0][r:r + QK, P:T], start=False, stop=False, skip_group_check=True)
                        mm(s[:, T:T + P], ident_b[:, :], maskt_b[:, :], start=False, stop=True,
                           skip_group_check=True).then_inc(pe_t, 1)
                    elif u in ("self_pv", "cross_pv"):
                        cross = u == "cross_pv"
                        group = (i * 8 - 8 + (0 if cross else 4) if i0 is None else (exp_base(i) if cross else self_exp_at(i, 0)) // 4) + k
                        pe.wait_ge(a_p, (exp_base(i) if cross else self_exp_at(i, 0)) + 4 * k + 4)
                        if not (i0 == 0 and k < 2):
                            pe.wait_ge(a_o, group - 1)
                        if cross and k == 0:
                            pe.wait_ge(a_cv, b + 2)
                        if not cross and k == 0:
                            pe.wait_ge(a_v, b + 1)
                        weighted_values(group, k, c_sb if cross else v_sb, not cross)
                    elif u == "self_norm":
                        pe.wait_ge(a_p, exp_base(i))
                        pe.wait_ge(a_o, exp_base(i) // 4 if isinstance(i, int) else i * 8 - 8)
                        by_token(0, ps_t)
                    elif u == "self_back":
                        pe.wait_ge(v_n1[0], b + 1)
                        back(0, ps_t[0])
                    elif u == "self_out":
                        pe.wait_ge(v_n2[0], b + 1)
                        project_heads(0, ps_t[1], wo_sb)
                    elif u == "stack_transpose":
                        if k == 0:
                            pe.wait_ge(a_x1h, b + 1)
                            pe.wait_ge(p_x1l, b + 1)
                            pe.wait_ge(a_ch, b + 1)
                            pe.wait_ge(p_cl, b + 2)
                        if k < 2:
                            pe.wait_ge(s_used, cross_used_at(i))
                        if k >= 2:
                            pe.wait_ge(a_xc, b * 4 + k - 1)
                        for n, hp in enumerate((2 * k, 2 * k + 1)):
                            for a, src in enumerate((x1s, cs)):
                                for t in range(TT):
                                    at = n * 2 * T + a * T + t * P
                                    last = nc.tensor.transpose(
                                        ps_sh[k % 2][:, at:at + P],
                                        src[:, t, 2 * hp:2 * hp + 2, :].rearrange("p h d -> p (h d)"), ident_h[:, :])
                        last.then_inc(pe_xc, 1)
                    elif u == "cross_max":
                        hp, r = k // 2, QK * (k % 2)
                        q, key = xc[r:r + QK, hp, 0, :], xc[r:r + QK, hp, 1, :]
                        if k == 0:
                            pe.wait_ge(a_xc, b * 4 + 4)
                        if k >= 2:
                            pe.wait_ge(s_used, cross_used_at(i) + k - 1)
                        for t in range(TT):
                            last = mm(ps_s[k % 2][:, t * T:(t + 1) * T], q[:, t * P:(t + 1) * P], key[:, :], start=True, stop=True)
                        last.then_inc(s_full, 1)
                    elif u == "cross_maxT":
                        if "x2_transpose" in has:
                            pe.wait_ge(a_x2T, i - 1)
                        transpose_max(1, b)
                    elif u == "cross_exp":
                        hp, r = k // 2, QK * (k % 2)
                        q, key = xc[r:r + QK, hp, 0, :], xc[r:r + QK, hp, 1, :]
                        pick = ident_b[r:r + QK, r + hp:r + hp + 1].broadcast_to([QK, P])
                        if k == 0:
                            pe.wait_ge(v_mT[1], b + 1)
                        if k < 2 and "self_out" in has:
                            pe.wait_ge(v_n2[0] if k == 0 else v_r[0], i + k)
                        pe.wait_ge(a_p, exp_base(i) + k - 1)
                        for t in range(TT):
                            mm(ps_t[k % 2][:, t * T:(t + 1) * T], key[:, t * P:(t + 1) * P], q[:, :], start=True, stop=False)
                            last = mm(ps_t[k % 2][:, t * T:(t + 1) * T], pick, mT[1][r:r + QK, :], start=False, stop=True)
                        last.then_inc(pe_t, 1)
                    elif u == "cross_norm":
                        if i0 is None:
                            pe.wait_ge(a_v, i + 1)
                            pe.wait_ge(a_o, i * 8 - 4)
                        else:
                            pe.wait_ge(a_o, exp_base(i) // 4 + 4)
                        by_token(1, ps_m)
                    elif u == "cross_back":
                        pe.wait_ge(v_n1[1], b + 1)
                        back(1, ps_m[0])
                    elif u == "cross_out":
                        pe.wait_ge(v_n2[1], b + 1)
                        project_heads(1, ps_m[1], wx_sb)
                    elif u == "x2_transpose":
                        pe.wait_ge(v_x2, b + 1)
                        for c in range(DC):
                            for t in range(TT):
                                last = nc.tensor.transpose(ps_m[0][:, c * T + t * P:c * T + (t + 1) * P],
                                                           x2[:, t, c * P:(c + 1) * P], ident)
                        last.then_inc(pe_x2T, 1)
                    elif u == "logits":
                        pe.wait_ge(a_x2T, b + 1)
                        for t in range(TT):
                            for c in range(DC):
                                last = mm(ps_m[1][:, t * E:(t + 1) * E], x2T[:, c, t * P:(t + 1) * P], wg_sb[:, c, :],
                                          start=(c == 0), stop=(c == DC - 1))
                        last.then_inc(pe_lg, 1)

            each_step(pe, step)

            pe.wait_ge(v_m, 1)
            m_flat = m_b[:, :, :].rearrange("p t e -> p (t e)")
            mm(bank[0][:, 0:NT * E], up_b[:, :], m_flat, start=True, stop=False, skip_group_check=True)
            for t in range(NT - 1):
                mm(bank[0][:, (t + 1) * E:NT * E].rearrange("p (t e) -> p t e", e=E), ones_b[:, :],
                   m_b[:, t:t + 1, :].broadcast_to([P, NT - 1 - t, E]), start=False, stop=(t == NT - 2), skip_group_check=True)
            for t in range(NT):
                last = mm(bank[1][:, 0:E], ones_b[:, :], m_b[:, t, :], start=(t == 0), stop=(t == NT - 1))
            last.then_inc(pe_rank, 1)
            for s in range(2 * NT):
                pe.wait_ge(v_oh, s + 1)
                mm(bank[2][:, 0:2 * N_TILES], oh_lane[s % 2], oh_tile[s % 2], start=(s == 0),
                   stop=(s == 2 * NT - 1)).then_inc(pe_slot, 1)

            pe.wait_ge(v_rows, 1)

            def slots_in(n, u, loaded):
                pe.wait_ge(g_ld[u], loaded)
                for c in range(DC):
                    last = nc.tensor.transpose(bank[u][:, c * P:(c + 1) * P], xg[u][:, c * P:(c + 1) * P], ident)
                last.then_inc(pe_ft, 1)

            def up(n, u, e):
                pe.wait_ge(v_xl, n + 1)
                for half in range(2):
                    for f in range(4 * half, 4 * half + 4):
                        o = bank[2 + 2 * u + half][:, (f % 4) * P:(f % 4 + 1) * P]
                        for c in range(DC):
                            at = bass.ds(e * EW + c * F + f * P, P)
                            mm(o, whi[:, at], xh[u][:, c, :], start=(c == 0), stop=False)
                            mm(o, whi[:, at], xl[u][:, c, :], start=False, stop=False)
                            last = mm(o, wlo[:, at], xh[u][:, c, :], start=False, stop=(c == DC - 1))
                    last.then_inc(pe_h, 1)

            def down(n, u, e):
                pe.wait_ge(v_al, n * 2 + 2)
                for f in range(FC):
                    at = bass.ds(e * EW + (DC * F + f * D), D)
                    o = bank[6 + u][:, 0:D]
                    mm(o, ah[:, u, f, :], whi[:, at], start=(f == 0), stop=False)
                    mm(o, ah[:, u, f, :], wlo[:, at], start=False, stop=False)
                    last = mm(o, al[:, u, f, :], whi[:, at], start=False, stop=(f == FC - 1))
                last.then_inc(pe_y, 1)

            def expert(n):
                return pe.value_load(tile_e[0:1, bass.ds(n, 1)], min_val=0, max_val=E - 1)

            def tile(n, u, act_read, loaded, out_read):
                e, e_before = expert(n), expert(n - 1)
                if act_read is not None:
                    pe.wait_ge(a_g, act_read)
                up(n, u, e)
                if loaded is not None:
                    slots_in(n + 1, 1 - u, loaded)
                if out_read is not None:
                    pe.wait_ge(v_y, out_read)
                down(n - 1, 1 - u, e_before)

            pe.wait_ge(w_lo, E * PIECES + 1)
            e_first = expert(0)
            slots_in(0, 0, 16)
            slots_in(1, 1, 16)
            up(0, 0, e_first)
            tile(1, 1, None, 32, None)
            tile(2, 0, 2, 32, None)
            with pe.Fori(0, (N_TILES - 5) // 2) as j:
                for u in range(2):
                    tile(j * 2 + 3 + u, (1 + u) % 2, j * 4 + 2 * u + 4, j * 16 + 48, j * 2 + u + 1)
            tile(N_TILES - 2, 1, 2 * (N_TILES - 3), 16 * ((N_TILES + 1) // 2), N_TILES - 4)
            tile(N_TILES - 1, 0, 2 * (N_TILES - 2), None, N_TILES - 3)
            e_last = expert(N_TILES - 1)
            pe.wait_ge(v_y, N_TILES - 2)
            down(N_TILES - 1, 0, e_last)


def _table():
    import numpy as np
    t = np.zeros((P, C_ALL), np.float32)
    lane = np.arange(P)
    inv = 1.0 / 10000.0 ** (np.arange(0, RD, 2, dtype=np.float32) / RD)
    freqs = np.outer(np.arange(T, dtype=np.float32), inv).astype(np.float32)
    r = lane % QK - (QK - RD)
    rot = r >= 0
    i = np.where(rot, r, 0) % (RD // 2)
    sign = np.where(r < RD // 2, -1.0, 1.0)
    t[:, C_COS:C_COS + T] = np.where(rot[:, None], np.cos(freqs).T[i], 1.0) / W_SCALE
    t[:, C_SIN:C_SIN + T] = np.where(rot[:, None], np.sin(freqs).T[i] * sign[:, None], 0.0) / W_SCALE
    t[:, C_ID:C_ID + P] = np.eye(P)
    t[:, C_MASK:C_MASK + P] = np.where(lane[None, :] > lane[:, None], -1e30, 0.0)
    t[:, C_MASKT:C_MASKT + P] = np.where(lane[:, None] > lane[None, :], -1e30, 0.0)
    t[:, C_UP:C_UP + P] = lane[:, None] < lane[None, :]
    t[:, C_REV:C_REV + E] = E - np.arange(E)
    t[:, C_CNT:C_CNT + NT] = P * np.arange(NT)
    t[:, C_LT:C_LT + E * E] = (np.arange(E)[None, :] < np.arange(E)[:, None]).reshape(-1)
    t[:, C_TILE:C_TILE + N_TILES] = np.arange(N_TILES)
    t[:, C_LANE:C_LANE + P] = lane
    t[:, C_TOK1:C_TOK1 + NT] = P * np.arange(NT)[None, :] + lane[:, None] + 1
    t[:, C_DUMMY] = TOK + 1 + lane
    return t


def kernel(**inputs):
    import numpy as np
    import concourse.bacc as bacc
    from concourse.bass_utils import run_bass_kernel_spmd as run

    a = {k: np.asarray(v) for k, v in inputs.items()}

    def heads(w, at, width):
        o = np.zeros((w.shape[0], H, QK), np.float32)
        o[:, :, at:at + width] = w.reshape(w.shape[0], H, width)
        return o.reshape(w.shape[0], H * QK)

    wq = heads(a["L0_attn_W_qdec"], 0, HD)
    wq.reshape(QR, H, QK)[:, :, QK - RD:] = a["L0_attn_W_qrope"].reshape(QR, H, RD)
    w2 = a["L0_ffn_W2"].reshape(E, 2, FC // 2, P, D).transpose(0, 1, 3, 2, 4).reshape(E, 2, P, PIECE)
    w_exp = np.concatenate([a["L0_ffn_W1"].reshape(E, DC, P, F), w2], 1).reshape(E * PIECES, P, PIECE)
    arrays = {
        "x": a["x"], "ctx": a["ctx_1024"], "w_kv": a["L0_attn_W_kv"], "g_kv": a["L0_attn_g_kv"], "w_q": a["L0_attn_W_q"],
        "wq_heads": wq, "wk_content": heads(a["L0_attn_W_kdec"], 0, HD), "wk_rope": heads(a["L0_attn_W_krope"], QK - RD, RD),
        "wv": a["L0_attn_W_vdec"], "wo": a["L0_attn_W_o"], "wx": a["L0_xattn_W"].T,
        "xb": a["L0_xattn_b"], "wg": a["L0_ffn_Wg"], "bg": a["L0_ffn_bg"], "w_exp": w_exp,
        "b1t": a["L0_ffn_b1"].reshape(E, FC, P).transpose(2, 0, 1).reshape(P, E * FC),
        "b2": a["L0_ffn_b2"], "table": _table()}
    arrays = {"in_" + k: np.ascontiguousarray(v) for k, v in arrays.items()}
    nc = bacc.Bacc("TRN2", target_bir_lowering=False, num_devices=1)
    aps = [nc.dram_tensor(k, v.shape, F32, kind="ExternalInput").ap() for k, v in arrays.items()]
    out = nc.dram_tensor("out", (B, T, D), F32, kind="ExternalOutput").ap()
    x2_rows = nc.dram_tensor("x2_rows", (ROWS, D), F32, kind="Internal").ap()
    acc_rows = nc.dram_tensor("acc_rows", (ROWS, D), F32, kind="Internal").ap()
    decoder_layer(nc, *aps, out, x2_rows, acc_rows)
    return run(nc, [arrays], core_ids=[0]).results[0]["out"]
```

```python
import concourse.bass as bass
from concourse import mybir
from contextlib import ExitStack

F32 = mybir.dt.float32
F16 = mybir.dt.float16
BF16 = mybir.dt.bfloat16
I32 = mybir.dt.int32
ACT = mybir.ActivationFunctionType
ALU = mybir.AluOpType
AX = mybir.AxisListType

P = 128
B, T, D = 8, 256, 256
TT = T // P
DC = D // P
H = 16
HD = D // H
RD = 32
QK = 64
KVR, QR = 64, 128
E, F = 8, 1024
EW = 2 * D * F // P
PIECE = F
PIECES = EW // PIECE
EARLY = 5
FC = F // P
NT = B * TT
TOK = B * T
N_TILES = (2 * TOK + E * (P - 1)) // P
ROWS = TOK + P
W_SCALE = 64.0
RMS_EPS, LN_EPS = 1e-6, 1e-5
SELF_SCALE = float(HD + RD) ** -0.5
CROSS_SCALE = float(HD) ** -0.5

C_COS = 0
C_SIN = C_COS + T
C_ID = C_SIN + T
C_MASK = C_ID + P
C_MASKT = C_MASK + P
C_UP = C_MASKT + P
C_REV = C_UP + P
C_CNT = C_REV + E
C_LT = C_CNT + NT
C_TILE = C_LT + E * E
C_LANE = C_TILE + N_TILES
C_TOK1 = C_LANE + P
C_DUMMY = C_TOK1 + NT
C_ALL = C_DUMMY + 1


BEHIND = {"x_transpose": 0, "latents": 0, "latents_scale": 0, "kv_transpose": 0, "values": 0, "qk": 0, "rot": 0, "add": 0, "cast": 0, "latents_root": 0,
          "self_max": 0, "self_maxT": 0,
          "self_exp": 1, "self_pv": 1, "self_norm": 1, "self_back": 1, "self_out": 1, "self_root": 1, "self_scale": 1, "context": 1,
          "values_in": 2, "stack_transpose": 2, "cross_max": 2, "cross_maxT": 2, "cross_exp": 2, "cross_pv": 2, "cross_norm": 2, "cross_divide": 2, "keep": 2,
          "split_high": 0, "split_low": 0, "late_high": 0, "late_low": 0,
          "cross_back": 3, "cross_out": 3, "cross_root": 3, "cross_scale": 3, "x2_transpose": 3, "logits": 3}
_AFTER_SELF_EXP = {
    0: [("cross_back", 0), ("stack_transpose", 1), ("split_high", 0), ("late_high", 9)],
    1: [("stack_transpose", 2), ("late_low", 9)],
    2: [("cross_out", 0), ("split_low", 0), ("late_high", 10)],
    3: [("cross_root", 0), ("stack_transpose", 3), ("late_low", 10)],
    4: [("self_pv", 0), ("cross_scale", 0), ("cross_max", 0), ("late_high", 11)],
    5: [("cross_max", 1), ("cross_max", 2)],
    6: [("x2_transpose", 0), ("split_high", 1), ("cross_max", 3), ("cross_max", 4), ("late_low", 11)],
    7: [("x_transpose", 0), ("cross_max", 5), ("cross_max", 6)],
    8: [("self_pv", 1), ("keep", 0), ("logits", 0), ("split_low", 1), ("cross_max", 7)],
    9: [("latents", 0), ("latents_root", 0), ("cross_max", 8)],
    10: [("latents_scale", 0), ("cross_max", 9), ("cross_max", 10)],
    11: [("kv_transpose", 0), ("cross_max", 11)],
    12: [("self_pv", 2), ("cross_max", 12), ("split_high", 2)],
    13: [("cross_max", 13), ("cross_max", 14)],
    14: [("cross_max", 15), ("qk", 0), ("rot", 0)],
    15: [("qk", 1), ("rot", 1), ("self_pv", 3), ("cross_maxT", 0), ("values", 0), ("qk", 2), ("rot", 2), ("add", 0), ("cast", 0),
         ("self_norm", 0), ("split_low", 2), ("qk", 3), ("rot", 3), ("add", 1), ("cast", 1),
         ("qk", 4), ("rot", 4), ("self_back", 0), ("add", 2), ("cast", 2), ("qk", 5), ("rot", 5), ("add", 3),
         ("context", 0), ("cast", 3), ("qk", 6), ("rot", 6), ("add", 4), ("split_high", 3), ("qk", 7), ("rot", 7), ("self_out", 0),
         ("cast", 4)]}
STEP = [("values_in", 0), ("stack_transpose", 0)]
STEP += [_u for _h in range(H) for _u in [("self_exp", _h)] + _AFTER_SELF_EXP[_h]]
_AFTER_CROSS_EXP = {0: [("add", 5)], 1: [("cast", 5)], 2: [("add", 6), ("self_root", 0)], 3: [("cast", 6)],
                    4: [("add", 7), ("self_scale", 0)], 5: [("cast", 7)],
                    8: [("split_low", 3)]}
for _h in range(H + 1):
    STEP += [("cross_exp", _h)] if _h < H else []
    STEP += [("cross_pv", _h // 4 - 1)] if _h % 4 == 0 and _h else []
    STEP += _AFTER_CROSS_EXP.get(_h, [])
    STEP += [("self_max", _h)] if _h < H else []
    for _k in (_h // 4, _h // 4 + PIECES) if _h < H else ():
        STEP += [("late_high", _k)] if _h % 4 == 1 else [("late_low", _k)] if _h % 4 == 3 else []
    STEP += {14: [("late_high", 8)], 16: [("late_low", 8)]}.get(_h, [])
STEP += [("cross_norm", 0), ("self_maxT", 0), ("cross_divide", 0)]
ADD_VECTOR = (0, 2, 4, 6, 7)
LATE = [(E - 3, 0), (E - 3, 1), (E - 3, 2), (E - 3, 3), (E - 2, 2), (E - 2, 3), (E - 1, 2), (E - 1, 3),
        (E - 2, 0), (E - 2, 1), (E - 1, 0), (E - 1, 1)]
LATE_STEP = [0, 0, 0, 0, 1, 1, 1, 1, 1, 2, 2, 2]
LOOP0, LOOP1 = max(BEHIND.values()), B
LAST_STEP = LOOP1 + LOOP0
EXP, PV, MAX = ("self_exp", "cross_exp"), ("self_pv", "cross_pv"), ("self_max", "cross_max")
FULL = ("qk",) + MAX


def units(i0):
    def runs(u, k):
        if u.startswith("split"):
            return i0 is None
        if u.startswith("late_"):
            return i0 == LOOP1 + LATE_STEP[k]
        return i0 is None or 0 <= i0 - BEHIND[u] < B

    return [(u, k) for u, k in STEP if runs(u, k)]


def before(names, i, unit, per=1):
    names = (names,) if isinstance(names, str) else names

    def count(listed):
        return sum(u in names for u, _ in listed)

    here = i if isinstance(i, int) else None
    inside = units(here)
    n = count(inside[:inside.index(unit)])
    if here is not None:
        return (sum(count(units(j)) for j in range(i)) + n) // per
    steady = count(STEP)
    return i * (steady // per) + (sum(count(units(j)) for j in range(LOOP0)) + n - LOOP0 * steady) // per


def decoder_layer(nc, x, ctx_in, w_kv, g_kv, w_q, wq_heads, wk_content, wk_rope, wv, wo, wx,
                  xb, wg, bg, w_exp, b1t, b2, table, out, x2_rows, acc_rows):
    stack = ExitStack()
    with stack:
        def sb(name, shape, dt=F32):
            return stack.enter_context(nc.sbuf_tensor(name, shape, dt))

        def sem(name):
            return stack.enter_context(nc.semaphore(name))

        tab = sb("tab", [P, C_ALL])
        ident = tab[:, C_ID:C_ID + P]
        ident_b = sb("ident_b", [P, P], BF16)
        ident_h = sb("ident_h", [P, P], F16)
        mask_b = sb("mask_b", [P, P], BF16)
        maskt_b = sb("maskt_b", [P, P], BF16)
        up_b = sb("up_b", [P, P], BF16)
        ones_b = sb("ones_b", [P, P], BF16)
        W_KV, W_Q, W_QH = 0, DC * KVR, DC * (KVR + QR)
        W_KR = W_QH + H * QK
        W_KC = W_KR + DC * H * QK
        W_V = W_KC + H * QK
        W_ALL = W_V + D
        wph = sb("wph", [P, W_ALL], F16)
        wpl = sb("wpl", [P, W_ALL], F16)
        wo_sb = sb("wo_sb", [P, DC, D])
        wx_sb = sb("wx_sb", [P, DC, D])
        wg_sb = sb("wg_sb", [P, DC, E])
        g_sb = sb("g_sb", [KVR, 1])
        xb_sb = sb("xb_sb", [P, D])
        bg_sb = sb("bg_sb", [P, E])
        b1_sb = sb("b1_sb", [P, E * FC])
        EW2, W2_AT = 2 * EW, 2 * DC * F
        w_sb = sb("w_sb", [P, E * EW2], F16)
        tail = w_sb[:, EARLY * EW2:E * EW2].bitcast(F32)
        hi_tail, lo_tail = tail[:, 0:(E - EARLY) * EW // 2], tail[:, (E - EARLY) * EW // 2:(E - EARLY) * EW]

        def piece_parts(e, j):
            if j < DC:
                return [w_sb[:, bass.ds(e * EW2 + (a * DC * F + j * F), F)] for a in range(2)]
            at = e * EW2 + (W2_AT + (j - DC) * 2 * PIECE)
            both = w_sb[:, bass.ds(at, 2 * PIECE)].rearrange("p (f a d) -> p f a d", a=2, d=D)
            return [both[:, :, a, :] for a in range(2)]

        def staged(stage, j):
            return stage if j < DC else stage.rearrange("p (f d) -> p f d", d=D)

        x_sb = sb("x_sb", [P, TT, D])
        x_res = sb("x_res", [P, TT, D])
        xT = sb("xT", [P, DC * T])
        xTh = xT[:, 0:T].bitcast(F16).rearrange("p (c t) -> p c t", c=DC)
        xTl = xT[:, T:2 * T].bitcast(F16).rearrange("p (c t) -> p c t", c=DC)
        qch, qcl = sb("qch", [P, T], F16), sb("qcl", [P, T], F16)
        kvn = sb("kvn", [P, TT, KVR])
        kvh, kvl = sb("kvh", [KVR, T], F16), sb("kvl", [KVR, T], F16)
        v_sb = lo_tail[:, 2048:3072].rearrange("p (t h d) -> p t h d", t=TT, h=H)
        sq = sb("sq", [P, KVR])
        ss = sb("ss", [P, TT])
        rs = sb("rs", [P, TT])
        qk = hi_tail[:, 0:4096].rearrange("p (g a t) -> p g a t", g=H // 2, a=2)
        qk_b = lo_tail[:, 0:2048].bitcast(BF16).rearrange("p (g a t) -> p g a t", g=H // 2, a=2)
        mx = sb("mx", [P, H, 3])
        mx2 = sb("mx2", [P, H])
        ctx_raw = sb("ctx_raw", [P, TT, D])
        c_sb = lo_tail[:, 3072:4096].rearrange("p (t h d) -> p t h d", t=TT, h=H)
        x1s = lo_tail[:, 4096:5120].bitcast(F16).rearrange("p (t h d) -> p t h d", t=TT, h=H)
        cs = lo_tail[:, 5120:6144].bitcast(F16).rearrange("p (t h d) -> p t h d", t=TT, h=H)
        xc = hi_tail[:, 4096:6144].bitcast(F16).rearrange("p (g a t) -> p g a t", g=H // 2, a=2)
        mxc = sb("mxc", [P, H, 2])
        negm = [sb(f"negm{i}", [P, TT, P], BF16) for i in range(2)]
        mT = [sb(f"mT{i}", [P, T], BF16) for i in range(2)]
        probs = sb("probs", [P, 4, 2 * T])
        oP = sb("oP", [P, 4, T])
        rec = sb("rec", [P, TT, H])
        o_tok = sb("o_tok", [P, TT, D])
        oT = sb("oT", [P, DC, T])
        stats = sb("stats", [P, TT, 6])
        mv = sb("mv", [P, TT, 2])
        rstd = sb("rstd", [P, TT])
        spare = sb("spare", [P, 1])
        minus_half = sb("minus_half", [P, 4])
        x1 = sb("x1", [P, TT, D])
        x1_prev = sb("x1_prev", [P, TT, D])
        x2 = sb("x2", [P, TT, D])
        x2T = sb("x2T", [P, DC, T])
        swap = [sb(f"swap{i}", [P, 2, T]) for i in range(2)] + [x2T]
        logits = sb("logits", [P, NT, E])
        wstage0 = sb("wstage0", [P, PIECE])

        rt = [(oP[:, i // 2, (i % 2) * P:(i % 2 + 1) * P]).rearrange("p (t e) -> p t e", e=E) for i in range(8)]
        OH = 4
        oh_lane = [probs[:, i, :].rearrange("p (t l) -> p t l", t=OH) for i in range(2)]
        oh_eq = [probs[:, 2 + i, 0:OH * N_TILES].rearrange("p (t i) -> p t i", t=OH) for i in range(2)]
        oh_tile = [a[:, :, :].rearrange("p t d -> p (t d)")[:, 0:OH * 2 * N_TILES].rearrange("p (t a i) -> p t a i", t=OH, a=2)
                   for a in (x1, x1_prev)]
        values = o_tok[:, 0, 0:4 * NT].rearrange("p (k t a) -> p k t a", k=2, a=2)
        flat = swap[0][:, :, :].rearrange("p a t -> p (a t)")
        ttmp = flat[:, 0:N_TILES * E].rearrange("p (i e) -> p i e", e=E)
        ltmp = flat[:, 320:320 + E * NT]
        rs1 = [sb(f"rs1_{i}", [P, NT]) for i in range(8)]
        m_b = sb("m_b", [P, NT, E], BF16)
        ex = [sb(f"ex{i}", [P, E]) for i in range(4)]
        slot_w = sb("slot_w", [P, N_TILES])
        slot_t = [sb(f"slot_t{i}", [P, N_TILES]) for i in range(3)]
        slot_row = sb("slot_row", [P, N_TILES], I32)
        tile_e = sb("tile_e", [P, N_TILES], I32)
        wstage = [wstage0[:, :]] + [wpl[:, 2 * i * PIECE:2 * (i + 1) * PIECE].bitcast(F32) for i in range(2)]

        b2_sb = wph[:, 0:2 * E * D].bitcast(F32)
        xg = [x_sb[:, i, :] for i in range(2)]
        idx_g = [sb(f"idx_g{i}", [P, 1], I32) for i in range(2)]
        idx_s = [sb(f"idx_s{i}", [P, 1], I32) for i in range(2)]
        xparts = xT[:, :].bitcast(F16).rearrange("p (u k c t) -> p u k c t", u=2, k=2, c=DC)
        xh = [xparts[:, i, 0, :, :] for i in range(2)]
        xl = [xparts[:, i, 1, :, :] for i in range(2)]
        act = probs[:, :, :].rearrange("p a n -> p (a n)").rearrange("p (u f t) -> p u f t", u=2, f=FC)
        ah = wpl[:, 0:2 * FC * P].rearrange("p (u f t) -> p u f t", u=2, f=FC)
        al = wpl[:, 2 * FC * P:4 * FC * P].rearrange("p (u f t) -> p u f t", u=2, f=FC)
        yb = [x_res[:, i, :] for i in range(2)]
        fin = w_sb[:, 0:NT * D * 2].bitcast(F32).rearrange("p (t d) -> p t d", d=D)
        fst = sb("fst", [P, NT, 6])
        fmv = sb("fmv", [P, NT, 2])
        frs = sb("frs", [P, NT])
        fnb = sb("fnb", [P, NT])

        W_RAW = [(W_KV, W_KR), (W_KR, W_KC), (W_KC, W_ALL)]
        wraw = hi_tail[:, 0:W_ALL]

        bank = [stack.enter_context(nc.psum_tensor(f"bank{i}", [P, 512], F32)) for i in range(8)]
        ps_s, ps_t, ps_o, ps_m = bank[0:2], bank[2:4], bank[4:6], bank[6:8]
        ps_qk = ps_s + ps_t + ps_s + ps_t
        ps_max = ps_s[1], ps_m[0]
        ps_sh = [ps_s[i][:, :].bitcast(F16) for i in range(2)]

        c_ld, r_ld = sem("consts_loaded"), sem("raw_weights_loaded")
        c_ms, c_bf = sem("pads_set"), sem("bf16_consts")
        pw_hi, pw_lo = sem("projections_high"), sem("projections_low")
        x_ld, xr_ld, ctx_ld = sem("x_loaded"), sem("x_residual_loaded"), sem("ctx_loaded")
        w_ld = [sem(f"wstage_loaded{i}") for i in range(3)]
        w_hi, w_lo = sem("w_high_done"), sem("w_low_done")
        pe_xT, a_xT, v_xT = sem("pe_x_transposed"), sem("xT_high"), sem("xT_low")
        pe_qkv, a_qc, v_qc = sem("pe_latents"), sem("qc_high"), sem("qc_low")
        a_ss, v_kvn = sem("kv_squares"), sem("kv_normed")
        pe_kvT, v_kvh, v_kvT = sem("pe_kv_transposed"), sem("kv_high"), sem("kv_low")
        pe_v, a_v = sem("pe_values"), sem("values_ready")
        s_full, s_used = sem("score_bank_filled"), sem("score_bank_used")
        p_sin, p_qk, v_qk, a_qkb = sem("qk_sin_done"), sem("qk_summed_by_gpsimd"), sem("qk_summed_by_vector"), sem("qk_bf16_ready")
        v_sw = sem("qk_swapped")
        v_nm = [sem(f"neg_max_ready{i}") for i in range(2)]
        pe_mT = [sem(f"pe_max_transposed{i}") for i in range(2)]
        v_mT = [sem(f"maxT_ready{i}") for i in range(2)]
        pe_t, a_p = sem("pe_scoresT"), sem("probs_ready")
        pe_pv, a_o = sem("pe_pv"), sem("pv_copied")
        pe_n1 = [sem(f"pe_out_by_token{i}") for i in range(2)]
        v_n1 = [sem(f"out_normed{i}") for i in range(2)]
        pe_n2 = [sem(f"pe_out_transposed{i}") for i in range(2)]
        a_n2 = [sem(f"outT_ready{i}") for i in range(2)]
        pe_w = [sem(f"pe_out_projected{i}") for i in range(2)]
        v_r = [sem(f"residual_added{i}") for i in range(2)]
        v_x1, a_x1h, p_x1l, p_prev = sem("x1_ready"), sem("x1_high"), sem("x1_low"), sem("x1_kept")
        a_ch, p_cl, a_cv = sem("ctx_high"), sem("ctx_low"), sem("ctx_values")
        pe_xc, a_xc = sem("pe_stacks_transposed"), sem("stacks_ready")
        v_x2, x2_st = sem("x2_ready"), sem("x2_stored")
        pe_x2T, a_x2T = sem("pe_x2_transposed"), sem("x2T_ready")
        pe_lg, v_lg = sem("pe_logits"), sem("logits_ready")
        v_var, p_rs = sem("variance_ready"), sem("inverse_root_ready")
        v_ch = sem("vector_chain")
        b2_ld = sem("b2_loaded")
        v_rl, a_re, v_m = sem("shifted_logits"), sem("gate_exp"), sem("choices_ready")
        pe_rank, v_oh, pe_slot = sem("pe_ranks"), sem("onehots_ready"), sem("pe_slots")
        v_te, v_rows = sem("tile_experts_ready"), sem("slot_rows_ready")
        p_ix0, p_ix, p_ixs = sem("first_gather_index_ready"), sem("gather_index_ready"), sem("scatter_index_ready")
        g_ld = [sem(f"slots_gathered{i}") for i in range(2)]
        pe_ft, a_xh, v_xl = sem("pe_slots_transposed"), sem("slots_high"), sem("slots_low")
        pe_h, a_g = sem("pe_hidden"), sem("hidden_act")
        v_ah, v_al = sem("hidden_high"), sem("hidden_low")
        pe_y, v_yt, v_y = sem("pe_expert_out"), sem("expert_biased"), sem("expert_weighted")
        sc_st = sem("scatter_added")
        f_ld = [sem(f"sums_loaded{i}") for i in range(4)]
        v_nb, v_f, a_f, f_st = sem("final_shift_ready"), sem("final_ready"), sem("final_ready_scalar"), sem("out_stored")

        def raw(at, n, rows=P):
            return wraw[0:rows, at:at + n]

        raw_loads = [
            (raw(W_KV, DC * KVR).rearrange("p (c n) -> p c n", c=DC), w_kv.rearrange("(c p) n -> p c n", p=P)),
            (raw(W_Q, DC * QR).rearrange("p (c n) -> p c n", c=DC), w_q.rearrange("(c p) n -> p c n", p=P)),
            (raw(W_QH, H * QK), wq_heads[:, :]),
            (raw(W_KR, DC * H * QK).rearrange("p (c n) -> p c n", c=DC), wk_rope.rearrange("(c p) n -> p c n", p=P)),
            (raw(W_KC, H * QK, KVR), wk_content[:, :]),
            (raw(W_V, D, KVR), wv[:, :])]
        loads = [(tab[:, :], table[:, :]),
                 (wo_sb[:, :, :], wo.rearrange("(c p) n -> p c n", p=P)),
                 (wx_sb[:, :, :], wx.rearrange("(c p) n -> p c n", p=P)),
                 (wg_sb[:, :, :], wg.rearrange("(c p) n -> p c n", p=P)),
                 (g_sb[:, :], g_kv.rearrange("(r a) -> r a", a=1)),
                 (xb_sb[:, :], xb.partition_broadcast(P)), (bg_sb[:, :], bg.partition_broadcast(P)),
                 (b1_sb[:, :], b1t[:, :])]
        N_LOADS, N_RAW = len(loads), len(raw_loads)

        x_rows = x.rearrange("b (t p) d -> p (b t) d", p=P)
        c_rows = ctx_in.rearrange("b (t p) d -> p (b t) d", p=P)
        w_pieces = w_exp.rearrange("n p f -> p n f")
        x2_st_rows = x2_rows[0:TOK, :].rearrange("(t p) d -> p t d", p=P)
        acc_st_rows = acc_rows[0:TOK, :].rearrange("(t p) d -> p t d", p=P)
        out_rows = out.rearrange("b (t p) d -> p (b t) d", p=P)

        def rotated(b, k):
            own = [h for h in range(H // 2) if (h in ADD_VECTOR) == (k in ADD_VECTOR)]
            return v_qk if k in ADD_VECTOR else p_qk, b * len(own) + own.index(k) + 1

        def late(k):
            stage = (k + 1) % 3
            return stage, ((EARLY * PIECES if stage == 0 else 0) + k // 3 + 1) * 16, *LATE[k]

        def each_step(engine, step):
            for i in range(LOOP0):
                step(i, i)
            with engine.Fori(LOOP0, LOOP1) as i:
                step(i, None)
            for i in range(LOOP1, LAST_STEP):
                step(i, i)

        block = stack.enter_context(nc.Block())

        @block.sync
        def _(sp):
            sp.dma_start(x_sb[:, :, :], x_rows[:, 0:TT, :]).then_inc(x_ld, 16)
            sp.dma_start(loads[0][0], loads[0][1]).then_inc(c_ld, 16)
            for dst, src in raw_loads:
                sp.dma_start(dst, src).then_inc(r_ld, 16)
            for dst, src in loads[1:]:
                sp.dma_start(dst, src).then_inc(c_ld, 16)
            sp.wait_ge(c_ms, 1)
            sp.dma_start(x2_rows[TOK:ROWS, :], oP[:, 0, :]).then_inc(x2_st, 16)
            sp.dma_start(acc_rows[TOK:ROWS, :], oP[:, 0, :]).then_inc(x2_st, 16)
            sp.wait_ge(x2_st, 32)

            def load_late(k):
                stage, _, e, j = late(k)
                if k < 2:
                    sp.wait_ge(v_sw, B * H // 2)
                else:
                    sp.wait_ge(w_lo, EARLY * PIECES + k - 1)
                sp.dma_start(wstage[stage].unsqueeze(1), w_pieces[:, e * PIECES + j:e * PIECES + j + 1, :]).then_inc(w_ld[stage], 16)

            def step(i, i0):
                if i0 is None or 1 <= i0 < B:
                    sp.wait_ge(pe_xT, i)
                    sp.dma_start(x_sb[:, :, :], x_rows[:, bass.ds(i * TT, TT), :]).then_inc(x_ld, 16)
                if i0 is None or 1 <= i0 <= B:
                    c = i - 1
                    sp.wait_ge(a_cv, i)
                    sp.wait_ge(p_cl, i)
                    sp.dma_start(ctx_raw[:, :, :], c_rows[:, bass.ds(c * TT, TT), :]).then_inc(ctx_ld, 16)
                for u, k in units(i0):
                    if u == "late_high":
                        load_late(k)
                for j in range(PIECES if i0 is None else 0):
                    p = i * PIECES + (j - LOOP0 * PIECES)
                    sp.wait_ge(w_lo, p + 1)
                    sp.dma_start(wstage[0].unsqueeze(1), w_pieces[:, bass.ds(p, 1), :]).then_inc(w_ld[0], 16)
                if i0 is None or i0 < B:
                    sp.wait_ge(v_r[0], i + 1)
                    sp.dma_start(x_res[:, :, :], x_rows[:, bass.ds(i * TT, TT), :]).then_inc(xr_ld, 16)

            each_step(sp, step)
            sp.dma_start(b2_sb, b2.rearrange("e d -> (e d)").partition_broadcast(P)).then_inc(b2_ld, 16)
            sp.wait_ge(sc_st, 16 * N_TILES)
            for k in range(4):
                sp.dma_start(fin[:, 4 * k:4 * k + 4, :], acc_st_rows[:, 4 * k:4 * k + 4, :]).then_inc(f_ld[k], 16)
            for k in range(4):
                sp.wait_ge(v_f, k + 1)
                sp.wait_ge(a_f, k + 1)
                sp.dma_start(out_rows[:, 4 * k:4 * k + 4, :], fin[:, 4 * k:4 * k + 4, :]).then_inc(f_st, 16)
            sp.wait_ge(f_st, 64)

        @block.gpsimd
        def _(pool):
            nc.gpsimd.memset(minus_half[:, :], -0.5)
            nc.gpsimd.memset(oP[:, 0, :], 0.0)
            nc.gpsimd.memset(x1s[:, :, :, 3 * HD:], 0.0)
            nc.gpsimd.memset(cs[:, :, :, 3 * HD:], 0.0)
            nc.gpsimd.memset(v_sb[:, :, :, :], 1.0)
            nc.gpsimd.memset(c_sb[:, :, :, :], 1.0).then_inc(c_ms, 1)
            nc.gpsimd.memset(rec[:, 0, 0:1], 0.0).then_inc(p_cl, 1)
            pool.wait_ge(c_ld, 16 * N_LOADS)
            roots = {"n": 0, "base": 0}

            def inverse_root(value):
                roots["n"] += 1
                pool.wait_ge(v_var, roots["base"] + roots["n"])
                nc.gpsimd.tensor_tensor(value, value, minus_half[:, 0:value.shape[1]], ALU.pow).then_inc(p_rs, 1)

            def step(i, i0):
                if i0 is None:
                    start, roots["base"], roots["n"] = roots["n"], i * 3 + (roots["n"] - 3 * LOOP0), 0
                for u, k in units(i0):
                    b = i - BEHIND[u]
                    if u == "latents_root":
                        inverse_root(rs[:, :])
                    elif u == "rot":
                        pool.wait_ge(v_sw, b * (H // 2) + k + 1)
                        nc.gpsimd.tensor_tensor(
                            swap[k % 3][:, :, :], swap[k % 3][:, :, :],
                            tab[:, C_SIN:C_SIN + T].unsqueeze(1).broadcast_to([P, 2, T]), ALU.mult).then_inc(p_sin, 1)
                        if k not in ADD_VECTOR:
                            pool.wait_ge(p_sin, b * (H // 2) + k + 1)
                            nc.gpsimd.tensor_tensor(qk[:, k, :, :], qk[:, k, :, :], swap[k % 3][:, :, :], ALU.add).then_inc(p_qk, 1)
                    elif u in ("self_root", "cross_root"):
                        inverse_root(rstd[:, :])
                    elif u == "self_scale":
                        pool.wait_ge(v_x1, b + 1)
                        pool.wait_ge(a_x1h, b + 1)
                        nc.gpsimd.tensor_tensor(
                            x1s[:, :, :, HD:2 * HD].rearrange("p t h d -> p (t h) d"),
                            x1[:, :, :].rearrange("p t (h d) -> p (t h) d", d=HD),
                            x1s[:, :, :, 0:HD].rearrange("p t h d -> p (t h) d"), ALU.subtract).then_inc(p_x1l, 1)
                    elif u == "context":
                        pool.wait_ge(a_ch, b + 1)
                        nc.gpsimd.tensor_tensor(
                            cs[:, :, :, 2 * HD:3 * HD].rearrange("p t h d -> p (t h) d"),
                            ctx_raw[:, :, :].rearrange("p t (h d) -> p (t h) d", d=HD),
                            cs[:, :, :, 0:HD].rearrange("p t h d -> p (t h) d"), ALU.subtract).then_inc(p_cl, 1)
                    elif u == "keep":
                        if i0 is None or before("cross_out", i, (u, k)):
                            pool.wait_ge(v_r[1], i - 2)
                        nc.gpsimd.tensor_tensor(x1_prev[:, :, :], x1[:, :, :], xb_sb[:, :].unsqueeze(1).broadcast_to([P, TT, D]),
                                                ALU.add).then_inc(p_prev, 1)
                if i0 is None:
                    assert roots["n"] == 3
                    roots["n"], roots["base"] = start + 3 * (LOOP1 - LOOP0), 0

            each_step(pool, step)
            pool.wait_ge(v_rows, 1)

            def gather(n, u, gate):
                if gate is not None:
                    pool.wait_ge(pe_ft, gate)
                first = gate is None
                nc.gpsimd.tensor_copy(idx_g[u][:, :], slot_row[:, bass.ds(n, 1)]).then_inc(p_ix0 if first else p_ix, 1)
                pool.wait_ge(x2_st, 32 * (B + 1))
                pool.wait_ge(p_ix0 if first else p_ix, n + 1 if first else gate)
                nc.gpsimd.indirect_dma_start(
                    out=xg[u], out_offset=None, in_=x2_rows[:, :],
                    in_offset=bass.IndirectOffsetOnAxis(ap=idx_g[u][:, 0:1], axis=0)).then_inc(g_ld[u], 16)

            def scatter(n, u, after):
                pool.wait_ge(v_y, n + 1)
                if after is not None:
                    pool.wait_ge(sc_st, after)
                nc.gpsimd.tensor_copy(idx_s[u][:, :], slot_row[:, bass.ds(n, 1)]).then_inc(p_ixs, 1)
                pool.wait_ge(x2_st, 32 * (B + 1))
                pool.wait_ge(p_ixs, n + 1)
                nc.gpsimd.indirect_dma_start(
                    out=acc_rows[:, :], out_offset=bass.IndirectOffsetOnAxis(ap=idx_s[u][:, 0:1], axis=0),
                    in_=yb[u], in_offset=None, compute_op=ALU.add).then_inc(sc_st, 16)

            gather(0, 0, None)
            gather(1, 1, None)
            gather(2, 0, 1)
            gather(3, 1, 2)
            scatter(0, 0, None)
            with pool.Fori(0, (N_TILES - 5) // 2) as j:
                for u in range(2):
                    gather(j * 2 + 4 + u, u, j * 2 + 3 + u)
                    scatter(j * 2 + 1 + u, (1 + u) % 2, (j * 2 + 1 + u) * 16)
            gather(N_TILES - 1, 0, N_TILES - 2)
            for n in range(N_TILES - 4, N_TILES):
                scatter(n, n % 2, 16 * n)
            pool.wait_ge(sc_st, 16 * N_TILES)
            for k in range(4):
                inverse_root(frs[:, 4 * k:4 * k + 4])

        @block.scalar
        def _(act_e):
            act_e.wait_ge(r_ld, 16 * N_RAW)
            for at, end in W_RAW:
                rows = KVR if at == W_KC else P
                nc.scalar.activation(wph[0:rows, at:end], wraw[0:rows, at:end], ACT.Copy, scale=W_SCALE).then_inc(pw_hi, 1)
            act_e.wait_ge(c_ld, 16 * N_LOADS)
            act_e.wait_ge(c_ms, 1)
            act_e.wait_ge(pw_lo, 3)
            act_e.wait_ge(x2_st, 32)

            def split_high(stage, loaded, e, j):
                act_e.wait_ge(w_ld[stage], loaded)
                nc.scalar.activation(piece_parts(e, j)[0], staged(wstage[stage], j), ACT.Copy, scale=W_SCALE).then_inc(w_hi, 1)

            def by_head(a):
                return a.rearrange("p t (h d) -> p (t h) d", d=HD)

            def part(a, n):
                return a[:, :, :, n * HD:(n + 1) * HD].rearrange("p t h d -> p (t h) d")

            def step(i, i0):
                for u, k in units(i0):
                    b = i - BEHIND[u]
                    if u == "x_transpose":
                        act_e.wait_ge(pe_xT, b + 1)
                        nc.scalar.activation(xTh.rearrange("p c t -> p (c t)"), ps_m[0][:, :], ACT.Copy).then_inc(a_xT, 1)
                    elif u == "latents":
                        act_e.wait_ge(pe_qkv, b + 1)
                        for t in range(TT):
                            if t:
                                act_e.wait_ge(a_ss, b * TT + t)
                            nc.scalar.activation(sq[:, :], ps_m[0][:, t * KVR:(t + 1) * KVR], ACT.Square, scale=1.0 / W_SCALE,
                                                 accum_out=ss[:, t:t + 1]).then_inc(a_ss, 1)
                        nc.scalar.activation(qch[:, :], ps_m[1][:, 0:T], ACT.Copy, scale=1.0 / W_SCALE).then_inc(a_qc, 1)
                    elif u == "values":
                        act_e.wait_ge(pe_v, b + 1)
                        nc.scalar.activation(part(v_sb, 0), ps_m[1][:, :].rearrange("p (s d) -> p s d", d=HD), ACT.Copy,
                                             scale=1.0 / W_SCALE).then_inc(a_v, 1)
                    elif u == "cast":
                        act_e.wait_ge(*rotated(b, k))
                        nc.scalar.activation(qk_b[:, k, :, :], qk[:, k, :, :], ACT.Copy).then_inc(a_qkb, 1)
                    elif u == "self_scale":
                        act_e.wait_ge(v_x1, b + 1)
                        nc.scalar.activation(part(x1s, 2), by_head(x1[:, :, :]), ACT.Copy)
                        nc.scalar.activation(part(x1s, 0), by_head(x1[:, :, :]), ACT.Copy).then_inc(a_x1h, 1)
                    elif u == "context":
                        act_e.wait_ge(ctx_ld, b * 16 + 16)
                        nc.scalar.activation(part(cs, 1), by_head(ctx_raw[:, :, :]), ACT.Copy)
                        nc.scalar.activation(part(cs, 0), by_head(ctx_raw[:, :, :]), ACT.Copy).then_inc(a_ch, 1)
                    elif u == "values_in":
                        if i0 is None or before("cross_pv", i, (u, k)):
                            act_e.wait_ge(pe_pv, before(PV, i, (u, k)))
                        nc.scalar.activation(part(c_sb, 0), by_head(ctx_raw[:, :, :]), ACT.Copy).then_inc(a_cv, 1)
                    elif u in ("cross_exp", "self_exp"):
                        cross = u == "cross_exp"
                        at = before(EXP, i, (u, k))
                        act_e.wait_ge(pe_t, at + 1)
                        if k % 4 == 0 and (i0 is None or at):
                            act_e.wait_ge(pe_pv, before(EXP, i, (u, k), per=4))
                        cols = 2 * T if cross else 3 * P
                        nc.scalar.activation(probs[:, k % 4, 0:cols], ps_t[k % 2][:, 0:cols], ACT.Exp,
                                             scale=CROSS_SCALE if cross else SELF_SCALE).then_inc(a_p, 1)
                    elif u == "split_high":
                        split_high(0, (i * PIECES + (k + 1 - LOOP0 * PIECES)) * 16, i - LOOP0, k)
                    elif u == "late_high":
                        split_high(*late(k))
                    elif u in ("cross_pv", "self_pv"):
                        act_e.wait_ge(pe_pv, before(PV, i, (u, k)) + 1)
                        other = 0 if u == "cross_pv" else 1
                        n_other = before(("self_norm", "cross_norm")[other], i, (u, k))
                        if k == 0 and (i0 is None or n_other):
                            act_e.wait_ge(pe_n1[other], n_other)
                        nc.scalar.activation(oP[:, k, :], ps_o[k % 2][:, 0:T], ACT.Copy).then_inc(a_o, 1)
                    elif u == "stack_transpose":
                        act_e.wait_ge(pe_xc, b * 4 + k + 1)
                        nc.scalar.activation(xc[:, 2 * k:2 * k + 2, :, :].rearrange("p g a t -> p (g a t)"), ps_sh[k % 2],
                                             ACT.Copy).then_inc(a_xc, 1)
                    elif u in ("self_back", "cross_back"):
                        a = 0 if u == "self_back" else 1
                        act_e.wait_ge(pe_n2[a], b + 1)
                        nc.scalar.activation(oT[:, :, :].rearrange("p c t -> p (c t)"), ps_m[0][:, :], ACT.Copy).then_inc(a_n2[a], 1)
                    elif u == "x2_transpose":
                        act_e.wait_ge(pe_x2T, b + 1)
                        nc.scalar.activation(x2T[:, :, :].rearrange("p c t -> p (c t)"), ps_m[0][:, :], ACT.Copy).then_inc(a_x2T, 1)
                        act_e.wait_ge(v_x2, b + 1)
                        rows = bass.ds(b * TT, TT)
                        act_e.dma_start(x2_st_rows[:, rows, :], x2[:, :, :]).then_inc(x2_st, 16)
                        act_e.dma_start(acc_st_rows[:, rows, :], x2[:, :, :]).then_inc(x2_st, 16)

            each_step(act_e, step)

            act_e.wait_ge(v_rl, 1)
            nc.scalar.activation(rt[1], rt[0], ACT.Exp).then_inc(a_re, 1)
            act_e.wait_ge(v_te, 1)

            def slots_high(n, u):
                act_e.wait_ge(pe_ft, n + 1)
                nc.scalar.activation(xh[u].rearrange("p c t -> p (c t)"), bank[u][:, 0:D], ACT.Copy).then_inc(a_xh, 1)

            def hidden(n, u, e, half):
                act_e.wait_ge(pe_h, n * 2 + half + 1)
                for f in range(4 * half, 4 * half + 4):
                    last = nc.scalar.activation(
                        act[:, u, f, :], bank[2 + 2 * u + half][:, (f % 4) * P:(f % 4 + 1) * P], ACT.Gelu,
                        bias=b1_sb[:, bass.ds(e * FC + f, 1)], scale=1.0 / W_SCALE)
                last.then_inc(a_g, 1)

            def tile(n, u, split, following=True):
                e = act_e.value_load(tile_e[0:1, bass.ds(n, 1)], min_val=0, max_val=E - 1)
                if split is not None:
                    act_e.wait_ge(v_al, split)
                hidden(n, u, e, 0)
                if following:
                    slots_high(n + 1, 1 - u)
                hidden(n, u, e, 1)

            slots_high(0, 0)
            slots_high(1, 1)
            tile(0, 0, None, False)
            tile(1, 1, None)
            tile(2, 0, 2)
            with act_e.Fori(0, (N_TILES - 5) // 2) as j:
                for u in range(2):
                    tile(j * 2 + 3 + u, (1 + u) % 2, j * 4 + 2 * u + 4)
            tile(N_TILES - 2, 1, 2 * (N_TILES - 3))
            tile(N_TILES - 1, 0, 2 * (N_TILES - 2), False)
            for k in range(4):
                act_e.wait_ge(v_nb, k + 1)
                for t in range(4 * k + 2, 4 * k + 4):
                    last = nc.scalar.activation(fin[:, t, :], fin[:, t, :], ACT.Identity, bias=fnb[:, t:t + 1], scale=frs[:, t:t + 1])
                last.then_inc(a_f, 1)

        @block.vector
        def _(dve):
            chain = {"n": 0, "base": 0}
            roots = {"n": 0, "base": 0}

            def link(ins, plain=False):
                chain["n"] += 1
                ins.then_inc(v_ch, 1)
                dve.wait_ge(v_ch, chain["base"] + chain["n"])
                if plain:
                    nc.vector.memset(spare[:, 0:1], 0.0)

            def inverse_root(ins):
                roots["n"] += 1
                ins.then_inc(v_var, 1)

            def root_ready():
                dve.wait_ge(p_rs, roots["base"] + roots["n"])

            nc.vector.memset(ones_b[:, :], 1.0)
            for m in negm:
                nc.vector.memset(m[:, :, :], 0.0)
            nc.vector.memset(rs[:, :], 0.0).then_inc(v_r[0], 1)
            nc.vector.memset(rstd[:, :], 0.0).then_inc(v_lg, 1)
            nc.vector.memset(mx2[:, :], 0.0).then_inc(w_lo, 1)
            link(nc.vector.memset(mx[:, :, :], 0.0))
            nc.vector.memset(mxc[:, :, :], 0.0).then_inc(a_cv, 1)
            dve.wait_ge(c_ld, 16 * N_LOADS)
            nc.vector.tensor_copy(ident_b[:, :], ident)
            nc.vector.tensor_copy(ident_h[:, :], ident)
            nc.vector.tensor_copy(mask_b[:, :], tab[:, C_MASK:C_MASK + P])
            nc.vector.tensor_copy(maskt_b[:, :], tab[:, C_MASKT:C_MASKT + P])
            nc.vector.tensor_copy(up_b[:, :], tab[:, C_UP:C_UP + P]).then_inc(c_bf, 1)
            for n, (at, end) in enumerate(W_RAW):
                dve.wait_ge(pw_hi, n + 1)
                rows = KVR if at == W_KC else P
                nc.vector.scalar_tensor_tensor(wpl[0:rows, at:end], wraw[0:rows, at:end], W_SCALE, wph[0:rows, at:end],
                                               ALU.mult, ALU.subtract).then_inc(pw_lo, 1)
            dve.wait_ge(pw_lo, 3)

            def split_low(stage, done, e, j):
                dve.wait_ge(w_hi, done)
                hi, lo = piece_parts(e, j)
                nc.vector.scalar_tensor_tensor(lo, staged(wstage[stage], j), W_SCALE, hi, ALU.mult, ALU.subtract).then_inc(w_lo, 1)

            def layer_norm(a):
                for t in range(TT):
                    last = nc.vector.bn_stats(stats[:, t, :], a[:, t, :])
                link(last, plain=True)
                for t in range(TT):
                    last = nc.vector.bn_aggr(mv[:, t, :], stats[:, t, :])
                link(last)
                inverse_root(nc.vector.tensor_scalar(rstd[:, :], mv[:, :, 1], LN_EPS, None, ALU.add))

            def layer_norm_scale(a, done):
                root_ready()
                for t in range(TT):
                    last = nc.vector.tensor_scalar(a[:, t, :], a[:, t, :], mv[:, t, 0:1], rstd[:, t:t + 1],
                                                   ALU.subtract, ALU.mult)
                last.then_inc(done, 1)

            def normalise(a, b):
                dve.wait_ge(pe_n1[a], b + 1)
                for t in range(TT):
                    o = ps_m[t][:, :].rearrange("p (h d) -> p h d", d=32)
                    last = nc.vector.reciprocal(rec[:, t, :], o[:, :, HD])
                link(last)
                for t in range(TT):
                    o = ps_m[t][:, :].rearrange("p (h d) -> p h d", d=32)
                    last = nc.vector.tensor_tensor(o_tok[:, t, :].rearrange("p (h d) -> p h d", d=HD), o[:, :, 0:HD],
                                                   rec[:, t, :].unsqueeze(2).broadcast_to([P, H, HD]), ALU.mult)
                last.then_inc(v_n1[a], 1)

            def max_transposed(a, b):
                dve.wait_ge(pe_mT[a], b + 1)
                nc.vector.tensor_copy(mT[a][:, :], ps_max[a][:, 0:T // 2].bitcast(BF16)).then_inc(v_mT[a], 1)

            VCH, VROOT = 7, 3

            def step(i, i0):
                if i0 is None:
                    chain0, roots0 = chain["n"], roots["n"]
                    chain["base"], chain["n"] = i * VCH + (chain0 - VCH * LOOP0), 0
                    roots["base"], roots["n"] = i * VROOT + (roots0 - VROOT * LOOP0), 0
                for u, k in units(i0):
                    b = i - BEHIND[u]
                    if u == "x_transpose":
                        dve.wait_ge(a_xT, b + 1)
                        nc.vector.tensor_tensor(xTl.rearrange("p c t -> p (c t)"), ps_m[0][:, :],
                                                xTh.rearrange("p c t -> p (c t)"), ALU.subtract).then_inc(v_xT, 1)
                    elif u == "latents":
                        dve.wait_ge(a_ss, b * TT + TT)
                        inverse_root(nc.vector.tensor_scalar(rs[:, :], ss[:, :], 1.0 / KVR, RMS_EPS, ALU.mult, ALU.add))
                    elif u == "latents_scale":
                        root_ready()
                        for t in range(TT):
                            last = nc.vector.tensor_scalar(kvn[:, t, :], ps_m[0][:, t * KVR:(t + 1) * KVR], rs[:, t:t + 1],
                                                           1.0 / W_SCALE, ALU.mult, ALU.mult)
                        last.then_inc(v_kvn, 1)
                        dve.wait_ge(a_qc, b + 1)
                        nc.vector.scalar_tensor_tensor(qcl[:, :], ps_m[1][:, 0:T], 1.0 / W_SCALE, qch[:, :], ALU.mult,
                                                       ALU.subtract).then_inc(v_qc, 1)
                    elif u == "kv_transpose":
                        dve.wait_ge(pe_kvT, b + 1)
                        nc.vector.tensor_scalar(kvh[:, :], ps_m[0][0:KVR, 0:T], g_sb[:, 0:1], None, ALU.mult).then_inc(v_kvh, 1)
                        dve.wait_ge(v_kvh, b + 1)
                        nc.vector.scalar_tensor_tensor(kvl[:, :], ps_m[0][0:KVR, 0:T], g_sb[:, 0:1], kvh[:, :], ALU.mult,
                                                       ALU.subtract).then_inc(v_kvT, 1)
                    elif u == "qk":
                        if k >= 3:
                            dve.wait_ge(*rotated(b, k - 3))
                        dve.wait_ge(s_full, before(FULL, i, (u, k)) + 1)
                        nc.vector.tensor_tensor(qk[:, k, :, :], ps_qk[k][:, :].rearrange("p (a t) -> p a t", a=2),
                                                tab[:, C_COS:C_COS + T].unsqueeze(1).broadcast_to([P, 2, T]), ALU.mult)
                        nc.vector.stream_shuffle(swap[k % 3][:, :, :].rearrange("p a t -> p (a t)"), ps_qk[k][:, :],
                                                 [(j + 16) % 32 for j in range(32)]).then_inc(v_sw, 1)
                    elif u == "add":
                        if k in ADD_VECTOR:
                            dve.wait_ge(p_sin, b * (H // 2) + k + 1)
                            nc.vector.tensor_tensor(qk[:, k, :, :], qk[:, k, :, :], swap[k % 3][:, :, :], ALU.add).then_inc(v_qk, 1)
                    elif u == "self_max":
                        dve.wait_ge(s_full, before(FULL, i, (u, k)) + 1)
                        nc.vector.tensor_reduce(mx[:, k, :], ps_s[k % 2][:, 0:3 * P].rearrange("p (a k) -> p a k", a=3),
                                                axis=AX.X, op=ALU.max).then_inc(s_used, 1)
                    elif u == "split_low":
                        split_low(0, i * PIECES + (k + 1 - LOOP0 * PIECES), i - LOOP0, k)
                    elif u == "late_low":
                        stage, _, e, j = late(k)
                        split_low(stage, EARLY * PIECES + k + 1, e, j)
                    elif u == "self_maxT":
                        dve.wait_ge(s_used, before(MAX, i, (u, k)))
                        nm = negm[0][:, :, :].rearrange("p t (a n) -> p t a n", a=2)[:, :, :, 0:H // 2]
                        nc.vector.tensor_scalar(nm[:, 0], mx[:, :, 0].rearrange("p (n a) -> p a n", a=2), -1.0, None, ALU.mult)
                        link(nc.vector.tensor_tensor(mx2[:, :], mx[:, :, 1], mx[:, :, 2], ALU.max))
                        nc.vector.tensor_scalar(nm[:, 1], mx2[:, :].rearrange("p (n a) -> p a n", a=2), -1.0, None,
                                                ALU.mult).then_inc(v_nm[0], 1)
                        max_transposed(0, b)
                    elif u == "self_norm":
                        normalise(0, b)
                    elif u == "cross_divide":
                        normalise(1, b)
                    elif u == "self_out":
                        dve.wait_ge(pe_w[0], b + 1)
                        dve.wait_ge(xr_ld, b * 16 + 16)
                        if i0 is None or b >= 1:
                            dve.wait_ge(p_prev, b)
                        nc.vector.tensor_tensor(x1[:, :, :].rearrange("p t d -> p (t d)"), ps_m[1][:, :],
                                                x_res[:, :, :].rearrange("p t d -> p (t d)"), ALU.add).then_inc(v_r[0], 1)
                        dve.wait_ge(v_r[0], b + 2)
                        layer_norm(x1)
                    elif u == "self_scale":
                        layer_norm_scale(x1, v_x1)
                    elif u == "cross_max":
                        dve.wait_ge(s_full, before(FULL, i, (u, k)) + 1)
                        nc.vector.tensor_reduce(mxc[:, k, :], ps_s[k % 2][:, :].rearrange("p (a k) -> p a k", a=2),
                                                axis=AX.X, op=ALU.max).then_inc(s_used, 1)
                    elif u == "cross_maxT":
                        dve.wait_ge(s_used, before(MAX, i, (u, k)))
                        nm = negm[1][:, :, :].rearrange("p t (a n) -> p t a n", a=2)[:, :, :, 0:H // 2]
                        for t in range(TT):
                            last = nc.vector.tensor_scalar(nm[:, t], mxc[:, :, t].rearrange("p (n a) -> p a n", a=2), -1.0,
                                                           None, ALU.mult)
                        last.then_inc(v_nm[1], 1)
                        max_transposed(1, b)
                    elif u == "cross_out":
                        dve.wait_ge(pe_w[1], b + 1)
                        dve.wait_ge(x2_st, b * 32 + 32)
                        dve.wait_ge(p_prev, b + 1)
                        nc.vector.tensor_tensor(x2[:, :, :].rearrange("p t d -> p (t d)"), ps_m[1][:, :],
                                                x1_prev[:, :, :].rearrange("p t d -> p (t d)"), ALU.add).then_inc(v_r[1], 1)
                        dve.wait_ge(v_r[1], b + 1)
                        layer_norm(x2)
                    elif u == "cross_scale":
                        layer_norm_scale(x2, v_x2)
                    elif u == "logits":
                        dve.wait_ge(pe_lg, b + 1)
                        nc.vector.tensor_tensor(logits[:, bass.ds(b * TT, TT), :],
                                                ps_m[1][:, 0:TT * E].rearrange("p (t e) -> p t e", e=E),
                                                bg_sb[:, :].unsqueeze(1).broadcast_to([P, TT, E]), ALU.add).then_inc(v_lg, 1)
                if i0 is None:
                    assert (chain["n"], roots["n"]) == (VCH, VROOT), (chain, roots)
                    chain["n"], chain["base"] = chain0 + VCH * (LOOP1 - LOOP0), 0
                    roots["n"], roots["base"] = roots0 + VROOT * (LOOP1 - LOOP0), 0

            each_step(dve, step)

            def over_e(a):
                return a[:, :].unsqueeze(2).broadcast_to([P, NT, E])

            def tab_e(col):
                return tab[:, col:col + E].unsqueeze(1).broadcast_to([P, NT, E])

            dve.wait_ge(v_lg, B + 1)
            top, total, best1, best2 = rs1[0], rs1[1], rs1[2], rs1[3]
            link(nc.vector.tensor_reduce(top[:, :], logits[:, :, :], axis=AX.X, op=ALU.max))
            nc.vector.tensor_tensor(rt[0], logits[:, :, :], over_e(top), ALU.subtract).then_inc(v_rl, 1)
            dve.wait_ge(a_re, 1)
            link(nc.vector.tensor_reduce(total[:, :], rt[1], axis=AX.X, op=ALU.add))
            prob = rt[2]
            link(nc.vector.reciprocal(total[:, :], total[:, :]))
            link(nc.vector.tensor_tensor(prob, rt[1], over_e(total), ALU.mult))

            def choose(src, best, rank, onehot, tmp):
                link(nc.vector.tensor_reduce(best[:, :], src, axis=AX.X, op=ALU.max))
                link(nc.vector.tensor_tensor(tmp, src, over_e(best), ALU.is_equal))
                link(nc.vector.tensor_tensor(tmp, tmp, tab_e(C_REV), ALU.mult))
                link(nc.vector.tensor_reduce(rank[:, :], tmp, axis=AX.X, op=ALU.max))
                link(nc.vector.tensor_tensor(onehot, tmp, over_e(rank), ALU.is_equal))

            first, second = rt[4], rt[5]
            choose(prob, best1, rs1[4], first, rt[3])
            rest = rt[6]
            link(nc.vector.scalar_tensor_tensor(rest.rearrange("p t e -> p (t e)"),
                                                first.rearrange("p t e -> p (t e)"), -2.0,
                                                prob.rearrange("p t e -> p (t e)"), ALU.mult, ALU.add))
            choose(rest, best2, rs1[5], second, rt[3])
            nc.vector.tensor_tensor(m_b[:, :, :], first, second, ALU.add).then_inc(v_m, 1)
            link(nc.vector.tensor_tensor(rs1[6][:, :], best1[:, :], best2[:, :], ALU.add))
            weight = [rs1[7], rs1[4]]
            link(nc.vector.reciprocal(rs1[6][:, :], rs1[6][:, :]))
            link(nc.vector.tensor_tensor(weight[0][:, :], best1[:, :], rs1[6][:, :], ALU.mult))
            link(nc.vector.tensor_tensor(weight[1][:, :], best2[:, :], rs1[6][:, :], ALU.mult))

            dve.wait_ge(pe_rank, 1)
            count, tiles, start, end = ex[0], ex[1], ex[2], ex[3]
            link(nc.vector.tensor_copy(count[:, :], bank[1][:, 0:E]))
            over = ltmp.rearrange("p (e k) -> p e k", e=E)
            link(nc.vector.tensor_tensor(over, count[:, :].unsqueeze(2).broadcast_to([P, E, NT]),
                                         tab[:, C_CNT:C_CNT + NT].unsqueeze(1).broadcast_to([P, E, NT]), ALU.is_gt))
            link(nc.vector.tensor_reduce(tiles[:, :], over, axis=AX.X, op=ALU.add))
            earlier = ltmp[:, 0:E * E].rearrange("p (e k) -> p e k", e=E)
            link(nc.vector.tensor_tensor(earlier, tiles[:, :].unsqueeze(1).broadcast_to([P, E, E]),
                                         tab[:, C_LT:C_LT + E * E].rearrange("p (e k) -> p e k", e=E), ALU.mult))
            link(nc.vector.tensor_reduce(start[:, :], earlier, axis=AX.X, op=ALU.add))
            link(nc.vector.tensor_tensor(end[:, :], start[:, :], tiles[:, :], ALU.add))
            link(nc.vector.tensor_tensor(ttmp,
                                         tab[:, C_TILE:C_TILE + N_TILES].unsqueeze(2).broadcast_to([P, N_TILES, E]),
                                         end[:, :].unsqueeze(1).broadcast_to([P, N_TILES, E]), ALU.is_ge))
            link(nc.vector.tensor_reduce(slot_t[0][:, :], ttmp, axis=AX.X, op=ALU.add))
            nc.vector.tensor_scalar(tile_e[:, :], slot_t[0][:, :], float(E - 1), None, ALU.min).then_inc(v_te, 1)
            rank = rt[0]
            link(nc.vector.tensor_copy(rank.rearrange("p t e -> p (t e)"), bank[0][:, 0:NT * E]))
            rtile = rt[1]
            link(nc.vector.tensor_scalar(rtile, rank, 1.0 / P, 0.5 / P - 0.5, ALU.mult, ALU.add))
            link(nc.vector.tensor_scalar(rtile, rtile, 1.5 * 2.0 ** 23, None, ALU.add))
            link(nc.vector.tensor_scalar(rtile, rtile, -1.5 * 2.0 ** 23, None, ALU.add))
            lane = rt[2]
            link(nc.vector.scalar_tensor_tensor(lane.rearrange("p t e -> p (t e)"),
                                                rtile.rearrange("p t e -> p (t e)"), -float(P),
                                                rank.rearrange("p t e -> p (t e)"), ALU.mult, ALU.add))
            link(nc.vector.tensor_tensor(rtile, rtile,
                                         start[:, :].unsqueeze(1).broadcast_to([P, NT, E]), ALU.add))
            lanes, tilenos = [rs1[0], rs1[1]], [rs1[2], rs1[3]]
            for k, onehot in enumerate((first, second)):
                for src, dst in ((lane, lanes[k]), (rtile, tilenos[k])):
                    link(nc.vector.tensor_tensor(rt[3], src, onehot, ALU.mult))
                    link(nc.vector.tensor_reduce(dst[:, :], rt[3], axis=AX.X, op=ALU.add))
            for k in range(2):
                nc.vector.tensor_copy(values[:, k, :, 0], tab[:, C_TOK1:C_TOK1 + NT])
                last = nc.vector.tensor_copy(values[:, k, :, 1], weight[k][:, :])
            link(last)
            for s in range(2 * NT // OH):
                k, t = divmod(s * OH, NT)
                if s >= 2:
                    dve.wait_ge(pe_slot, s - 1)
                nc.vector.tensor_tensor(oh_lane[s % 2], tab[:, C_LANE:C_LANE + P].unsqueeze(1).broadcast_to([P, OH, P]),
                                        lanes[k][:, t:t + OH].unsqueeze(2).broadcast_to([P, OH, P]), ALU.is_equal)
                link(nc.vector.tensor_tensor(oh_eq[s % 2], tab[:, C_TILE:C_TILE + N_TILES].unsqueeze(1).broadcast_to([P, OH, N_TILES]),
                                             tilenos[k][:, t:t + OH].unsqueeze(2).broadcast_to([P, OH, N_TILES]), ALU.is_equal))
                nc.vector.tensor_tensor(oh_tile[s % 2], oh_eq[s % 2].unsqueeze(2).broadcast_to([P, OH, 2, N_TILES]),
                                        values[:, k, t:t + OH, :].unsqueeze(3).broadcast_to([P, OH, 2, N_TILES]),
                                        ALU.mult).then_inc(v_oh, 1)
            dve.wait_ge(pe_slot, 2 * NT // OH)
            link(nc.vector.tensor_copy(slot_t[0][:, :], bank[2][:, 0:N_TILES]))
            link(nc.vector.tensor_copy(slot_w[:, :], bank[2][:, N_TILES:2 * N_TILES]))
            link(nc.vector.tensor_scalar(slot_t[1][:, :], slot_t[0][:, :], 0.0, tab[:, C_DUMMY:C_DUMMY + 1],
                                         ALU.is_equal, ALU.mult))
            link(nc.vector.tensor_tensor(slot_t[2][:, :], slot_t[0][:, :], slot_t[1][:, :], ALU.add))
            nc.vector.tensor_scalar(slot_row[:, :], slot_t[2][:, :], -1.0, None, ALU.add).then_inc(v_rows, 1)
            dve.wait_ge(v_rows, 1)

            def low_slots(n, u):
                dve.wait_ge(a_xh, n + 1)
                nc.vector.tensor_tensor(xl[u].rearrange("p c t -> p (c t)"), bank[u][:, 0:D],
                                        xh[u].rearrange("p c t -> p (c t)"), ALU.subtract).then_inc(v_xl, 1)

            def split_hidden(n, u, half):
                dve.wait_ge(a_g, n * 2 + half + 1)
                at = slice(4 * half, 4 * half + 4)
                nc.vector.tensor_copy(ah[:, u, at, :], act[:, u, at, :]).then_inc(v_ah, 1)
                dve.wait_ge(v_ah, n * 2 + half + 1)
                nc.vector.tensor_tensor(al[:, u, at, :], act[:, u, at, :], ah[:, u, at, :], ALU.subtract).then_inc(v_al, 1)

            def weigh(n, u, after):
                e = dve.value_load(tile_e[0:1, bass.ds(n, 1)], min_val=0, max_val=E - 1)
                dve.wait_ge(pe_y, n + 1)
                if after is not None:
                    dve.wait_ge(sc_st, after)
                nc.vector.scalar_tensor_tensor(yb[u], bank[6 + u][:, 0:D], 1.0 / W_SCALE,
                                               b2_sb[:, bass.ds(e * D, D)], ALU.mult, ALU.add).then_inc(v_yt, 1)
                dve.wait_ge(v_yt, n * 2 + 1)
                nc.vector.scalar_tensor_tensor(yb[u], bank[6 + u][:, D:2 * D], 1.0 / W_SCALE, yb[u],
                                               ALU.mult, ALU.add).then_inc(v_yt, 1)
                dve.wait_ge(v_yt, n * 2 + 2)
                nc.vector.tensor_scalar(yb[u], yb[u], slot_w[:, bass.ds(n, 1)], None, ALU.mult).then_inc(v_y, 1)

            def tile(n, u, following=True):
                split_hidden(n, u, 0)
                if following:
                    low_slots(n + 1, 1 - u)
                split_hidden(n, u, 1)

            dve.wait_ge(b2_ld, 16)
            low_slots(0, 0)
            low_slots(1, 1)
            tile(0, 0, False)
            tile(1, 1)
            weigh(0, 0, None)
            tile(2, 0)
            weigh(1, 1, None)
            with dve.Fori(0, (N_TILES - 5) // 2) as j:
                for u in range(2):
                    tile(j * 2 + 3 + u, (1 + u) % 2)
                    weigh(j * 2 + 2 + u, u % 2, (j * 2 + 1 + u) * 16)
            tile(N_TILES - 2, 1)
            weigh(N_TILES - 3, 0, (N_TILES - 4) * 16)
            tile(N_TILES - 1, 0, False)
            weigh(N_TILES - 2, 1, (N_TILES - 3) * 16)
            weigh(N_TILES - 1, 0, (N_TILES - 2) * 16)

            def last_scale(k):
                root_ready_at(k)
                at = slice(4 * k, 4 * k + 4)
                link(nc.vector.tensor_tensor(fnb[:, at], fmv[:, at, 0], frs[:, at], ALU.mult))
                nc.vector.tensor_scalar(fnb[:, at], fnb[:, at], -1.0, None, ALU.mult).then_inc(v_nb, 1)
                for t in range(4 * k, 4 * k + 2):
                    last = nc.vector.tensor_scalar(fin[:, t, :], fin[:, t, :], fmv[:, t, 0:1], frs[:, t:t + 1],
                                                   ALU.subtract, ALU.mult)
                last.then_inc(v_f, 1)

            root0 = roots["n"]

            def root_ready_at(k):
                dve.wait_ge(p_rs, root0 + k + 1)

            for k in range(4):
                dve.wait_ge(f_ld[k], 16)
                at = slice(4 * k, 4 * k + 4)
                for t in range(4 * k, 4 * k + 4):
                    last = nc.vector.bn_stats(fst[:, t, :], fin[:, t, :])
                link(last)
                for t in range(4 * k, 4 * k + 4):
                    last = nc.vector.bn_aggr(fmv[:, t, :], fst[:, t, :])
                link(last)
                inverse_root(nc.vector.tensor_scalar(frs[:, at], fmv[:, at, 1], LN_EPS, None, ALU.add))
                if k:
                    last_scale(k - 1)
            last_scale(3)

        @block.tensor
        def _(pe):
            mm = nc.tensor.matmul
            pe.wait_ge(c_ld, 16 * N_LOADS)
            pe.wait_ge(c_bf, 1)
            pe.wait_ge(pw_lo, 3)

            def three(o, lhs, rhs, first=True, final=True):
                mm(o, lhs[0], rhs[0], start=first, stop=False, skip_group_check=True)
                mm(o, lhs[0], rhs[1], start=False, stop=False, skip_group_check=True)
                return mm(o, lhs[1], rhs[0], start=False, stop=final, skip_group_check=True)

            def w_part(at, n, rows=P):
                return wph[0:rows, at:at + n], wpl[0:rows, at:at + n]

            def transpose_max(a, b):
                pe.wait_ge(v_nm[a], b + 1)
                out_b = ps_max[a][:, 0:T // 2].bitcast(BF16)
                for t in range(TT):
                    last = nc.tensor.transpose(out_b[:, t * P:(t + 1) * P], negm[a][:, t, :], ident_b[:, :])
                last.then_inc(pe_mT[a], 1)

            def weighted_values(g, values, causal):
                for k in range(TT):
                    for j in range(4):
                        h = 4 * g + j
                        o = ps_o[g % 2][32 * j:32 * j + 32, :]
                        if k == 0 or not causal:
                            last = mm(o[:, 0:T], values[:, k, h, :], probs[:, j, k * T:(k + 1) * T],
                                      start=(k == 0), stop=(k == 1), skip_group_check=True)
                        else:
                            last = mm(o[:, P:T], values[:, k, h, :], probs[:, j, T:T + P],
                                      start=False, stop=True, skip_group_check=True)
                last.then_inc(pe_pv, 1)

            def by_token(a):
                for t in range(TT):
                    for g in range(4):
                        last = nc.tensor.transpose(ps_m[t][:, g * P:(g + 1) * P], oP[:, g, t * P:(t + 1) * P], ident)
                last.then_inc(pe_n1[a], 1)

            def back(a):
                for c in range(DC):
                    for t in range(TT):
                        last = nc.tensor.transpose(ps_m[0][:, c * T + t * P:c * T + (t + 1) * P],
                                                   o_tok[:, t, c * P:(c + 1) * P], ident)
                last.then_inc(pe_n2[a], 1)

            def project_heads(a, w):
                for t in range(TT):
                    for c in range(DC):
                        last = mm(ps_m[1][:, t * D:(t + 1) * D], oT[:, c, t * P:(t + 1) * P], w[:, c, :],
                                  start=(c == 0), stop=(c == DC - 1))
                last.then_inc(pe_w[a], 1)

            def pair_read(b, k):
                pe.wait_ge(v_sw, b * (H // 2) + k + 1)

            def step(i, i0):
                inside = i0 is None
                for u, k in units(i0):
                    b = i - BEHIND[u]

                    def seen(names):
                        return before(names, i, (u, k))

                    if u == "x_transpose":
                        if inside or seen("x2_transpose"):
                            pe.wait_ge(a_x2T, seen("x2_transpose"))
                        pe.wait_ge(x_ld, b * 16 + 16)
                        for c in range(DC):
                            for t in range(TT):
                                last = nc.tensor.transpose(ps_m[0][:, c * T + t * P:c * T + (t + 1) * P],
                                                           x_sb[:, t, c * P:(c + 1) * P], ident)
                        last.then_inc(pe_xT, 1)
                    elif u == "latents":
                        if inside or seen("logits"):
                            pe.wait_ge(v_lg, seen("logits") + 1)
                        elif seen("self_out"):
                            pe.wait_ge(v_r[0], seen("self_out") + 1)
                        pe.wait_ge(v_xT, b + 1)
                        for t in range(TT):
                            at = slice(t * P, (t + 1) * P)
                            for c in range(DC):
                                three(ps_m[0][:, t * KVR:(t + 1) * KVR], (xTh[:, c, at], xTl[:, c, at]),
                                      w_part(W_KV + c * KVR, KVR), c == 0, c == DC - 1)
                        for c in range(DC):
                            last = three(ps_m[1][:, 0:T], w_part(W_Q + c * QR, QR), (xTh[:, c, :], xTl[:, c, :]),
                                         c == 0, c == DC - 1)
                        last.then_inc(pe_qkv, 1)
                    elif u == "kv_transpose":
                        pe.wait_ge(c_ld, 16 * N_LOADS)
                        pe.wait_ge(v_kvn, b + 1)
                        for t in range(TT):
                            last = nc.tensor.transpose(ps_m[0][0:KVR, t * P:(t + 1) * P], kvn[:, t, :], ident)
                        last.then_inc(pe_kvT, 1)
                    elif u == "values":
                        pe.wait_ge(v_qc, b + 1)
                        pe.wait_ge(v_kvT, b + 1)
                        for t in range(TT):
                            at = slice(t * P, (t + 1) * P)
                            last = three(ps_m[1][:, t * D:(t + 1) * D], (kvh[:, at], kvl[:, at]), w_part(W_V, D, KVR))
                        last.then_inc(pe_v, 1)
                    elif u == "qk":
                        s = ps_qk[k]
                        if k == 0:
                            pe.wait_ge(v_qc, b + 1)
                            pe.wait_ge(v_kvT, b + 1)
                        if k < 2:
                            if inside or seen(MAX):
                                pe.wait_ge(s_used, before(MAX, i, ("qk", 0)) - 1 + k)
                        elif k < 4:
                            if inside or seen(EXP):
                                pe.wait_ge(a_p, before(EXP, i, ("qk", 2)) - 3 + k)
                        else:
                            pair_read(b, k - 4)
                        three(s[:, 0:T], w_part(W_QH + k * P, P), (qch[:, :], qcl[:, :]))
                        for c in range(DC):
                            three(s[:, T:2 * T], w_part(W_KR + c * H * QK + k * P, P), (xTh[:, c, :], xTl[:, c, :]), c == 0, False)
                        three(s[:, T:2 * T], w_part(W_KC + k * P, P, KVR), (kvh[:, :], kvl[:, :]), False, True).then_inc(s_full, 1)
                    elif u == "self_max":
                        hp, r = k // 2, QK * (k % 2)
                        q, key = qk_b[r:r + QK, hp, 0, :], qk_b[r:r + QK, hp, 1, :]
                        s = ps_s[k % 2]
                        pe.wait_ge(a_qkb, b * (H // 2) + hp + 1)
                        if k == 0:
                            pair_read(b, 4)
                            pair_read(b, 5)
                        if k >= 2:
                            pe.wait_ge(s_used, seen(MAX) - 1)
                        mm(s[:, 0:P], q[:, 0:P], key[:, 0:P], start=True, stop=False)
                        mm(s[:, 0:P], ident_b[:, :], mask_b[:, :], start=False, stop=True)
                        mm(s[:, P:3 * P], q[:, P:T], key[:, 0:T], start=True, stop=False, skip_group_check=True)
                        mm(s[:, 2 * P:3 * P], ident_b[:, :], mask_b[:, :], start=False, stop=True,
                           skip_group_check=True).then_inc(s_full, 1)
                    elif u in ("self_maxT", "cross_maxT"):
                        if u == "cross_maxT" and (inside or seen("kv_transpose")):
                            pe.wait_ge(v_kvT, seen("kv_transpose"))
                        if u == "cross_maxT" and (inside or seen("x2_transpose")):
                            pe.wait_ge(a_x2T, seen("x2_transpose"))
                        transpose_max(0 if u == "self_maxT" else 1, b)
                    elif u == "self_exp":
                        hp, r = k // 2, QK * (k % 2)
                        q, key = qk[r:r + QK, hp, 0, :], qk[r:r + QK, hp, 1, :]
                        pick = ident_b[:, r + hp:r + hp + 1].broadcast_to([P, P])
                        s = ps_t[k % 2]
                        if k == 0:
                            pe.wait_ge(v_mT[0], b + 1)
                        if inside or seen(EXP) >= 2:
                            pe.wait_ge(a_p, seen(EXP) - 1)
                        mm(s[:, 0:T], key[:, 0:P], q[:, :], start=True, stop=False, skip_group_check=True)
                        mm(s[:, 0:T], pick, mT[0][:, :], start=False, stop=False, skip_group_check=True)
                        mm(s[:, 0:P], ident_b[:, :], maskt_b[:, :], start=False, stop=True, skip_group_check=True)
                        mm(s[:, T:T + P], key[:, P:T], q[:, P:T], start=True, stop=False, skip_group_check=True)
                        mm(s[:, T:T + P], pick, mT[0][:, P:T], start=False, stop=False, skip_group_check=True)
                        mm(s[:, T:T + P], ident_b[:, :], maskt_b[:, :], start=False, stop=True,
                           skip_group_check=True).then_inc(pe_t, 1)
                    elif u == "cross_exp":
                        hp, r = k // 2, QK * (k % 2)
                        q, key = xc[r:r + QK, hp, 0, :], xc[r:r + QK, hp, 1, :]
                        pick = ident_b[:, r + hp:r + hp + 1].broadcast_to([P, P])
                        if k == 0:
                            pe.wait_ge(v_mT[1], b + 1)
                        if k < 2 and (inside or i < B):
                            pair_read(i, 6 + k)
                        pe.wait_ge(a_p, seen(EXP) - 1)
                        for t in range(TT):
                            mm(ps_t[k % 2][:, t * T:(t + 1) * T], key[:, t * P:(t + 1) * P], q[:, :], start=True, stop=False)
                            last = mm(ps_t[k % 2][:, t * T:(t + 1) * T], pick, mT[1][:, :], start=False, stop=True)
                        last.then_inc(pe_t, 1)
                    elif u in ("self_pv", "cross_pv"):
                        cross = u == "cross_pv"
                        if inside or seen(PV) >= 2:
                            pe.wait_ge(a_o, seen(PV) - 1)
                        if k == 0 and cross:
                            pe.wait_ge(a_cv, b + 2)
                        if k == 0 and not cross:
                            pe.wait_ge(a_v, b + 1)
                        pe.wait_ge(a_p, before(EXP, i, ("cross_exp" if cross else "self_exp", 4 * k + 3)) + 1)
                        weighted_values(k, c_sb if cross else v_sb, not cross)
                    elif u == "self_norm":
                        if inside or seen("values"):
                            pe.wait_ge(a_v, seen("values"))
                        if inside or seen("cross_maxT"):
                            pe.wait_ge(v_mT[1], seen("cross_maxT"))
                        pe.wait_ge(a_o, seen(PV))
                        by_token(0)
                    elif u == "cross_norm":
                        if inside or seen("self_out"):
                            pe.wait_ge(v_r[0], seen("self_out") + 1)
                        pe.wait_ge(a_o, seen(PV))
                        by_token(1)
                    elif u in ("self_back", "cross_back"):
                        a = 0 if u == "self_back" else 1
                        pe.wait_ge(v_n1[a], b + 1)
                        back(a)
                    elif u in ("self_out", "cross_out"):
                        a = 0 if u == "self_out" else 1
                        pe.wait_ge(a_n2[a], b + 1)
                        project_heads(a, (wo_sb, wx_sb)[a])
                    elif u == "stack_transpose":
                        if k == 0:
                            pe.wait_ge(a_x1h, b + 1)
                            pe.wait_ge(p_x1l, b + 1)
                            pe.wait_ge(a_ch, b + 1)
                            pe.wait_ge(p_cl, b + 2)
                            pe.wait_ge(s_used, seen(MAX))
                        if k == 1:
                            pe.wait_ge(v_mT[0], i if inside or i < B else B)
                        if k >= 2:
                            pe.wait_ge(a_xc, b * 4 + k - 1)
                        for n, hp in enumerate((2 * k, 2 * k + 1)):
                            for a, src in enumerate((x1s, cs)):
                                for t in range(TT):
                                    at = n * 2 * T + a * T + t * P
                                    last = nc.tensor.transpose(
                                        ps_sh[k % 2][:, at:at + P],
                                        src[:, t, 2 * hp:2 * hp + 2, :].rearrange("p h d -> p (h d)"), ident_h[:, :])
                        last.then_inc(pe_xc, 1)
                    elif u == "cross_max":
                        hp, r = k // 2, QK * (k % 2)
                        q, key = xc[r:r + QK, hp, 0, :], xc[r:r + QK, hp, 1, :]
                        if k == 0:
                            pe.wait_ge(a_xc, b * 4 + 4)
                        if k >= 2:
                            pe.wait_ge(s_used, seen(MAX) - 1)
                        for t in range(TT):
                            last = mm(ps_s[k % 2][:, t * T:(t + 1) * T], q[:, t * P:(t + 1) * P], key[:, :], start=True, stop=True)
                        last.then_inc(s_full, 1)
                    elif u == "x2_transpose":
                        pe.wait_ge(v_x2, b + 1)
                        for c in range(DC):
                            for t in range(TT):
                                last = nc.tensor.transpose(ps_m[0][:, c * T + t * P:c * T + (t + 1) * P],
                                                           x2[:, t, c * P:(c + 1) * P], ident)
                        last.then_inc(pe_x2T, 1)
                    elif u == "logits":
                        pe.wait_ge(a_x2T, b + 1)
                        for t in range(TT):
                            for c in range(DC):
                                last = mm(ps_m[1][:, t * E:(t + 1) * E], x2T[:, c, t * P:(t + 1) * P], wg_sb[:, c, :],
                                          start=(c == 0), stop=(c == DC - 1))
                        last.then_inc(pe_lg, 1)

            each_step(pe, step)

            pe.wait_ge(v_m, 1)
            m_flat = m_b[:, :, :].rearrange("p t e -> p (t e)")
            mm(bank[0][:, 0:NT * E], up_b[:, :], m_flat, start=True, stop=False, skip_group_check=True)
            for t in range(NT - 1):
                mm(bank[0][:, (t + 1) * E:NT * E].rearrange("p (t e) -> p t e", e=E), ones_b[:, :],
                   m_b[:, t:t + 1, :].broadcast_to([P, NT - 1 - t, E]), start=False, stop=(t == NT - 2), skip_group_check=True)
            for t in range(NT):
                last = mm(bank[1][:, 0:E], ones_b[:, :], m_b[:, t, :], start=(t == 0), stop=(t == NT - 1))
            last.then_inc(pe_rank, 1)
            for s in range(2 * NT // OH):
                pe.wait_ge(v_oh, s + 1)
                for t in range(OH):
                    last = mm(bank[2][:, 0:2 * N_TILES], oh_lane[s % 2][:, t, :], oh_tile[s % 2][:, t, :, :].rearrange("p a i -> p (a i)"),
                              start=(s == 0 and t == 0), stop=(s == 2 * NT // OH - 1 and t == OH - 1))
                last.then_inc(pe_slot, 1)

            pe.wait_ge(v_rows, 1)

            def slots_in(n, u, loaded):
                pe.wait_ge(g_ld[u], loaded)
                for c in range(DC):
                    last = nc.tensor.transpose(bank[u][:, c * P:(c + 1) * P], xg[u][:, c * P:(c + 1) * P], ident)
                last.then_inc(pe_ft, 1)

            w_bytes = w_sb[:, :].bitcast(mybir.dt.uint8)

            def weights(e, at, n):
                return w_bytes[:, bass.ds(e + 2 * at, 2 * n)].bitcast(F16)

            def up(u, f, e):
                o = bank[2 + 2 * u + f // 4][:, (f % 4) * P:(f % 4 + 1) * P]
                for c in range(DC):
                    hi = weights(e, c * F + f * P, P)
                    lo = weights(e, DC * F + c * F + f * P, P)
                    mm(o, hi, xh[u][:, c, :], start=(c == 0), stop=False)
                    mm(o, hi, xl[u][:, c, :], start=False, stop=False)
                    last = mm(o, lo, xh[u][:, c, :], start=False, stop=(c == DC - 1))
                if f % 4 == 3:
                    last.then_inc(pe_h, 1)

            def down(u, f, e):
                at = W2_AT + f * 2 * D
                o = bank[6 + u]
                mm(o[:, 0:2 * D], ah[:, u, f, :], weights(e, at, 2 * D), start=(f == 0), stop=(f == FC - 1),
                   skip_group_check=True)
                last = mm(o[:, 0:D], al[:, u, f, :], weights(e, at, D), start=False, stop=(f == FC - 1),
                          skip_group_check=True)
                if f == FC - 1:
                    last.then_inc(pe_y, 1)

            LAG = 4
            expert = [pe.alloc_register(f"expert_{name}") for name in ("before", "now", "next")]

            def load_expert(k, n):
                pe.reg_load(expert[k], tile_e[0:1, bass.ds(n, 1)])

            def shift_experts():
                pe.reg_mov(expert[0], expert[1])
                pe.reg_mov(expert[1], expert[2])

            def weights_at(k):
                return nc.tensor.snap(nc.tensor.snap(expert[k], min_val=0, max_val=E - 1) * (2 * EW2))

            def tile(n, u, act_read, loaded, out_read, first=False):
                before, now = None if first else weights_at(0), weights_at(1)
                pe.wait_ge(v_xl, n + 1)
                if act_read is not None:
                    pe.wait_ge(a_g, act_read)
                for f in range(FC + LAG):
                    if f < FC:
                        up(u, f, now)
                    if f == FC // 2 and loaded is not None:
                        slots_in(n + 1, 1 - u, loaded)
                    if f == LAG and not first:
                        pe.wait_ge(v_al, n * 2 - 1)
                        if out_read is not None:
                            pe.wait_ge(v_y, out_read)
                    if f == LAG + FC // 2 and not first:
                        pe.wait_ge(v_al, n * 2)
                    if f >= LAG and not first:
                        down(1 - u, f - LAG, before)
                    if f == FC + 1 and loaded is not None:
                        load_expert(2, n + 1)
                shift_experts()

            pe.wait_ge(w_lo, E * PIECES + 1)
            load_expert(1, 0)
            slots_in(0, 0, 16)
            tile(0, 0, None, 16, None, first=True)
            tile(1, 1, None, 32, None)
            tile(2, 0, 2, 32, None)
            with pe.Fori(0, (N_TILES - 5) // 2) as j:
                for u in range(2):
                    tile(j * 2 + 3 + u, (1 + u) % 2, j * 4 + 2 * u + 4, j * 16 + 48, j * 2 + u + 1)
            N = N_TILES
            tile(N - 2, 1, 2 * (N - 3), 16 * ((N + 1) // 2), N - 4)
            tile(N - 1, 0, 2 * (N - 2), None, N - 3)
            last_at = weights_at(0)
            pe.wait_ge(v_y, N - 2)
            pe.wait_ge(v_al, 2 * N)
            for f in range(FC):
                down(0, f, last_at)


def _table():
    import numpy as np
    t = np.zeros((P, C_ALL), np.float32)
    lane = np.arange(P)
    inv = 1.0 / 10000.0 ** (np.arange(0, RD, 2, dtype=np.float32) / RD)
    freqs = np.outer(np.arange(T, dtype=np.float32), inv).astype(np.float32)
    r = lane % QK - (QK - RD)
    rot = r >= 0
    i = np.where(rot, r, 0) % (RD // 2)
    sign = np.where(r < RD // 2, -1.0, 1.0)
    t[:, C_COS:C_COS + T] = np.where(rot[:, None], np.cos(freqs).T[i], 1.0) / W_SCALE
    t[:, C_SIN:C_SIN + T] = np.where(rot[:, None], np.sin(freqs).T[i] * sign[:, None], 0.0) / W_SCALE
    t[:, C_ID:C_ID + P] = np.eye(P)
    t[:, C_MASK:C_MASK + P] = np.where(lane[None, :] > lane[:, None], -1e30, 0.0)
    t[:, C_MASKT:C_MASKT + P] = np.where(lane[:, None] > lane[None, :], -1e30, 0.0)
    t[:, C_UP:C_UP + P] = lane[:, None] < lane[None, :]
    t[:, C_REV:C_REV + E] = E - np.arange(E)
    t[:, C_CNT:C_CNT + NT] = P * np.arange(NT)
    t[:, C_LT:C_LT + E * E] = (np.arange(E)[None, :] < np.arange(E)[:, None]).reshape(-1)
    t[:, C_TILE:C_TILE + N_TILES] = np.arange(N_TILES)
    t[:, C_LANE:C_LANE + P] = lane
    t[:, C_TOK1:C_TOK1 + NT] = P * np.arange(NT)[None, :] + lane[:, None] + 1
    t[:, C_DUMMY] = TOK + 1 + lane
    return t


def kernel(**inputs):
    import numpy as np
    import concourse.bacc as bacc
    from concourse.bass_utils import run_bass_kernel_spmd as run

    a = {k: np.asarray(v) for k, v in inputs.items()}

    def heads(w, at, width):
        o = np.zeros((w.shape[0], H, QK), np.float32)
        o[:, :, at:at + width] = w.reshape(w.shape[0], H, width)
        return o.reshape(w.shape[0], H * QK)

    wq = heads(a["L0_attn_W_qdec"], 0, HD)
    wq.reshape(QR, H, QK)[:, :, QK - RD:] = a["L0_attn_W_qrope"].reshape(QR, H, RD)
    w2 = a["L0_ffn_W2"].reshape(E, 2, FC // 2, P, D).transpose(0, 1, 3, 2, 4).reshape(E, 2, P, PIECE)
    w_exp = np.concatenate([a["L0_ffn_W1"].reshape(E, DC, P, F), w2], 1).reshape(E * PIECES, P, PIECE)
    arrays = {
        "x": a["x"], "ctx": a["ctx_1024"], "w_kv": a["L0_attn_W_kv"], "g_kv": a["L0_attn_g_kv"], "w_q": a["L0_attn_W_q"],
        "wq_heads": wq, "wk_content": heads(a["L0_attn_W_kdec"], 0, HD), "wk_rope": heads(a["L0_attn_W_krope"], QK - RD, RD),
        "wv": a["L0_attn_W_vdec"], "wo": a["L0_attn_W_o"], "wx": a["L0_xattn_W"].T,
        "xb": a["L0_xattn_b"], "wg": a["L0_ffn_Wg"], "bg": a["L0_ffn_bg"], "w_exp": w_exp,
        "b1t": a["L0_ffn_b1"].reshape(E, FC, P).transpose(2, 0, 1).reshape(P, E * FC),
        "b2": a["L0_ffn_b2"], "table": _table()}
    arrays = {"in_" + k: np.ascontiguousarray(v) for k, v in arrays.items()}
    nc = bacc.Bacc("TRN2", target_bir_lowering=False, num_devices=1)
    aps = [nc.dram_tensor(k, v.shape, F32, kind="ExternalInput").ap() for k, v in arrays.items()]
    out = nc.dram_tensor("out", (B, T, D), F32, kind="ExternalOutput").ap()
    x2_rows = nc.dram_tensor("x2_rows", (ROWS, D), F32, kind="Internal").ap()
    acc_rows = nc.dram_tensor("acc_rows", (ROWS, D), F32, kind="Internal").ap()
    decoder_layer(nc, *aps, out, x2_rows, acc_rows)
    return run(nc, [arrays], core_ids=[0]).results[0]["out"]
```
